# Optimizing a Trainium2 kernel written in Bass

```python
import numpy as np
import jax
import jax.numpy as jnp

def _softmax(x, axis=-1):
    return jax.nn.softmax(x, axis=axis)

def _gelu(x):
    return jax.nn.gelu(x, approximate=True)

def _silu(x):
    return jax.nn.silu(x)

def _sigmoid(x):
    return jax.nn.sigmoid(x)

def _layernorm(x, axis=-1, eps=1e-05):
    m = jnp.mean(x, axis=axis, keepdims=True)
    v = jnp.var(x, axis=axis, keepdims=True)
    return (x - m) / jnp.sqrt(v + eps)

def _scatter_add(tgt, idx, src, axis=0):
    return tgt.at[idx].add(src)

def _segment_sum(src, seg, n):
    return jax.ops.segment_sum(src, seg, n)
kernel_name = 'mk_flamingo_gated_d2_seqx_r8_59462b'

def setup_inputs(seed: int=0):
    np.random.seed(seed)
    _w = jnp.asarray

    def _rec_inputs():
        import jax
        import jax.numpy as jnp
        _rk = jax.random.key(seed)
        x = -0.0002928 + 1 * jax.random.normal(jax.random.fold_in(_rk, 1), (64, 64, 256), jnp.float32)
        _lenS = 64 - jax.random.randint(jax.random.fold_in(_rk, 7), (64,), 0, max(1, 64 // 4) + 1, jnp.int32)
        _lenS2 = 64 - jax.random.randint(jax.random.fold_in(_rk, 8), (64,), 0, max(1, 64 // 4) + 1, jnp.int32)
        _ctx_2048P = jax.random.normal(jax.random.fold_in(_rk, 11), (64, 16, 256), jnp.float32)
        _ctx_2048c = jax.random.dirichlet(jax.random.fold_in(_rk, 511), 0.3 * jnp.ones((16,), jnp.float32), (64, 64))
        _ctx_2048t = jnp.einsum('bsk,bkd->bsd', _ctx_2048c, _ctx_2048P)
        _ctx_2048t = _ctx_2048t * jax.lax.rsqrt(jnp.mean(jnp.square(_ctx_2048t)) + 1e-12) * 0.953939
        ctx_2048 = -1.39393e-06 + 0.999914 * (_ctx_2048t + 0.3 * jax.random.normal(jax.random.fold_in(_rk, 611), (64, 64, 256), jnp.float32))
        _validS = jnp.arange(64)[None, :] < _lenS[:, None]
        _validS2 = jnp.arange(64)[None, :] < _lenS2[:, None]
        _causal = jnp.tril(jnp.ones((64, 64), dtype=bool))
        mask_BxS2_ff1 = jnp.where(jnp.ones((64, 64), dtype=bool), 1.0, 0.0).astype(jnp.float32)
        _g = jax.random.normal(jax.random.fold_in(_rk, 9001), (2, 2), jnp.float32)
        _g = jnp.sign(_g) * jnp.maximum(jnp.abs(_g), 1.0) + (_g == 0) * 1.0
        g_xattn = _g[0]
        g_ffn = _g[1]
        return (x, ctx_2048, mask_BxS2_ff1, g_xattn, g_ffn)
    x, ctx_2048, mask_BxS2_ff1, g_xattn, g_ffn = _rec_inputs()

    def _L0_xattn_setup():
        import math
        import jax, jax.numpy as jnp
        import numpy as np
        N_HEADS = 8
        CHANNELS = 64
        K_CH = CHANNELS // N_HEADS
        THETA = 10000.0

        def _rope_freqs(length, dim):
            inv_freq = 1.0 / THETA ** (jnp.arange(0, dim, 2, dtype=jnp.float32) / dim)
            f = jnp.arange(length, dtype=jnp.float32)[:, None] * inv_freq[None, :]
            return jnp.concatenate([f, f], axis=-1)

        def _apply_rotary(pos, t):
            half = t.shape[-1] // 2
            rot = jnp.concatenate([-t[..., half:], t[..., :half]], axis=-1)
            return t * jnp.cos(pos) + rot * jnp.sin(pos)

        def _proj(inp, W, b):
            return jnp.einsum('oc,bct->bot', W, inp) + b[None, :, None]
        key = jax.random.key(seed)
        ks = jax.random.split(key, 10)
        B, C, T = (4, CHANNELS, 256)
        bound = math.sqrt(6.0 / (C + C))

        def w(k):
            return jax.random.uniform(k, (C, C), jnp.float32, -bound, bound)
        return {'x': jax.random.normal(ks[0], (B, C, T), jnp.float32), 'c': jax.random.normal(ks[1], (B, C, T), jnp.float32), 'Wq': w(ks[2]), 'bq': jnp.zeros((C,), jnp.float32), 'Wk': w(ks[3]), 'bk': jnp.zeros((C,), jnp.float32), 'Wv': w(ks[4]), 'bv': jnp.zeros((C,), jnp.float32), 'Wo': w(ks[5]), 'bo': jnp.zeros((C,), jnp.float32)}
    _L0_xattn_all = _L0_xattn_setup()
    _L0_xattn_in = {k: v for k, v in _L0_xattn_all.items() if k in ('Wq', 'bq', 'Wk', 'bk', 'Wv', 'bv', 'Wo', 'bo')}
    del _L0_xattn_all

    def _L0_ffn_setup():
        import jax, jax.numpy as jnp
        import numpy as np
        NUM_EXPERTS = 8
        EXPERTS_PER_TOK = 2
        key = jax.random.key(seed)
        k1, k2, k3, k4, k5 = jax.random.split(key, 5)
        B, T, D, F, E = (4, 128, 256, 128, NUM_EXPERTS)
        return {'x': jax.random.normal(k1, (B, T, D), dtype=jnp.float32), 'router_w': jax.random.normal(k2, (D, E), dtype=jnp.float32) * 0.02, 'gate_proj': jax.random.normal(k3, (E, D, F), dtype=jnp.float32) * 0.02, 'up_proj': jax.random.normal(k4, (E, D, F), dtype=jnp.float32) * 0.02, 'down_proj': jax.random.normal(k5, (E, F, D), dtype=jnp.float32) * 0.02}
    _L0_ffn_all = _L0_ffn_setup()
    _L0_ffn_in = {k: v for k, v in _L0_ffn_all.items() if k in ('router_w', 'gate_proj', 'up_proj', 'down_proj')}
    del _L0_ffn_all

    def _L1_xattn_setup():
        import jax, jax.numpy as jnp
        import numpy as np
        H = 256
        NH = 16
        HD = H // NH
        FD = 64
        key = jax.random.key(seed)
        ks = jax.random.split(key, 12)
        B, S = (4, 512)
        s = 1.0 / np.sqrt(H)
        sf = 1.0 / np.sqrt(HD)
        return {'query': jax.random.normal(ks[0], (B, S, H), jnp.float32), 'key': jax.random.normal(ks[1], (B, S, H), jnp.float32), 'value': jax.random.normal(ks[2], (B, S, H), jnp.float32), 'attention_mask': jnp.ones((B, S), jnp.float32), 'Wq': jax.random.normal(ks[3], (H, H), jnp.float32) * s, 'bq': jnp.zeros((H,), jnp.float32), 'Wk': jax.random.normal(ks[4], (H, H), jnp.float32) * s, 'bk': jnp.zeros((H,), jnp.float32), 'Wv': jax.random.normal(ks[5], (H, H), jnp.float32) * s, 'bv': jnp.zeros((H,), jnp.float32), 'Wqf': jax.random.normal(ks[6], (FD, HD), jnp.float32) * sf, 'Wkf': jax.random.normal(ks[7], (FD, HD), jnp.float32) * sf, 'Wo': jax.random.normal(ks[8], (H, H), jnp.float32) * s, 'bo': jnp.zeros((H,), jnp.float32)}
    _L1_xattn_all = _L1_xattn_setup()
    _L1_xattn_in = {k: v for k, v in _L1_xattn_all.items() if k in ('Wq', 'bq', 'Wk', 'bk', 'Wv', 'bv', 'Wqf', 'Wkf', 'Wo', 'bo')}
    del _L1_xattn_all

    def _L1_ffn_setup():
        import jax, jax.numpy as jnp
        import numpy as np
        EPS = 1e-05
        ROPE_BASE = 150000.0
        NHEADS = 32
        KVHEADS = 8
        HEAD_DIM = 64
        TOP_K = 4

        def _rms(x, w):
            return x * jax.lax.rsqrt(jnp.mean(x * x, -1, keepdims=True) + EPS) * w

        def _rope(q, k):
            S, hd = (q.shape[1], q.shape[-1])
            half = hd // 2
            inv = 1.0 / ROPE_BASE ** (jnp.arange(half, dtype=jnp.float32) / half)
            ang = jnp.arange(S, dtype=jnp.float32)[:, None] * inv
            cos = jnp.concatenate([jnp.cos(ang), jnp.cos(ang)], -1)[None, :, None, :]
            sin = jnp.concatenate([jnp.sin(ang), jnp.sin(ang)], -1)[None, :, None, :]

            def rot(t):
                t1, t2 = (t[..., :half], t[..., half:])
                return jnp.concatenate([-t2, t1], -1)
            return (q * cos + rot(q) * sin, k * cos + rot(k) * sin)
        key = jax.random.key(seed)
        ks = jax.random.split(key, 12)
        B, S, D, H, E = (1, 128, 256, 256, 16)
        s = 0.02
        return {'x': jax.random.normal(ks[0], (B, S, D), jnp.float32), 'ln_w': jnp.ones((D,), jnp.float32), 'ff_ln_w': jnp.ones((D,), jnp.float32), 'wq': jax.random.normal(ks[1], (D, NHEADS * HEAD_DIM), jnp.float32) * s, 'wk': jax.random.normal(ks[2], (D, KVHEADS * HEAD_DIM), jnp.float32) * s, 'wv': jax.random.normal(ks[3], (D, KVHEADS * HEAD_DIM), jnp.float32) * s, 'wo': jax.random.normal(ks[4], (NHEADS * HEAD_DIM, D), jnp.float32) * s, 'wg': jax.random.normal(ks[5], (D, E), jnp.float32) * s, 'w1': jax.random.normal(ks[6], (E, D, H), jnp.float32) * s, 'w3': jax.random.normal(ks[7], (E, D, H), jnp.float32) * s, 'w2': jax.random.normal(ks[8], (E, H, D), jnp.float32) * s}
    _L1_ffn_all = _L1_ffn_setup()
    _L1_ffn_in = {k: v for k, v in _L1_ffn_all.items() if k in ('ln_w', 'ff_ln_w', 'wq', 'wk', 'wv', 'wo', 'wg', 'w1', 'w3', 'w2')}
    del _L1_ffn_all
    return {'x': x, 'ctx_2048': ctx_2048, 'mask_BxS2_ff1': mask_BxS2_ff1, 'g_xattn': g_xattn, 'g_ffn': g_ffn, 'L0_xattn_Wq': _L0_xattn_in['Wq'], 'L0_xattn_bq': _L0_xattn_in['bq'], 'L0_xattn_Wk': _L0_xattn_in['Wk'], 'L0_xattn_bk': _L0_xattn_in['bk'], 'L0_xattn_Wv': _L0_xattn_in['Wv'], 'L0_xattn_bv': _L0_xattn_in['bv'], 'L0_xattn_Wo': _L0_xattn_in['Wo'], 'L0_xattn_bo': _L0_xattn_in['bo'], 'L0_ffn_router_w': _L0_ffn_in['router_w'], 'L0_ffn_gate_proj': _L0_ffn_in['gate_proj'], 'L0_ffn_up_proj': _L0_ffn_in['up_proj'], 'L0_ffn_down_proj': _L0_ffn_in['down_proj'], 'L1_xattn_Wq': _L1_xattn_in['Wq'], 'L1_xattn_bq': _L1_xattn_in['bq'], 'L1_xattn_Wk': _L1_xattn_in['Wk'], 'L1_xattn_bk': _L1_xattn_in['bk'], 'L1_xattn_Wv': _L1_xattn_in['Wv'], 'L1_xattn_bv': _L1_xattn_in['bv'], 'L1_xattn_Wqf': _L1_xattn_in['Wqf'], 'L1_xattn_Wkf': _L1_xattn_in['Wkf'], 'L1_xattn_Wo': _L1_xattn_in['Wo'], 'L1_xattn_bo': _L1_xattn_in['bo'], 'L1_ffn_ln_w': _L1_ffn_in['ln_w'], 'L1_ffn_ff_ln_w': _L1_ffn_in['ff_ln_w'], 'L1_ffn_wq': _L1_ffn_in['wq'], 'L1_ffn_wk': _L1_ffn_in['wk'], 'L1_ffn_wv': _L1_ffn_in['wv'], 'L1_ffn_wo': _L1_ffn_in['wo'], 'L1_ffn_wg': _L1_ffn_in['wg'], 'L1_ffn_w1': _L1_ffn_in['w1'], 'L1_ffn_w3': _L1_ffn_in['w3'], 'L1_ffn_w2': _L1_ffn_in['w2']}

def reference(x, ctx_2048, mask_BxS2_ff1, g_xattn, g_ffn, L0_xattn_Wq, L0_xattn_bq, L0_xattn_Wk, L0_xattn_bk, L0_xattn_Wv, L0_xattn_bv, L0_xattn_Wo, L0_xattn_bo, L0_ffn_router_w, L0_ffn_gate_proj, L0_ffn_up_proj, L0_ffn_down_proj, L1_xattn_Wq, L1_xattn_bq, L1_xattn_Wk, L1_xattn_bk, L1_xattn_Wv, L1_xattn_bv, L1_xattn_Wqf, L1_xattn_Wkf, L1_xattn_Wo, L1_xattn_bo, L1_ffn_ln_w, L1_ffn_ff_ln_w, L1_ffn_wq, L1_ffn_wk, L1_ffn_wv, L1_ffn_wo, L1_ffn_wg, L1_ffn_w1, L1_ffn_w3, L1_ffn_w2):
    import jax
    import jax.numpy as jnp

    def _L0_xattn_ref(x, c, Wq, bq, Wk, bk, Wv, bv, Wo, bo):
        import math
        import jax, jax.numpy as jnp
        import numpy as np
        N_HEADS = 8
        CHANNELS = 64
        K_CH = CHANNELS // N_HEADS
        THETA = 10000.0

        def _rope_freqs(length, dim):
            inv_freq = 1.0 / THETA ** (jnp.arange(0, dim, 2, dtype=jnp.float32) / dim)
            f = jnp.arange(length, dtype=jnp.float32)[:, None] * inv_freq[None, :]
            return jnp.concatenate([f, f], axis=-1)

        def _apply_rotary(pos, t):
            half = t.shape[-1] // 2
            rot = jnp.concatenate([-t[..., half:], t[..., :half]], axis=-1)
            return t * jnp.cos(pos) + rot * jnp.sin(pos)

        def _proj(inp, W, b):
            return jnp.einsum('oc,bct->bot', W, inp) + b[None, :, None]
        b, _, t_t = x.shape
        t_s = c.shape[2]
        q_emb = _rope_freqs(t_t, K_CH)
        k_emb = _rope_freqs(t_s, K_CH)

        def split_heads(t):
            return t.reshape(b, N_HEADS, K_CH, t.shape[2]).transpose(0, 1, 3, 2)
        q = split_heads(_proj(x, Wq, bq))
        k = split_heads(_proj(c, Wk, bk))
        v = split_heads(_proj(c, Wv, bv))
        q = _apply_rotary(q_emb, q)
        k = _apply_rotary(k_emb, k)
        scores = jnp.einsum('bhtc,bhsc->bhts', q, k) / math.sqrt(K_CH)
        p_attn = jax.nn.softmax(scores, axis=-1)
        out = jnp.einsum('bhts,bhsc->bhtc', p_attn, v)
        out = out.transpose(0, 1, 3, 2).reshape(b, N_HEADS * K_CH, t_t)
        return _proj(out, Wo, bo)

    def _L0_ffn_ref(x, router_w, gate_proj, up_proj, down_proj):
        import jax, jax.numpy as jnp
        import numpy as np
        NUM_EXPERTS = 8
        EXPERTS_PER_TOK = 2
        E, K = (NUM_EXPERTS, EXPERTS_PER_TOK)
        scores = jnp.einsum('btd,de->bte', x, router_w).astype(jnp.float32)
        routing_weights, routing_idx = jax.lax.top_k(jax.nn.softmax(scores, axis=-1), K)
        routing_weights = (routing_weights / jnp.sum(routing_weights, axis=-1, keepdims=True)).astype(x.dtype)
        onehot = jax.nn.one_hot(routing_idx, E, dtype=x.dtype)
        dispatch_mask = jnp.sum(onehot, axis=2)
        combine_weights = jnp.einsum('btke,btk->bte', onehot, routing_weights)
        dispatched = x[:, :, None, :] * dispatch_mask[..., None]
        gate = jnp.einsum('bted,edf->btef', dispatched, gate_proj)
        up = jnp.einsum('bted,edf->btef', dispatched, up_proj)
        act = jax.nn.silu(gate) * up
        expert_out = jnp.einsum('btef,efd->bted', act, down_proj)
        return jnp.einsum('bted,bte->btd', expert_out, combine_weights)

    def _L1_xattn_ref(query, key, value, attention_mask, Wq, bq, Wk, bk, Wv, bv, Wqf, Wkf, Wo, bo):
        import jax, jax.numpy as jnp
        import numpy as np
        H = 256
        NH = 16
        HD = H // NH
        FD = 64
        B, Sq, _ = query.shape
        Sk = key.shape[1]

        def heads(x, W, b, S):
            return (x @ W.T + b).reshape(B, S, NH, HD).transpose(0, 2, 1, 3)
        q = heads(query, Wq, bq, Sq)
        k = heads(key, Wk, bk, Sk)
        v = heads(value, Wv, bv, Sk)
        q_prime = jax.nn.relu(jnp.einsum('bhnd,fd->bhnf', q, Wqf))
        k_prime = jax.nn.relu(jnp.einsum('bhnd,fd->bhnf', k, Wkf))
        k_prime = k_prime * attention_mask[:, None, :, None]
        kv = jnp.einsum('bhnf,bhne->bhfe', k_prime, v)
        qkv = jnp.einsum('bhmf,bhfe->bhme', q_prime, kv)
        k_sum = jnp.sum(k_prime, axis=2)
        qk_sum = jnp.einsum('bhmf,bhf->bhm', q_prime, k_sum)[..., None]
        out = qkv / (qk_sum + 1e-08)
        out = out.transpose(0, 2, 1, 3).reshape(B, Sq, H)
        return out @ Wo.T + bo

    def _L1_ffn_ref(x, ln_w, ff_ln_w, wq, wk, wv, wo, wg, w1, w3, w2):
        import jax, jax.numpy as jnp
        import numpy as np
        EPS = 1e-05
        ROPE_BASE = 150000.0
        NHEADS = 32
        KVHEADS = 8
        HEAD_DIM = 64
        TOP_K = 4

        def _rms(x, w):
            return x * jax.lax.rsqrt(jnp.mean(x * x, -1, keepdims=True) + EPS) * w

        def _rope(q, k):
            S, hd = (q.shape[1], q.shape[-1])
            half = hd // 2
            inv = 1.0 / ROPE_BASE ** (jnp.arange(half, dtype=jnp.float32) / half)
            ang = jnp.arange(S, dtype=jnp.float32)[:, None] * inv
            cos = jnp.concatenate([jnp.cos(ang), jnp.cos(ang)], -1)[None, :, None, :]
            sin = jnp.concatenate([jnp.sin(ang), jnp.sin(ang)], -1)[None, :, None, :]

            def rot(t):
                t1, t2 = (t[..., :half], t[..., half:])
                return jnp.concatenate([-t2, t1], -1)
            return (q * cos + rot(q) * sin, k * cos + rot(k) * sin)
        B, S, D = x.shape
        h = _rms(x, ln_w)
        q = (h @ wq).reshape(B, S, NHEADS, HEAD_DIM)
        k = (h @ wk).reshape(B, S, KVHEADS, HEAD_DIM)
        v = (h @ wv).reshape(B, S, KVHEADS, HEAD_DIM)
        q, k = _rope(q, k)
        g = NHEADS // KVHEADS
        k = jnp.repeat(k, g, axis=2)
        v = jnp.repeat(v, g, axis=2)
        scores = jnp.einsum('bqhd,bkhd->bhqk', q, k) / np.float32(np.sqrt(HEAD_DIM))
        causal = jnp.tril(jnp.ones((S, S), bool))
        scores = jnp.where(causal[None, None], scores, jnp.float32(-1e+30))
        attn = jax.nn.softmax(scores, -1)
        o = jnp.einsum('bhqk,bkhd->bqhd', attn, v).reshape(B, S, NHEADS * HEAD_DIM)
        x = x + o @ wo
        h = _rms(x, ff_ln_w)
        logits = h @ wg
        topv, topi = jax.lax.top_k(logits, TOP_K)
        gate = jax.nn.softmax(topv, -1)
        bidx = jnp.arange(B)[:, None, None]
        sidx = jnp.arange(S)[None, :, None]
        weights = jnp.zeros_like(logits).at[bidx, sidx, topi].set(gate)
        a = jax.nn.silu(jnp.einsum('bsd,edh->bseh', h, w1)) * jnp.einsum('bsd,edh->bseh', h, w3)
        y = jnp.einsum('bseh,ehd->bsed', a, w2)
        moe = jnp.einsum('bsed,bse->bsd', y, weights)
        return x + moe
    x = x + jnp.tanh(g_xattn[0]) * _L0_xattn_ref(_layernorm(x, axis=-1), ctx_2048, L0_xattn_Wq, L0_xattn_bq, L0_xattn_Wk, L0_xattn_bk, L0_xattn_Wv, L0_xattn_bv, L0_xattn_Wo, L0_xattn_bo)
    x = x + jnp.tanh(g_ffn[0]) * _L0_ffn_ref(_layernorm(x, axis=-1), L0_ffn_router_w, L0_ffn_gate_proj, L0_ffn_up_proj, L0_ffn_down_proj)
    x = x + jnp.tanh(g_xattn[1]) * _L1_xattn_ref(_layernorm(x, axis=-1), ctx_2048, ctx_2048, mask_BxS2_ff1, L1_xattn_Wq, L1_xattn_bq, L1_xattn_Wk, L1_xattn_bk, L1_xattn_Wv, L1_xattn_bv, L1_xattn_Wqf, L1_xattn_Wkf, L1_xattn_Wo, L1_xattn_bo)
    x = x + jnp.tanh(g_ffn[1]) * _L1_ffn_ref(_layernorm(x, axis=-1), L1_ffn_ln_w, L1_ffn_ff_ln_w, L1_ffn_wq, L1_ffn_wk, L1_ffn_wv, L1_ffn_wo, L1_ffn_wg, L1_ffn_w1, L1_ffn_w3, L1_ffn_w2)
    return x

_drawn_inputs = setup_inputs


def setup_inputs(seed=0):
    import zlib

    import numpy as np

    out = dict(_drawn_inputs(seed))
    spreads = {'g_ffn': (-1.0, 0.6),
     'L0_xattn_bq': (0.0, 0.1),
     'L0_xattn_bk': (0.0, 0.563),
     'L0_xattn_bv': (0.0, 0.47),
     'L0_xattn_bo': (0.0, 0.403),
     'L1_xattn_bq': (0.0, 2.0),
     'L1_xattn_bk': (0.0, 2.0),
     'L1_xattn_bv': (0.0, 0.434),
     'L1_xattn_bo': (0.0, 0.444),
     'L1_ffn_ln_w': (1.0, 0.6),
     'L1_ffn_ff_ln_w': (1.0, 0.6)}
    factors = {'L0_ffn_router_w': 8.0,
     'L0_ffn_gate_proj': 8.0,
     'L0_ffn_up_proj': 8.0,
     'L0_ffn_down_proj': 8.0,
     'L1_ffn_wq': 4.102,
     'L1_ffn_wk': 4.115,
     'L1_ffn_wg': 12.526,
     'L1_ffn_w1': 10.95,
     'L1_xattn_Wq': 8.0,
     'L1_xattn_Wk': 5.356,
     'L1_xattn_Wqf': 7.17,
     'L1_xattn_Wkf': 6.292,
     'L1_ffn_w3': 3.769,
     'L1_ffn_w2': 3.746}
    for name, (base, spread) in spreads.items():
        noise = np.random.default_rng([zlib.crc32(name.encode()), seed]).standard_normal(out[name].shape)
        drawn = base * np.exp(spread * noise) if base else spread * noise
        out[name] = jnp.asarray(drawn.astype(out[name].dtype))
    for name, factor in factors.items():
        out[name] = (out[name] * factor).astype(out[name].dtype)
    return out
```

```python
from contextlib import ExitStack

import numpy as np
import concourse.bass as bass
from concourse import mybir

fp32 = mybir.dt.float32
fp32r = mybir.dt.float32r
ALU = mybir.AluOpType
ACT = mybir.ActivationFunctionType
AX = mybir.AxisListType.X

BATCH, SEQ, DIM = 64, 64, 256
ROWS = BATCH * SEQ
PART = 128
TILES = ROWS // PART
EPS = 1e-5


class Tile:

    def __init__(self, k, c):
        self.k, self.c = k, c
        self.n = 2 * k + c
        self.slot = c % 2
        self.turn = k + c // 2
        self.live = not isinstance(k, int) or 0 <= self.n < TILES

    def plus(self, d):
        return Tile(self.k, self.c + d)


def past(eng, sem, count):
    if not (isinstance(count, int) and count <= 0):
        eng.wait_ge(sem, count)


def hold(eng, sem, count, held):
    if not (isinstance(count, int) and count <= 0):
        eng.wait_ge(sem, count)
        if not isinstance(count, int):
            eng.sem_inc(held, 1)


def stage_softmax_attention(nc, x_in, x_out, ctx, c):
    HEADS, GROUPS, KC, T, HALF = 16, 4, 8, 256, 2
    SPLIT = 3 * KC
    st = ExitStack()
    sb = lambda n, s, d=fp32: st.enter_context(nc.sbuf_tensor("soft_" + n, s, d))
    sem = lambda n: nc.alloc_semaphore("soft_" + n)
    with st:
        w_in = sb("w_in", [PART, 5, PART])
        w_out = sb("w_out", [PART, GROUPS, PART])
        spread = sb("spread", [PART, PART])
        cos_t, sin_t = sb("cos", [PART, 2 * T]), sb("sin", [PART, 2 * T])
        cols = sb("cols", [PART, 8])
        bv = sb("bv", [PART, 2 * PART])
        sel_f = sb("sel_f", [PART, 17, PART])
        sel = sb("sel", [PART, 17, PART], fp32r)
        gate = sb("gate", [PART, 1])
        half_neg = sb("half_neg", [PART, 1])
        xt, ct = sb("xt", [PART, 2, T]), sb("ct", [PART, 2, T])
        xr = sb("xr", [PART, 2, T])
        xn = sb("xn", [PART, 2, T])
        stats, mv = sb("stats", [PART, 6]), sb("mv", [PART, 2])
        var_eps, rstd = sb("var_eps", [PART, 1]), sb("rstd", [PART, 1])
        by_cos, by_sin = sb("by_cos", [PART, 2 * T]), sb("by_sin", [PART, 2 * T])
        roped = sb("roped", [PART, 2 * T])
        hi, lo = sb("hi", [PART, 2, 2 * T], fp32r), sb("lo", [PART, 2, 2 * T], fp32r)
        rep = sb("rep", [PART, 2, GROUPS, 2 * T], fp32r)
        qm = sb("qm", [PART, GROUPS, T], fp32r)
        top = sb("top", [PART, 2, GROUPS, HALF, PART], fp32r)
        vaug = sb("vaug", [PART, 2, HALF, HEADS, 32])
        prob = sb("prob", [PART, 4, 2 * T])
        o_raw = sb("o_raw", [PART, 2, GROUPS, T])
        den = sb("den", [PART, 32])
        rden = sb("rden", [PART, 32])
        rrow = sb("rrow", [PART, GROUPS, T])
        on = sb("on", [PART, GROUPS, T])
        y, xo = sb("y", [PART, T]), sb("xo", [PART, 2, T])
        ps = lambda n: st.enter_context(nc.psum_tensor("soft_" + n, [PART, 2 * T], fp32))
        p_a, p_b, p_o, p_x = ([ps(f"{n}{i}") for i in range(2)] for n in ("pa", "pb", "po", "px"))

        const_in, zeroed = sem("const_in"), sem("zeroed")
        sel_ready, gate_ready = sem("sel_ready"), sem("gate_ready")
        x_in_s, c_in_s, xr_in_s = ([sem(f"{n}{i}") for i in range(2)] for n in ("x", "c", "xr"))
        stats_ready, var_ready, rstd_ready, xn_ready = sem("stats"), sem("var"), sem("rstd"), sem("xn")
        qk_ready, qkrot_ready, v_ready = sem("qk"), sem("qkrot"), sem("v")
        cos_done, sin_done, roped_ready = sem("cosd"), sem("sind"), sem("roped")
        hi_ready, lo_ready, vaug_ready = sem("hi"), sem("lo"), sem("vaug")
        rep_ready, rep_out = sem("rep"), sem("rep_out")
        a_ready, a_done = sem("a"), sem("a_done")
        m_ready, qm_ready = sem("m"), sem("qm")
        b_ready, prob_ready, pv_done, o_out = sem("b"), sem("prob"), sem("pv"), sem("o_out")
        den_in, rden_ready, rrow_in = sem("den_in"), sem("rden"), sem("rrow_in")
        spread_ready, on_ready, wo_ready = sem("spread"), sem("on"), sem("wo")
        y_ready, xo_ready = sem("y"), sem("xo")
        held = sem("held")
        stored = [sem(f"stored{i}") for i in range(2)]

        def program(eng, step):
            for s in range(-3, 3):
                step(Tile(0, s))
            with eng.Fori(0, (TILES - 6) // 2) as k:
                step(Tile(k, 3))
                step(Tile(k, 4))
            for s in range(TILES - 3, TILES + 1):
                step(Tile(0, s))

        with nc.Block() as block:
            @block.sync
            def _(sp):
                for dst, src in ((w_in, c["sa_w_in"]), (w_out, c["sa_w_out"]), (spread, c["spread"]),
                                 (cos_t, c["sa_cos"]), (sin_t, c["sa_sin"]), (cols, c["sa_cols"]),
                                 (bv, c["sa_bv"]), (sel_f, c["sa_sel"])):
                    sp.dma_start(dst[:], src).then_inc(const_in, 16)

                def step(i):
                    new, last = i.plus(3), i.plus(-1)
                    if new.live:
                        hold(sp, xn_ready, new.n - 1, held)
                        sp.dma_start(xt[:, new.slot, :], x_in[new.n]).then_inc(x_in_s[new.slot], 16)
                    if last.live:
                        hold(sp, o_out, 4 * (last.n + 1), held)
                        hold(sp, rden_ready, last.n, held)
                        for j in range(4):
                            sp.dma_start(den[32 * j:32 * j + 32, :],
                                         o_raw[32 * j + KC:32 * j + KC + 1, last.slot, :, :]
                                         ).then_inc(den_in, 16)
                        hold(sp, rden_ready, last.n + 1, held)
                        hold(sp, spread_ready, 2 * last.n, held)
                        for j in range(4):
                            sp.dma_start(rrow[32 * j:32 * j + 1, :, :],
                                         rden[32 * j:32 * j + 32, :]).then_inc(rrow_in, 16)
                        sp.dma_start(xr[:, last.slot, :], x_in[last.n]).then_inc(xr_in_s[last.slot], 16)
                    if new.live:
                        hold(sp, v_ready, new.n - 1, held)
                        hold(sp, qkrot_ready, new.n - 1, held)
                        sp.dma_start(ct[:, new.slot, :], ctx[new.n]).then_inc(c_in_s[new.slot], 16)
                    if last.live:
                        hold(sp, xo_ready, last.n + 1, held)
                        sp.dma_start(x_out[last.n], xo[:, last.slot, :]).then_inc(stored[last.slot], 16)
                program(sp, step)
                for s in range(2):
                    sp.wait_ge(stored[s], 16 * TILES // 2)

            @block.gpsimd
            def _(pool):
                pool.memset(half_neg[:], -0.5).then_inc(zeroed, 1)
                pool.memset(top[:].bitcast(fp32), 0.0).then_inc(zeroed, 1)
                pool.memset(vaug[:], 0.0).then_inc(zeroed, 1)
                pool.memset(rrow[:], 0.0).then_inc(zeroed, 1)
                pool.wait_ge(zeroed, 4)
                pool.memset(vaug[:, :, :, :, KC:KC + 1], 1.0).then_inc(zeroed, 1)
                pool.wait_ge(zeroed, 5)

                def step(i):
                    new, proj, last = i.plus(3), i.plus(2), i.plus(-1)
                    if proj.live:
                        pool.wait_ge(cos_done, 2 * (proj.n + 1))
                        pool.wait_ge(sin_done, 2 * (proj.n + 1))
                        past(pool, lo_ready, proj.n)
                        past(pool, hi_ready, proj.n)
                        pool.tensor_tensor(roped[:], by_cos[:], by_sin[:], ALU.add).then_inc(roped_ready, 1)
                        pool.wait_ge(hi_ready, proj.n + 1)
                        past(pool, rep_ready, 4 * (proj.n - 1))
                        pool.tensor_tensor(lo[:, proj.slot, :], roped[:], hi[:, proj.slot, :].bitcast(fp32),
                                           ALU.subtract).then_inc(lo_ready, 1)
                    if new.live:
                        pool.wait_ge(var_ready, new.n + 1)
                        pool.tensor_tensor(rstd[:], var_eps[:], half_neg[:], ALU.pow).then_inc(rstd_ready, 1)
                    if last.live:
                        pool.wait_ge(y_ready, last.n + 1)
                        pool.wait_ge(xr_in_s[last.slot], 16 * (last.turn + 1))
                        past(pool, stored[last.slot], 16 * last.turn)
                        pool.tensor_tensor(xo[:, last.slot, :], y[:], xr[:, last.slot, :],
                                           ALU.add).then_inc(xo_ready, 1)
                program(pool, step)

            @block.scalar
            def _(act):
                act.wait_ge(const_in, 16 * 8)
                act.activation(gate[:], cols[:, 6:7], ACT.Tanh).then_inc(gate_ready, 1)

                def step(i):
                    proj, nxt = i.plus(2), i.plus(1)
                    for s in range(20):
                        if nxt.live and s in (0, 3, 6, 9):
                            g = s // 3
                            act.wait_ge(rep_ready, 4 * nxt.n + g + 1)
                            act.activation(rep[:, nxt.slot, g, :], p_x[0][:], ACT.Identity,
                                           bias=cols[:, 5:6]).then_inc(rep_out, 1)
                        if i.live and s < HEADS:
                            act.wait_ge(b_ready, HEADS * i.n + s + 1)
                            past(act, pv_done, HEADS * i.n + s + 1 - 4)
                            act.activation(prob[:, s % 4, :], p_b[s % 2][:], ACT.Exp).then_inc(prob_ready, 1)
                        if i.live and s >= 6 and (s - 6) % 4 == 0:
                            g = (s - 6) // 4
                            act.wait_ge(pv_done, HEADS * i.n + 4 * g + 4)
                            if g == 0:
                                past(act, den_in, 64 * (i.n - 1))
                                past(act, on_ready, 2 * (i.n - 1))
                            act.activation(o_raw[:, i.slot, g, :], p_o[g % 2][:, 0:T], ACT.Copy
                                           ).then_inc(o_out, 1)
                        if proj.live and s == 12:
                            act.wait_ge(roped_ready, proj.n + 1)
                            past(act, rep_ready, 4 * (proj.n - 1))
                            act.activation(hi[:, proj.slot, :], roped[:], ACT.Copy).then_inc(hi_ready, 1)
                program(act, step)

            @block.vector
            def _(dve):
                dve.wait_ge(const_in, 16 * 8)
                dve.tensor_copy(sel[:], sel_f[:]).then_inc(sel_ready, 1)
                dve.wait_ge(gate_ready, 1)
                dve.wait_ge(zeroed, 5)

                def rope(i, rotated):
                    table, out, done = (sin_t, by_sin, sin_done) if rotated else (cos_t, by_cos, cos_done)
                    dve.wait_ge(qkrot_ready if rotated else qk_ready, i.n + 1)
                    past(dve, roped_ready, i.n)
                    for n in range(2):
                        b = 2 * n + int(rotated)
                        dve.scalar_tensor_tensor(out=out[:, n * T:(n + 1) * T], in0=p_x[1][:, n * T:(n + 1) * T],
                                                 scalar=cols[:, b:b + 1], in1=table[:, n * T:(n + 1) * T],
                                                 op0=ALU.add, op1=ALU.mult).then_inc(done, 1)

                def with_maxima(i, g):
                    dve.wait_ge(m_ready, GROUPS * i.n + g + 1)
                    dve.wait_ge(rep_out, GROUPS * i.n + g + 1)
                    past(dve, b_ready, HEADS * (i.n - 1) + 4 * g + 4)
                    dve.tensor_tensor(qm[:, g, :], p_o[g % 2][:, T:2 * T], rep[:, i.slot, g, 0:T].bitcast(fp32),
                                      ALU.add).then_inc(qm_ready, 1)

                def step(i):
                    new, proj, nxt, last = i.plus(3), i.plus(2), i.plus(1), i.plus(-1)
                    for s in range(20):
                        if i.live and s == 2:
                            with_maxima(i, 3)
                        if nxt.live and 2 <= s <= HEADS + 1:
                            h = s - 2
                            dve.wait_ge(a_ready, HEADS * nxt.n + h + 1)
                            if h == 0:
                                past(dve, m_ready, GROUPS * (nxt.n - 1))
                            dve.tensor_reduce(top[:, nxt.slot, h // 4, :, 32 * (h % 4) + SPLIT],
                                              p_a[h % 2][:].rearrange("p (c s) -> p c s", c=HALF), AX, ALU.max
                                              ).then_inc(a_done, 1)
                        if nxt.live and s in (8, 12, 16):
                            with_maxima(nxt, (s - 8) // 4)
                        if proj.live and s == 3:
                            rope(proj, False)
                        if proj.live and s == 9:
                            rope(proj, True)
                        if last.live and s == 7:
                            dve.wait_ge(den_in, 64 * (last.n + 1))
                            dve.reciprocal(rden[:], den[:]).then_inc(rden_ready, 1)
                        if nxt.live and s == 11:
                            dve.wait_ge(v_ready, nxt.n + 1)
                            past(dve, pv_done, HEADS * (nxt.n - 1))
                            dve.tensor_tensor(vaug[:, nxt.slot, :, :, 0:KC].rearrange("p c h k -> p (c h) k"),
                                              p_x[0][:, 0:2 * PART].rearrange("p (n k) -> p n k", k=KC),
                                              bv[:].rearrange("p (n k) -> p n k", k=KC), ALU.add
                                              ).then_inc(vaug_ready, 1)
                        if last.live and s in (14, 15):
                            g2 = s - 14
                            dve.wait_ge(spread_ready, 2 * last.n + g2 + 1)
                            past(dve, wo_ready, last.n)
                            dve.tensor_tensor(on[:, 2 * g2:2 * g2 + 2, :],
                                              p_x[1 - g2][:].rearrange("p (g t) -> p g t", g=2),
                                              o_raw[:, last.slot, 2 * g2:2 * g2 + 2, :], ALU.mult
                                              ).then_inc(on_ready, 1)
                        if last.live and s == 19:
                            dve.wait_ge(wo_ready, last.n + 1)
                            past(dve, xo_ready, last.n)
                            dve.tensor_scalar(y[:], p_x[1][:, 0:T], cols[:, 4:5], gate[:], ALU.add, ALU.mult
                                              ).then_inc(y_ready, 1)
                        if new.live and s == 13:
                            dve.wait_ge(x_in_s[new.slot], 16 * (new.turn + 1))
                            dve.bn_stats(stats[:], xt[:, new.slot, :]).then_inc(stats_ready, 1)
                            hold(dve, stats_ready, 2 * new.n + 1, held)
                            dve.bn_aggr(mv[:], stats[:]).then_inc(stats_ready, 1)
                            dve.wait_ge(stats_ready, 2 * new.n + 2)
                            past(dve, rstd_ready, new.n)
                            dve.tensor_scalar_add(var_eps[:], mv[:, 1:2], EPS).then_inc(var_ready, 1)
                        if new.live and s == 17:
                            dve.wait_ge(rstd_ready, new.n + 1)
                            past(dve, qkrot_ready, new.n - 1)
                            dve.tensor_scalar(xn[:, new.slot, :], xt[:, new.slot, :], mv[:, 0:1], rstd[:],
                                              ALU.subtract, ALU.mult).then_inc(xn_ready, 1)
                program(dve, step)

            @block.tensor
            def _(pe):
                pe.wait_ge(sel_ready, 1)
                pe.wait_ge(zeroed, 5)

                def project(i, rotated):
                    r = int(rotated)
                    if not rotated:
                        pe.wait_ge(xn_ready, i.n + 1)
                        pe.wait_ge(c_in_s[i.slot], 16 * (i.turn + 1))
                    pe.matmul(p_x[1][:, 0:T], w_in[:, r, :], xn[:, i.slot, :], start=True, stop=True)
                    pe.matmul(p_x[1][:, T:2 * T], w_in[:, 2 + r, :], ct[:, i.slot, :], start=True, stop=True
                              ).then_inc(qkrot_ready if rotated else qk_ready, 1)

                def move_maxima(i, g):
                    pe.wait_ge(a_done, HEADS * i.n + 4 * g + 4)
                    past(pe, o_out, GROUPS * (i.n - 1) + g + 1)
                    for tc in range(HALF):
                        mm = pe.matmul(p_o[g % 2][:, T + tc * PART:T + (tc + 1) * PART], top[:, i.slot, g, tc, :],
                                       sel[:, 16, :], start=True, stop=True)
                    mm.then_inc(m_ready, 1)

                def step(i):
                    proj, nxt, last = i.plus(2), i.plus(1), i.plus(-1)
                    for s in range(20):
                        if i.live and s == 2:
                            move_maxima(i, 3)
                        if nxt.live and s in (7, 11, 15):
                            move_maxima(nxt, (s - 7) // 4)
                        if nxt.live and s in (0, 3, 6, 9):
                            g = s // 3
                            if g == 0:
                                pe.wait_ge(lo_ready, nxt.n + 1)
                                past(pe, vaug_ready, nxt.n)
                                past(pe, on_ready, 2 * last.n)
                            else:
                                pe.wait_ge(rep_out, 4 * nxt.n + g)
                            for n in range(2):
                                for part, of in enumerate((hi, lo)):
                                    mm = pe.matmul(p_x[0][:, n * T:(n + 1) * T], sel[:, 4 * g + 2 * n + part, :],
                                                   of[:, nxt.slot, n * T:(n + 1) * T],
                                                   start=(part == 0), stop=(part == 1))
                            mm.then_inc(rep_ready, 1)
                        if proj.live and s == 2:
                            past(pe, y_ready, i.n - 1)
                            past(pe, sin_done, 2 * proj.n)
                            project(proj, False)
                        if proj.live and s == 8:
                            pe.wait_ge(cos_done, 2 * (proj.n + 1))
                            project(proj, True)
                        if nxt.live and s == 10:
                            pe.wait_ge(rep_out, 4 * nxt.n + 4)
                            for sc in range(HALF):
                                mm = pe.matmul(p_x[0][:, sc * PART:(sc + 1) * PART],
                                               ct[:, nxt.slot, sc * PART:(sc + 1) * PART], w_in[:, 4, :],
                                               start=True, stop=True)
                            mm.then_inc(v_ready, 1)
                        if last.live and s in (13, 14):
                            g2 = s - 13
                            if g2 == 0:
                                pe.wait_ge(rrow_in, 64 * (last.n + 1))
                                if proj.live:
                                    pe.wait_ge(sin_done, 2 * (proj.n + 1))
                                else:
                                    past(pe, y_ready, last.n)
                            elif nxt.live:
                                pe.wait_ge(vaug_ready, nxt.n + 1)
                            for g in range(2):
                                mm = pe.matmul(p_x[1 - g2][:, g * T:(g + 1) * T], spread[:],
                                               rrow[:, 2 * g2 + g, :], start=True, stop=True)
                            mm.then_inc(spread_ready, 1)
                        if last.live and s == 18:
                            pe.wait_ge(on_ready, 2 * last.n + 2)
                            for g in range(GROUPS):
                                mm = pe.matmul(p_x[1][:, 0:T], w_out[:, g, :], on[:, g, :],
                                               start=(g == 0), stop=(g == GROUPS - 1))
                            mm.then_inc(wo_ready, 1)
                        if i.live and s < HEADS:
                            h, g, r = s, s // 4, 32 * (s % 4)
                            if s % 4 == 0:
                                pe.wait_ge(qm_ready, GROUPS * i.n + g + 1)
                            past(pe, prob_ready, HEADS * i.n + h - 1)
                            for sc in range(HALF):
                                at = T + sc * PART
                                mm = pe.matmul(p_b[h % 2][:, sc * T:(sc + 1) * T],
                                               rep[r:r + SPLIT + 1, i.slot, g, at:at + PART],
                                               qm[r:r + SPLIT + 1, g, :], start=True, stop=True)
                            mm.then_inc(b_ready, 1)
                        if i.live and 2 <= s <= HEADS + 1:
                            h, g, r = s - 2, (s - 2) // 4, 32 * ((s - 2) % 4)
                            pe.wait_ge(prob_ready, HEADS * i.n + h + 1)
                            if h % 4 == 0:
                                past(pe, o_out, GROUPS * i.n + g - 1)
                                if g < 2 or nxt.live:
                                    pe.wait_ge(qm_ready, GROUPS * i.n + 3 + g)
                            for sc in range(HALF):
                                mm = pe.matmul(p_o[g % 2][r:r + 32, 0:T], vaug[:, i.slot, sc, h, :],
                                               prob[:, h % 4, sc * T:(sc + 1) * T],
                                               start=(sc == 0), stop=(sc == HALF - 1), tile_position=(0, r))
                            mm.then_inc(pv_done, 1)
                        if nxt.live and 2 <= s <= HEADS + 1:
                            h = s - 2
                            g, r = h // 4, 32 * (h % 4)
                            if h % 4 == 0:
                                pe.wait_ge(rep_out, 4 * nxt.n + g + 1)
                            past(pe, a_done, HEADS * nxt.n + h - 1)
                            for tc in range(HALF):
                                mm = pe.matmul(p_a[h % 2][:, tc * T:(tc + 1) * T],
                                               rep[r:r + SPLIT, nxt.slot, g, tc * PART:(tc + 1) * PART],
                                               rep[r:r + SPLIT, nxt.slot, g, T:2 * T], start=True, stop=True)
                            mm.then_inc(a_ready, 1)
                program(pe, step)


def _tables():
    f = np.float32
    inv = f(1.0) / f(10000.0) ** (np.arange(0, 8, 2, dtype=f) / f(8))
    ang = np.arange(256, dtype=f)[None, :] * np.tile(inv, 2)[:, None].astype(f)
    cos8, sin8 = np.cos(ang).astype(f), np.sin(ang).astype(f)
    sin8 = sin8 * np.array([-1] * 4 + [1] * 4, f)[:, None]
    s = f(1 / np.sqrt(8.0))
    out = {}
    out["sa_cos"] = np.concatenate([np.tile(cos8, (16, 1)) * s, np.tile(cos8, (16, 1))], 1).astype(f)
    out["sa_sin"] = np.concatenate([np.tile(sin8, (16, 1)) * s, np.tile(sin8, (16, 1))], 1).astype(f)
    sel = np.zeros((128, 17, 128), f)
    for g in range(4):
        for j in range(4):
            for c in range(8):
                row = (4 * g + j) * 8 + c
                at = 32 * j + c
                for kind, places in enumerate(((0, 8), (16,), (0, 16), (8,))):
                    for p in places:
                        sel[row, 4 * g + kind, at + p] = 1
    sel[:, 16, :] = np.eye(128, dtype=f)
    out["sa_sel"] = sel
    spread = np.zeros((128, 128), f)
    for j in range(4):
        spread[32 * j, 32 * j:32 * j + 32] = 1
    out["spread"] = spread
    return out


def _layout_softmax_attention(a):
    f = np.float32
    perm = np.arange(64).reshape(8, 2, 4)[:, ::-1].reshape(64)
    w_in = np.zeros((128, 5, 128), f)
    Wq, Wk, Wv, Wo = (np.asarray(a[f"L0_xattn_W{n}"]) for n in "qkvo")
    for n, w in enumerate((Wq, Wq[perm], Wk, Wk[perm], Wv)):
        for b in range(2):
            w_in[64 * b:64 * b + 64, n, 64 * b:64 * b + 64] = w.T
    w_out = np.zeros((128, 4, 128), f)
    for g in range(4):
        for j in range(4):
            h = 4 * (g % 2) + j
            w_out[32 * j:32 * j + 8, g, 64 * (g // 2):64 * (g // 2) + 64] = Wo[:, 8 * h:8 * h + 8].T
    cols = np.zeros((128, 8), f)
    bq, bk, bo, bv = (np.asarray(a[f"L0_xattn_b{n}"]) for n in ("q", "k", "o", "v"))
    for n, b in enumerate((bq, bq[perm], bk, bk[perm], bo)):
        cols[:, n] = np.tile(b, 2)
    cols[24::32, 5] = -1
    cols[:, 6] = np.asarray(a["g_xattn"])[0]
    return {"sa_w_in": w_in, "sa_w_out": w_out, "sa_cols": cols, "sa_bv": np.tile(bv, (128, 4))}

CHUNK = 512
CHUNKS = ROWS // CHUNK


def stage_experts(nc, name, x_in, x_out, w_gate, w_up, w_down, c, EXPERTS, HIDDEN, TOP, norm, skip=None):
    KC = DIM // PART
    MC = HIDDEN // PART
    WIDTH = 2 * KC * HIDDEN + MC * DIM
    UP, DOWN = KC * HIDDEN, 2 * KC * HIDDEN
    E8 = EXPERTS + 8
    LOWEST, MARK = -3.0e38, -3.2e38
    GRP = 8
    FREE = 2 * CHUNK // PART
    st = ExitStack()
    sb = lambda n, s, d=fp32: st.enter_context(nc.sbuf_tensor(f"{name}_{n}", s, d))
    sem = lambda n: nc.alloc_semaphore(f"{name}_{n}")
    with st:
        total = sb("total", [PART, TILES, DIM])
        ht_hi, ht_lo = (sb(n, [PART, KC, ROWS], fp32r) for n in ("ht_hi", "ht_lo"))
        ident, router = sb("ident", [PART, PART]), sb("router", [PART, KC, EXPERTS])
        g_col, gate = sb("g_col", [PART, 1]), sb("gate", [PART, 1])
        norm_w = sb("norm_w", [PART, DIM]) if norm == "rms" else None
        half_neg = sb("half_neg", [PART, GRP])
        stats, mv = sb("stats", [PART, TILES, 6]), sb("mv", [PART, TILES, 2])
        var_eps, rstd = sb("var_eps", [PART, TILES]), sb("rstd", [PART, TILES])
        hn, ht = sb("hn", [PART, 2, DIM]), sb("ht", [PART, 2, DIM])
        score, left = sb("score", [PART, TILES, E8]), sb("left", [PART, TILES, E8])
        top8, taken = sb("top8", [PART, TILES, 8]), sb("taken", [PART, TILES, 8])
        shifted, picked = sb("shifted", [PART, TILES, EXPERTS]), sb("picked", [PART, TILES, EXPERTS])
        weight = sb("weight", [PART, TILES, EXPERTS])
        wsum = sb("wsum", [PART, TILES])
        raw = sb("raw", [PART, 2, WIDTH])
        w_hi, w_lo = (sb(n, [PART, 2, WIDTH], fp32r) for n in ("w_hi", "w_lo"))
        silu, act_f = sb("silu", [PART, 2, CHUNK]), sb("act_f", [PART, 2, CHUNK])
        a_hi, a_lo = (sb(n, [PART, 2, MC, CHUNK], fp32r) for n in ("a_hi", "a_lo"))
        bank = lambda n: st.enter_context(nc.psum_tensor(f"{name}_{n}", [PART, CHUNK], fp32))
        p_gate, p_up = [bank(f"pg{i}") for i in range(2)], [bank(f"pu{i}") for i in range(2)]
        p_y = [bank(f"py{i}") for i in range(4)]
        p_t, p_s = p_gate, p_up

        const_in, zeroed, gate_ready = sem("const_in"), sem("zeroed"), sem("gate")
        x_loaded = [sem(f"x{i}") for i in range(TILES // GRP)]
        stat, var_ready, rstd_ready, hn_ready = sem("stat"), sem("var"), sem("rstd"), sem("hn")
        t_ready, ht_ready, hi_ready, lo_ready = sem("t"), sem("ht"), sem("hi"), sem("lo")
        s_ready, score_out, route = sem("s"), sem("score_out"), sem("route")
        shifted_ready, exp_ready = sem("shifted"), sem("exp")
        weight_ready, square = sem("weight"), sem("square")
        raw_in = [sem(f"raw{i}") for i in range(2)]
        whi_ready, wlo_ready = sem("whi"), sem("wlo")
        gate_mm, up_mm, silu_ready, act_ready = sem("gate_mm"), sem("up_mm"), sem("silu"), sem("act")
        ahi_ready, alo_ready, y_mm, y_added = sem("ahi"), sem("alo"), sem("y_mm"), sem("y_added")
        skip_in = [sem(f"skip{i}") for i in range(2)]
        final = sem("final")
        held = sem("held")
        stored = sem("stored")

        def per_tile(eng, step):
            for n in range(-1, 3):
                step(Tile(0, n))
            with eng.Fori(0, (TILES - 4) // 2) as k:
                step(Tile(k, 3))
                step(Tile(k, 4))
            step(Tile(0, TILES - 1))

        def per_unit(eng, begin, unit):
            def chunks(e):
                begin(e)
                unit(e, Tile(0, 0), (e.plus(-1), Tile(0, CHUNKS - 1)))
                unit(e, Tile(0, 1), (e, Tile(0, 0)))
                with eng.Fori(0, CHUNKS // 2 - 1) as j:
                    unit(e, Tile(j, 2), (e, Tile(j, 1)))
                    unit(e, Tile(j, 3), (e, Tile(j, 2)))
            for s in range(2):
                chunks(Tile(0, s))
            with eng.Fori(0, EXPERTS // 2 - 1) as k:
                for s in range(2, 4):
                    chunks(Tile(k, s))

        def first(e):
            return isinstance(e.k, int) and e.n < 0

        with nc.Block() as block:
            @block.sync
            def _(sp):
                consts = [(ident, c["ident"]), (router, c[name + "_router"]), (g_col, c[name + "_g"])]
                if norm == "rms":
                    consts.append((norm_w, c[name + "_norm_w"]))
                for dst, src in consts:
                    sp.dma_start(dst[:], src).then_inc(const_in, 16)
                for g in range(TILES // GRP):
                    sp.dma_start(total[:, g * GRP:(g + 1) * GRP, :],
                                 x_in[g * GRP:(g + 1) * GRP].rearrange("t p d -> p t d")).then_inc(x_loaded[g], 16)

                def load(e):
                    hold(sp, whi_ready, e.n - 1, held)
                    hold(sp, wlo_ready, e.n - 1, held)
                    r = raw[:, e.slot, :]
                    sp.dma_start(r[:, 0:UP].rearrange("p (k h) -> p k h", k=KC),
                                 w_gate[e.n].rearrange("(k p) h -> p k h", p=PART)).then_inc(raw_in[e.slot], 16)
                    sp.dma_start(r[:, UP:DOWN].rearrange("p (k h) -> p k h", k=KC),
                                 w_up[e.n].rearrange("(k p) h -> p k h", p=PART)).then_inc(raw_in[e.slot], 16)
                    sp.dma_start(r[:, DOWN:WIDTH].rearrange("p (k h) -> p k h", k=MC),
                                 w_down[e.n].rearrange("(k p) h -> p k h", p=PART)).then_inc(raw_in[e.slot], 16)
                for s in range(2):
                    load(Tile(0, s))
                with sp.Fori(0, EXPERTS // 2 - 1) as k:
                    for s in range(2, 4):
                        load(Tile(k, s))
                if norm == "layer":
                    for g in range(TILES // GRP):
                        sp.wait_ge(y_added, FREE + (EXPERTS - 1) * TILES + (g + 1) * GRP)
                        sp.dma_start(x_out[g * GRP:(g + 1) * GRP].rearrange("t p d -> p t d"),
                                     total[:, g * GRP:(g + 1) * GRP, :]).then_inc(stored, 16)
                    sp.wait_ge(stored, 16 * TILES // GRP)
                else:
                    sp.wait_ge(y_mm, 2 * CHUNKS * EXPERTS)
                    room = ht_hi[:].rearrange("p k r -> p (k r)").rearrange("p (t d) -> p t d", d=DIM)
                    for g in range(2):
                        sp.dma_start(room[:, g * 16:(g + 1) * 16, :].bitcast(fp32),
                                     skip[g * 16:(g + 1) * 16].rearrange("t p d -> p t d")
                                     ).then_inc(skip_in[g], 16)
                    for g in range(8):
                        sp.wait_ge(final, g + 1)
                        sp.dma_start(x_out[g * 4:(g + 1) * 4].rearrange("t p d -> p t d"),
                                     total[:, g * 4:(g + 1) * 4, :]).then_inc(stored, 16)
                    sp.wait_ge(stored, 16 * 8)

            @block.gpsimd
            def _(pool):
                pool.memset(half_neg[:], -0.5).then_inc(zeroed, 1)
                pool.memset(score[:], LOWEST).then_inc(zeroed, 1)
                pool.memset(taken[:], LOWEST).then_inc(zeroed, 1)
                pool.wait_ge(zeroed, 3)

                for g in range(TILES // GRP):
                    grp = slice(g * GRP, (g + 1) * GRP)
                    pool.wait_ge(var_ready, g + 1)
                    pool.tensor_tensor(rstd[:, grp], var_eps[:, grp], half_neg[:], ALU.pow).then_inc(rstd_ready, GRP)

                def step(i):
                    if i.live:
                        pool.wait_ge(hi_ready, i.n + 1)
                        pool.wait_ge(ht_ready, i.n + 1)
                        pool.tensor_tensor(ht_lo[:, :, bass.ds(i.n * PART, PART)],
                                           ht[:, i.slot, :].rearrange("p (k t) -> p k t", k=KC),
                                           ht_hi[:, :, bass.ds(i.n * PART, PART)].bitcast(fp32),
                                           ALU.subtract).then_inc(lo_ready, 1)
                per_tile(pool, step)

                def unit(e, ch, prev):
                    for m in range(MC):
                        n = (e.n * CHUNKS + ch.n) * MC + m
                        pool.wait_ge(ahi_ready, n + 1)
                        pool.tensor_tensor(a_lo[:, ch.slot, m, :], act_f[:, m if MC == 2 else ch.slot, :],
                                           a_hi[:, ch.slot, m, :].bitcast(fp32), ALU.subtract
                                           ).then_inc(alo_ready, 1)
                per_unit(pool, lambda e: None, unit)

            @block.scalar
            def _(act):
                act.wait_ge(const_in, 16 * (4 if norm == "rms" else 3))
                act.activation(gate[:], g_col[:], ACT.Tanh).then_inc(gate_ready, 1)
                act.wait_ge(zeroed, 3)

                def keep_score(i):
                    act.wait_ge(s_ready, i.n + 1)
                    act.activation(score[:, i.n, 0:EXPERTS], p_s[i.slot][:, 0:EXPERTS], ACT.Copy
                                   ).then_inc(score_out, 1)

                def step(i):
                    old = i.plus(-1)
                    if i.live:
                        act.wait_ge(t_ready, i.n + 1)
                        past(act, s_ready, i.n - 1)
                        past(act, lo_ready, i.n - 1)
                        act.activation(ht[:, i.slot, :], p_t[i.slot][:, 0:DIM], ACT.Copy).then_inc(ht_ready, 1)
                        act.activation(ht_hi[:, :, bass.ds(i.n * PART, PART)],
                                       p_t[i.slot][:, 0:DIM].rearrange("p (k t) -> p k t", k=KC),
                                       ACT.Copy).then_inc(hi_ready, 1)
                    if old.live:
                        keep_score(old)
                per_tile(act, step)
                keep_score(Tile(0, TILES - 1))

                def split(e):
                    act.wait_ge(raw_in[e.slot], 48 * (e.turn + 1))
                    past(act, y_mm, 2 * CHUNKS * (e.n - 1))
                    act.activation(w_hi[:, e.slot, :], raw[:, e.slot, :], ACT.Copy).then_inc(whi_ready, 1)
                split(Tile(0, 0))
                split(Tile(0, 1))
                act.wait_ge(shifted_ready, 1)
                act.activation(weight[:], shifted[:], ACT.Exp).then_inc(exp_ready, 1)

                def begin(e):
                    if not isinstance(e.k, int):
                        split(e)

                def unit(e, ch, prev):
                    for m in range(MC):
                        n = (e.n * CHUNKS + ch.n) * MC + m
                        slot = m if MC == 2 else ch.slot
                        act.wait_ge(gate_mm, n + 1)
                        past(act, act_ready, n - 1)
                        act.activation(silu[:, slot, :], p_gate[slot][:], ACT.Silu).then_inc(silu_ready, 1)
                    for m in range(MC):
                        n = (e.n * CHUNKS + ch.n) * MC + m
                        slot = m if MC == 2 else ch.slot
                        act.wait_ge(act_ready, n + 1)
                        past(act, y_mm, 2 * (e.n * CHUNKS + ch.n - 1))
                        act.activation(a_hi[:, ch.slot, m, :], act_f[:, slot, :], ACT.Copy).then_inc(ahi_ready, 1)
                per_unit(act, begin, unit)

            @block.vector
            def _(dve):
                dve.wait_ge(zeroed, 3)
                dve.wait_ge(const_in, 16 * (4 if norm == "rms" else 3))
                for g in range(TILES // GRP):
                    grp = slice(g * GRP, (g + 1) * GRP)
                    dve.wait_ge(x_loaded[g], 16)
                    for t in range(g * GRP, (g + 1) * GRP):
                        dve.bn_stats(stats[:, t, :], total[:, t, :]).then_inc(stat, 1)
                    dve.wait_ge(stat, (2 * g + 1) * GRP)
                    for t in range(g * GRP, (g + 1) * GRP):
                        dve.bn_aggr(mv[:, t, :], stats[:, t, :]).then_inc(stat, 1)
                    dve.wait_ge(stat, (2 * g + 2) * GRP)
                    mean, var = mv[:, grp, 0], mv[:, grp, 1]
                    if norm == "rms":
                        dve.tensor_tensor(var_eps[:, grp], mean, mean, ALU.mult).then_inc(square, 1)
                        dve.wait_ge(square, 2 * g + 1)
                        dve.tensor_tensor(var_eps[:, grp], var_eps[:, grp], var, ALU.add).then_inc(square, 1)
                        dve.wait_ge(square, 2 * g + 2)
                        var = var_eps[:, grp]
                    dve.tensor_scalar_add(var_eps[:, grp], var, EPS).then_inc(var_ready, 1)

                def step(i):
                    new = i.plus(1)
                    if new.live:
                        s = new.slot
                        dve.wait_ge(rstd_ready, new.n + 1)
                        past(dve, t_ready, new.n - 1)
                        if norm == "rms":
                            dve.scalar_tensor_tensor(out=hn[:, s, :], in0=total[:, new.n, :],
                                                     scalar=rstd[:, bass.ds(new.n, 1)], in1=norm_w[:],
                                                     op0=ALU.mult, op1=ALU.mult).then_inc(hn_ready, 1)
                        else:
                            dve.tensor_scalar(hn[:, s, :], total[:, new.n, :], mv[:, new.n, 0:1],
                                              rstd[:, bass.ds(new.n, 1)], ALU.subtract, ALU.mult
                                              ).then_inc(hn_ready, 1)
                per_tile(dve, step)

                def split(e):
                    dve.wait_ge(whi_ready, e.n + 1)
                    dve.tensor_tensor(w_lo[:, e.slot, :], raw[:, e.slot, :], w_hi[:, e.slot, :].bitcast(fp32),
                                      ALU.subtract).then_inc(wlo_ready, 1)
                split(Tile(0, 0))
                split(Tile(0, 1))

                dve.wait_ge(score_out, TILES)
                for t in range(TILES):
                    dve.max(top8[:, t, :], score[:, t, 0:EXPERTS]).then_inc(route, 1)
                dve.wait_ge(route, TILES)
                dve.tensor_tensor(shifted[:], score[:, :, 0:EXPERTS],
                                  top8[:, :, 0:1].to_broadcast([PART, TILES, EXPERTS]), ALU.subtract
                                  ).then_inc(shifted_ready, 1)
                dve.tensor_copy(taken[:, :, 0:TOP], top8[:, :, 0:TOP]).then_inc(route, 1)
                dve.wait_ge(route, TILES + 1)
                for t in range(TILES):
                    dve.match_replace(left[:, t, :], taken[:, t, :], score[:, t, :], MARK).then_inc(route, 1)
                dve.wait_ge(route, 2 * TILES + 1)
                dve.tensor_tensor(picked[:], left[:, :, 0:EXPERTS], score[:, :, 0:EXPERTS], ALU.not_equal
                                  ).then_inc(weight_ready, 1)
                dve.wait_ge(weight_ready, 1)
                dve.engine_nop().then_inc(y_added, FREE)
                dve.wait_ge(exp_ready, 1)
                dve.tensor_tensor(weight[:], weight[:], picked[:], ALU.mult).then_inc(weight_ready, 1)
                dve.wait_ge(weight_ready, 2)
                dve.tensor_reduce(wsum[:], weight[:], AX, ALU.add).then_inc(weight_ready, 1)
                dve.wait_ge(weight_ready, 3)
                dve.reciprocal(wsum[:], wsum[:]).then_inc(weight_ready, 1)
                dve.wait_ge(weight_ready, 4)
                if norm == "layer":
                    dve.wait_ge(gate_ready, 1)
                    dve.tensor_scalar(wsum[:], wsum[:], gate[:], None, ALU.mult).then_inc(weight_ready, 1)
                else:
                    dve.tensor_scalar(wsum[:], wsum[:], 1.0, None, ALU.mult).then_inc(weight_ready, 1)
                dve.wait_ge(weight_ready, 5)
                dve.tensor_tensor(weight[:], weight[:], wsum[:].unsqueeze(2).to_broadcast([PART, TILES, EXPERTS]),
                                  ALU.mult).then_inc(weight_ready, 1)
                dve.wait_ge(weight_ready, 6)

                def begin(e):
                    if not isinstance(e.k, int):
                        split(e)

                def add(e, ch):
                    for t in range(CHUNK // PART):
                        n = (e.n * CHUNKS + ch.n) * 4 + t
                        if t % 2 == 0:
                            dve.wait_ge(y_mm, (e.n * CHUNKS + ch.n) * 2 + t // 2 + 1)
                        tile = 4 * ch.n + t
                        if not (isinstance(e.k, int) and e.n == 0):
                            dve.wait_ge(y_added, FREE + n - 31)
                        dve.scalar_tensor_tensor(out=total[:, tile, :],
                                                 in0=p_y[2 * ch.slot + t // 2][:, (t % 2) * DIM:(t % 2 + 1) * DIM],
                                                 scalar=weight[:, tile, bass.ds(e.n, 1)], in1=total[:, tile, :],
                                                 op0=ALU.mult, op1=ALU.add).then_inc(y_added, 1)

                def unit(e, ch, prev):
                    for m in range(MC):
                        n = (e.n * CHUNKS + ch.n) * MC + m
                        slot = m if MC == 2 else ch.slot
                        dve.wait_ge(silu_ready, n + 1)
                        dve.wait_ge(up_mm, n + 1)
                        past(dve, alo_ready, n - 1)
                        dve.tensor_tensor(act_f[:, slot, :], silu[:, slot, :], p_up[slot][:], ALU.mult
                                          ).then_inc(act_ready, 1)
                    if not first(prev[0]):
                        add(*prev)
                per_unit(dve, begin, unit)
                add(Tile(0, EXPERTS - 1), Tile(0, CHUNKS - 1))
                if norm == "rms":
                    dve.wait_ge(gate_ready, 1)
                    dve.wait_ge(y_added, FREE + EXPERTS * TILES)
                    room = ht_hi[:].rearrange("p k r -> p (k r)").rearrange("p (t d) -> p t d", d=DIM)
                    for g in range(8):
                        if g % 4 == 0:
                            dve.wait_ge(skip_in[g // 4], 16)
                        rows = total[:, 4 * g:4 * g + 4, :]
                        dve.scalar_tensor_tensor(out=rows, in0=rows, scalar=gate[:],
                                                 in1=room[:, 4 * g:4 * g + 4, :].bitcast(fp32),
                                                 op0=ALU.mult, op1=ALU.add).then_inc(final, 1)

            @block.tensor
            def _(pe):
                pe.wait_ge(const_in, 16 * (4 if norm == "rms" else 3))

                def step(i):
                    new = i.plus(1)
                    if new.live:
                        pe.wait_ge(hn_ready, new.n + 1)
                        past(pe, ht_ready, new.n - 1)
                        past(pe, hi_ready, new.n - 1)
                        for k in range(KC):
                            mm = pe.transpose(p_t[new.slot][:, k * PART:(k + 1) * PART],
                                              hn[:, new.slot, k * PART:(k + 1) * PART], ident[:])
                        mm.then_inc(t_ready, 1)
                    if i.live:
                        pe.wait_ge(ht_ready, i.n + 1)
                        past(pe, score_out, i.n - 1)
                        for k in range(KC):
                            mm = pe.matmul(p_s[i.slot][:, 0:EXPERTS], ht[:, i.slot, k * PART:(k + 1) * PART],
                                           router[:, k, :], start=(k == 0), stop=(k == KC - 1))
                        mm.then_inc(s_ready, 1)
                per_tile(pe, step)
                pe.wait_ge(lo_ready, TILES)
                pe.wait_ge(score_out, TILES)

                def product(out, lhs, rhs, blocks):
                    n = 0
                    for b in range(blocks):
                        (lh, ll), (rh, rl) = lhs(b), rhs(b)
                        for x, y in ((lh, rh), (lh, rl), (ll, rh)):
                            mm = pe.matmul(out, x, y, start=(n == 0), stop=(n == 3 * blocks - 1))
                            n += 1
                    return mm

                def down(e, ch):
                    pe.wait_ge(alo_ready, (e.n * CHUNKS + ch.n + 1) * MC)
                    for t in range(4):
                        if t % 2 == 0:
                            pe.wait_ge(y_added, FREE + 4 * (e.n * CHUNKS + ch.n - 2) + 2 * (t // 2) + 2)
                        mm = product(p_y[2 * ch.slot + t // 2][:, (t % 2) * DIM:(t % 2 + 1) * DIM],
                                     lambda m: [a[:, ch.slot, m, t * PART:(t + 1) * PART] for a in (a_hi, a_lo)],
                                     lambda m: [w[:, e.slot, DOWN + m * DIM:DOWN + (m + 1) * DIM]
                                                for w in (w_hi, w_lo)], MC)
                        if t % 2 == 1:
                            mm.then_inc(y_mm, 1)

                def begin(e):
                    pe.wait_ge(wlo_ready, e.n + 1)

                def unit(e, ch, prev):
                    for m in range(MC):
                        n = (e.n * CHUNKS + ch.n) * MC + m
                        slot = m if MC == 2 else ch.slot
                        for bank_, at, done, free in ((p_gate, 0, gate_mm, silu_ready), (p_up, UP, up_mm, act_ready)):
                            past(pe, free, n - 1)
                            product(bank_[slot][:],
                                    lambda k: [w[:, e.slot, at + k * HIDDEN + m * PART:at + k * HIDDEN + (m + 1) * PART]
                                               for w in (w_hi, w_lo)],
                                    lambda k: [h[:, k, bass.ds(ch.n * CHUNK, CHUNK)] for h in (ht_hi, ht_lo)], KC
                                    ).then_inc(done, 1)
                    if not first(prev[0]):
                        down(*prev)
                per_unit(pe, begin, unit)
                down(Tile(0, EXPERTS - 1), Tile(0, CHUNKS - 1))



def _layout_experts(a):
    f = np.float32
    block = lambda w: np.ascontiguousarray(np.asarray(w).reshape(2, 128, -1).transpose(1, 0, 2))
    col = lambda v: np.full((128, 1), v, f)
    return {"ident": np.eye(128, dtype=f),
            "moe0_router": block(a["L0_ffn_router_w"]), "moe0_g": col(np.asarray(a["g_ffn"])[0]),
            "moe1_router": block(a["L1_ffn_wg"]), "moe1_g": col(np.asarray(a["g_ffn"])[1]),
            "moe1_norm_w": np.tile(np.asarray(a["L1_ffn_ff_ln_w"]), (128, 1))}


def stage_linear_attention(nc, x_in, x_out, ctx, c):
    KC, TPC, HEADS, HC, F = 2, CHUNK // PART, 16, 16, 64
    PAIRS, HALF = HEADS // 2, 4
    E = HC + 1
    WQ, WK, WV, WFQ, WFK, WEND = 0, 512, 1024, 1536, 2048, 2560
    st = ExitStack()
    sb = lambda n, s, d=fp32: st.enter_context(nc.sbuf_tensor(f"la_{n}", s, d))
    sem = lambda n: nc.alloc_semaphore(f"la_{n}")
    with st:
        raw = sb("raw", [PART, WEND])
        w_hi, w_lo = (sb(n, [PART, WEND], fp32r) for n in ("w_hi", "w_lo"))
        w_out = sb("w_out", [PART, KC, DIM])
        ident, cols, mask = sb("ident", [PART, PART]), sb("cols", [PART, 8]), sb("mask", [PART, TILES])
        bv, bo = sb("bv", [PART, DIM]), sb("bo", [PART, DIM])
        gate, half_neg = sb("gate", [PART, 1]), sb("half_neg", [PART, 1])
        rows = sb("rows", [PART, 2, 2, TPC, DIM])
        stats, mv = sb("stats", [PART, 6]), sb("mv", [PART, 2])
        var_eps, rstd = sb("var_eps", [PART, 1]), sb("rstd", [PART, 1])
        hn = sb("hn", [PART, 2, DIM])
        t_hi, t_lo = (sb(n, [PART, 2, 2, KC, CHUNK], fp32r) for n in ("t_hi", "t_lo"))
        qk_hi, qk_lo = (sb(n, [PART, 2, 4, CHUNK], fp32r) for n in ("qk_hi", "qk_lo"))
        qf = sb("qf", [PART, 2, PAIRS, CHUNK])
        kf = sb("kf", [PART, 2, HEADS * F])
        vb = sb("vb", [PART, 2, PAIRS, 2, 2, E])
        kv = sb("kv", [PART, 2, PAIRS, 2, 2, E])
        den, rden = sb("den", [PART, 2, HALF, 2]), sb("rden", [PART, 2, HALF, 2])
        on, o_t = sb("on", [PART, 2, DIM]), sb("o_t", [PART, 2, DIM])
        xr, y, xo = sb("xr", [PART, 2, DIM]), sb("y", [PART, DIM]), sb("xo", [PART, 2, DIM])
        bank = lambda n: st.enter_context(nc.psum_tensor(f"la_{n}", [PART, CHUNK], fp32))
        p_t, p_k, p_v, p_kv, p_q, p_y = (bank(n) for n in ("ptt", "pk", "pv", "pkv", "pq", "py"))
        p_p = [bank(f"pp{i}") for i in range(2)]

        const_in, zeroed, gate_ready = sem("const_in"), sem("zeroed"), sem("gate")
        whi_ready, wlo_ready = sem("whi"), sem("wlo")
        in_s = [sem(f"in{i}") for i in range(2)]
        xr_s = [sem(f"xr{i}") for i in range(2)]
        stat, var_ready, rstd_ready, hn_ready = sem("stat"), sem("var"), sem("rstd"), sem("hn")
        t_ready, thi_ready, tlo_ready = sem("t"), sem("thi"), sem("tlo")
        qk_mm, qkhi_ready, qklo_ready, qf_mm, qf_ready = sem("qk_mm"), sem("qkhi"), sem("qklo"), sem("qf_mm"), sem("qf")
        kf_mm, kf_ready, v_mm, v_ready = sem("kf_mm"), sem("kf"), sem("v_mm"), sem("v")
        kv_mm, kv_low, kv_high = sem("kv_mm"), sem("kv_low"), sem("kv_high")
        q_mm, den_ready, on_ready = sem("q_mm"), sem("den"), sem("on")
        ot_mm, ot_ready, y_mm, y_ready, xo_ready = sem("ot_mm"), sem("ot"), sem("y_mm"), sem("y"), sem("xo")
        held = sem("held")
        stored = [sem(f"stored{i}") for i in range(2)]

        def live(ch):
            return not isinstance(ch.k, int) or 0 <= ch.n < CHUNKS

        def program(eng, chunk_step, turns=(CHUNKS - 2) // 2):
            chunk_step(Tile(0, -1))
            chunk_step(Tile(0, 0))
            with eng.Fori(0, turns) as k:
                chunk_step(Tile(k, 1))
                chunk_step(Tile(k, 2))
            for n in range(2 * turns + 1, CHUNKS + 1):
                chunk_step(Tile(0, n))

        class Row:
            def __init__(self, ch, t):
                self.ch, self.t = ch.plus(t // TPC), t % TPC
                self.live = live(self.ch)
                self.n = TPC * self.ch.n + self.t
                self.slot = self.t % 2
                self.turn = 2 * self.ch.n + self.t // 2

        with nc.Block() as block:
            @block.sync
            def _(sp):
                for dst, name in ((raw, "la_w"), (w_out, "la_w_out"), (ident, "ident"), (cols, "la_cols"),
                                  (mask, "la_mask"), (bv, "la_bv"), (bo, "la_bo")):
                    sp.dma_start(dst[:], c[name]).then_inc(const_in, 16)

                def load(ch):
                    for k, src in enumerate((x_in, ctx)):
                        sp.dma_start(rows[:, ch.slot, k, :, :],
                                     src[bass.ds(ch.n * TPC, TPC)].rearrange("t p d -> p t d")).then_inc(in_s[ch.slot], 16)
                load(Tile(0, 0))
                load(Tile(0, 1))

                def chunk_step(ch):
                    after = ch.plus(2)
                    if live(after) and after.c >= 2:
                        hold(sp, t_ready, TPC * (ch.n + 1), held)
                        load(after)
                    for t in range(TPC):
                        r = Row(ch, t - 4)
                        if r.live:
                            sp.dma_start(xr[:, r.slot, :], x_in[r.n]).then_inc(xr_s[r.slot], 16)
                            hold(sp, xo_ready, r.n + 1, held)
                            sp.dma_start(x_out[r.n], xo[:, r.slot, :]).then_inc(stored[r.slot], 16)
                program(sp, chunk_step, (CHUNKS - 4) // 2)
                for s in range(2):
                    sp.wait_ge(stored[s], 16 * TILES // 2)

            @block.gpsimd
            def _(pool):
                pool.memset(half_neg[:], -0.5).then_inc(zeroed, 1)
                pool.memset(vb[:], 0.0).then_inc(zeroed, 1)
                pool.memset(kv[:], 0.0).then_inc(zeroed, 1)
                pool.wait_ge(zeroed, 3)
                for b in range(2):
                    pool.memset(vb[64 * b:64 * b + 64, :, :, b, :, HC:E], 1.0).then_inc(zeroed, 1)

                def chunk_step(ch):
                    new = ch.plus(1)
                    if live(new):
                        for t in range(TPC):
                            n = TPC * new.n + t
                            pool.wait_ge(var_ready, n + 1)
                            pool.tensor_tensor(rstd[:], var_eps[:], half_neg[:], ALU.pow).then_inc(rstd_ready, 1)
                program(pool, chunk_step)

            @block.scalar
            def _(act):
                act.wait_ge(const_in, 16 * 7)
                act.activation(w_hi[:], raw[:], ACT.Copy).then_inc(whi_ready, 1)
                act.activation(gate[:], cols[:, 4:5], ACT.Tanh).then_inc(gate_ready, 1)

                def chunk_step(ch):
                    new = ch.plus(1)
                    for t in range(TPC):
                        r = Row(ch, t - 1)
                        for half in range(2):
                            if r.live:
                                n = 2 * r.n + half
                                act.wait_ge(kv_mm, n + 1)
                                past(act, q_mm, n - 3)
                                act.activation(kv[0:F, r.slot, HALF * half:HALF * half + HALF, :, 0, :],
                                               p_kv[0:F, 0:HALF * 4 * E].rearrange("p (a b h e) -> p a b h e", a=HALF, b=2, h=2)[:, :, :, 0, :],
                                               ACT.Copy).then_inc(kv_low, 1)
                            if half == 0 and live(new) and t < 2:
                                for tt in range(2):
                                    m = 2 * t + tt
                                    act.wait_ge(t_ready, TPC * new.n + m + 1)
                                    act.activation(t_hi[:, new.slot, :, :, m * PART:(m + 1) * PART],
                                                   p_t[:].rearrange("p (x k t) -> p x k t", x=2, k=KC), ACT.Copy
                                                   ).then_inc(thi_ready, 1)
                            if half == 0 and live(new) and t == 2:
                                for m in range(4):
                                    act.wait_ge(qk_mm, 4 * new.n + m + 1)
                                    act.activation(qk_hi[:, new.slot, m, :], p_p[m % 2][:], ACT.Identity,
                                                   bias=cols[:, m:m + 1]).then_inc(qkhi_ready, 1)
                            if half == 0 and live(new) and t == 3:
                                for m in range(PAIRS):
                                    act.wait_ge(qf_mm, PAIRS * new.n + m + 1)
                                    act.activation(qf[:, new.slot, m, :], p_p[m % 2][:], ACT.Relu).then_inc(qf_ready, 1)
                        r = Row(ch, t - 3)
                        if r.live:
                            act.wait_ge(ot_mm, r.n + 1)
                            past(act, y_mm, r.n - 1)
                            act.activation(o_t[:, r.slot, :], p_y[:, 0:DIM], ACT.Copy).then_inc(ot_ready, 1)
                program(act, chunk_step)

            @block.vector
            def _(dve):
                dve.wait_ge(const_in, 16 * 7)
                dve.wait_ge(whi_ready, 1)
                dve.tensor_tensor(w_lo[:], raw[:], w_hi[:].bitcast(fp32), ALU.subtract).then_inc(wlo_ready, 1)
                dve.wait_ge(gate_ready, 1)
                dve.wait_ge(zeroed, 5)

                def normalise(ch, t):
                    n = TPC * ch.n + t
                    x = rows[:, ch.slot, 0, t, :]
                    dve.bn_stats(stats[:], x).then_inc(stat, 1)
                    hold(dve, stat, 2 * n + 1, held)
                    dve.bn_aggr(mv[:], stats[:]).then_inc(stat, 1)
                    dve.wait_ge(stat, 2 * n + 2)
                    dve.tensor_scalar_add(var_eps[:], mv[:, 1:2], EPS).then_inc(var_ready, 1)
                    dve.wait_ge(rstd_ready, n + 1)
                    past(dve, t_ready, n - 1)
                    dve.tensor_scalar(hn[:, t % 2, :], x, mv[:, 0:1], rstd[:], ALU.subtract, ALU.mult
                                      ).then_inc(hn_ready, 1)

                def chunk_step(ch):
                    new = ch.plus(1)
                    for t in range(TPC):
                        now, r1, r2, r4 = Row(ch, t), Row(ch, t - 1), Row(ch, t - 2), Row(ch, t - 4)
                        for half in range(2):
                            if now.live:
                                dve.wait_ge(kf_mm, 2 * now.n + half + 1)
                                past(dve, kv_mm, 2 * (now.n - 1))
                                dve.tensor_scalar(kf[:, now.slot, half * CHUNK:(half + 1) * CHUNK], p_k[:], 0.0,
                                                  mask[:, bass.ds(now.n, 1)], ALU.max, ALU.mult).then_inc(kf_ready, 1)
                            if r1.live:
                                n = 2 * r1.n + half
                                dve.wait_ge(kv_mm, n + 1)
                                past(dve, q_mm, n - 3)
                                dve.tensor_copy(kv[F:PART, r1.slot, HALF * half:HALF * half + HALF, :, 1, :],
                                                p_kv[F:PART, 0:HALF * 4 * E].rearrange("p (a b h e) -> p a b h e", a=HALF, b=2, h=2)[:, :, :, 1, :]
                                                ).then_inc(kv_high, 1)
                            if now.live and half == 0:
                                dve.wait_ge(v_mm, now.n + 1)
                                for b in range(2):
                                    p = slice(64 * b, 64 * b + 64)
                                    dve.tensor_tensor(vb[p, now.slot, :, b, :, 0:HC],
                                                      p_v[p, 0:DIM].rearrange("p (a h e) -> p a h e", a=PAIRS, h=2),
                                                      bv[p].rearrange("p (a h e) -> p a h e", a=PAIRS, h=2), ALU.add
                                                      ).then_inc(v_ready, 1)
                            if half == 0 and live(new) and t < 2:
                                if t == 0:
                                    dve.wait_ge(in_s[new.slot], 32 * (new.turn + 1))
                                for tt in range(2):
                                    normalise(new, 2 * t + tt)
                                for tt in range(2):
                                    m = 2 * t + tt
                                    dve.wait_ge(thi_ready, TPC * new.n + m + 1)
                                    at = slice(m * PART, (m + 1) * PART)
                                    dve.tensor_tensor(t_lo[:, new.slot, :, :, at],
                                                      p_t[:].rearrange("p (x k t) -> p x k t", x=2, k=KC),
                                                      t_hi[:, new.slot, :, :, at].bitcast(fp32), ALU.subtract
                                                      ).then_inc(tlo_ready, 1)
                            if half == 0 and live(new) and t == 2:
                                for m in range(4):
                                    dve.wait_ge(qkhi_ready, 4 * new.n + m + 1)
                                    dve.scalar_tensor_tensor(out=qk_lo[:, new.slot, m, :], in0=p_p[m % 2][:],
                                                             scalar=cols[:, m:m + 1],
                                                             in1=qk_hi[:, new.slot, m, :].bitcast(fp32),
                                                             op0=ALU.add, op1=ALU.subtract).then_inc(qklo_ready, 1)
                            if r2.live:
                                n = 2 * r2.n + half
                                dve.wait_ge(q_mm, n + 1)
                                if half == 0:
                                    past(dve, ot_mm, r2.n - 1)
                                for b in range(2):
                                    p = slice(64 * b, 64 * b + 64)
                                    src = p_q[p, 0:HALF * 4 * E].rearrange("p (a b h e) -> p a b h e", a=HALF, b=2, h=2)[:, :, b, :, :]
                                    k = 4 * n + 2 * b
                                    dve.tensor_scalar_add(den[p, b, :, :], src[:, :, :, HC], 1e-8).then_inc(den_ready, 1)
                                    dve.wait_ge(den_ready, k + 1)
                                    dve.reciprocal(rden[p, b, :, :], den[p, b, :, :]).then_inc(den_ready, 1)
                                    dve.wait_ge(den_ready, k + 2)
                                    dve.tensor_tensor(on[p, r2.slot, half * PART:(half + 1) * PART].rearrange("p (a h e) -> p a h e", a=HALF, h=2),
                                                      src[:, :, :, 0:HC],
                                                      rden[p, b, :, :].unsqueeze(3).to_broadcast([64, HALF, 2, HC]),
                                                      ALU.mult).then_inc(on_ready, 1)
                        if r4.live:
                            dve.wait_ge(y_mm, r4.n + 1)
                            past(dve, stored[r4.slot], 16 * r4.turn)
                            past(dve, xo_ready, r4.n)
                            dve.tensor_tensor(y[:], p_y[:, DIM:2 * DIM], bo[:], ALU.add).then_inc(y_ready, 1)
                            dve.wait_ge(y_ready, r4.n + 1)
                            dve.wait_ge(xr_s[r4.slot], 16 * (r4.turn + 1))
                            dve.scalar_tensor_tensor(out=xo[:, r4.slot, :], in0=y[:], scalar=gate[:],
                                                     in1=xr[:, r4.slot, :], op0=ALU.mult, op1=ALU.add).then_inc(xo_ready, 1)
                program(dve, chunk_step)

            @block.tensor
            def _(pe):
                pe.wait_ge(const_in, 16 * 7)
                pe.wait_ge(wlo_ready, 1)
                pe.wait_ge(zeroed, 5)

                def products(out, pairs):
                    todo = [xy for lh, ll, rh, rl in pairs for xy in ((lh, rh), (lh, rl), (ll, rh))]
                    for n, (x, y) in enumerate(todo):
                        mm = pe.matmul(out, x, y, start=(n == 0), stop=(n == len(todo) - 1))
                    return mm

                def chunk_step(ch):
                    new = ch.plus(1)
                    for t in range(TPC):
                        now, r1, r2, r3, r4 = (Row(ch, t - d) for d in range(5))
                        for half in range(2):
                            if now.live:
                                past(pe, kf_ready, 2 * now.n + half)
                                tok = slice(t * PART, (t + 1) * PART)
                                products(p_k[:], [(qk_hi[:, ch.slot, 2 + half, tok], qk_lo[:, ch.slot, 2 + half, tok],
                                                   w_hi[:, WFK:WFK + CHUNK], w_lo[:, WFK:WFK + CHUNK])]
                                         ).then_inc(kf_mm, 1)
                            if r1.live:
                                if half == 0:
                                    pe.wait_ge(v_ready, 2 * (r1.n + 1))
                                pe.wait_ge(kf_ready, 2 * r1.n + half + 1)
                                past(pe, kv_low, 2 * r1.n + half)
                                past(pe, kv_high, 2 * r1.n + half)
                                for a in range(HALF):
                                    pair = HALF * half + a
                                    mm = pe.matmul(p_kv[:, a * 4 * E:(a + 1) * 4 * E],
                                                   kf[:, r1.slot, pair * PART:(pair + 1) * PART],
                                                   vb[:, r1.slot, pair, :, :, :].rearrange("p b h e -> p (b h e)"),
                                                   start=True, stop=True)
                                mm.then_inc(kv_mm, 1)
                            if now.live and half == 0:
                                past(pe, v_ready, 2 * now.n)
                                tok = slice(t * PART, (t + 1) * PART)
                                products(p_v[:, 0:DIM], [(t_hi[:, ch.slot, 1, k, tok], t_lo[:, ch.slot, 1, k, tok],
                                                          w_hi[:, WV + k * DIM:WV + (k + 1) * DIM],
                                                          w_lo[:, WV + k * DIM:WV + (k + 1) * DIM])
                                                         for k in range(KC)]).then_inc(v_mm, 1)
                            if half == 0 and live(new) and t < 2:
                                for tt in range(2):
                                    m = 2 * t + tt
                                    pe.wait_ge(hn_ready, TPC * new.n + m + 1)
                                    if m == 0:
                                        pe.wait_ge(in_s[new.slot], 32 * (new.turn + 1))
                                    past(pe, tlo_ready, TPC * new.n + m)
                                    for k in range(KC):
                                        at = slice(k * PART, (k + 1) * PART)
                                        pe.transpose(p_t[:, k * PART:(k + 1) * PART], hn[:, m % 2, at], ident[:])
                                        mm = pe.transpose(p_t[:, DIM + k * PART:DIM + (k + 1) * PART],
                                                          rows[:, new.slot, 1, m, at], ident[:])
                                    mm.then_inc(t_ready, 1)
                            if half == 0 and live(new) and t == 2:
                                pe.wait_ge(tlo_ready, TPC * (new.n + 1))
                                for m in range(4):
                                    if m < 2:
                                        past(pe, qf_ready, PAIRS * new.n)
                                    else:
                                        pe.wait_ge(qklo_ready, 4 * new.n + m - 1)
                                    at = (WQ, WK)[m // 2] + (m % 2) * PART
                                    products(p_p[m % 2][:], [(w_hi[:, at + k * DIM:at + k * DIM + PART],
                                                              w_lo[:, at + k * DIM:at + k * DIM + PART],
                                                              t_hi[:, new.slot, m // 2, k, :],
                                                              t_lo[:, new.slot, m // 2, k, :]) for k in range(KC)]
                                             ).then_inc(qk_mm, 1)
                            if half == 0 and live(new) and t == 3:
                                for m in range(PAIRS):
                                    if m < 2:
                                        pe.wait_ge(qklo_ready, 4 * (new.n + 1))
                                    else:
                                        pe.wait_ge(qf_ready, PAIRS * new.n + m - 1)
                                    at = WFQ + (m % HALF) * PART
                                    products(p_p[m % 2][:], [(w_hi[:, at:at + PART], w_lo[:, at:at + PART],
                                                              qk_hi[:, new.slot, m // HALF, :],
                                                              qk_lo[:, new.slot, m // HALF, :])]).then_inc(qf_mm, 1)
                            if r2.live:
                                if half == 0 and r2.t == 0:
                                    pe.wait_ge(qf_ready, PAIRS * (r2.ch.n + 1))
                                pe.wait_ge(kv_low, 2 * r2.n + half + 1)
                                pe.wait_ge(kv_high, 2 * r2.n + half + 1)
                                past(pe, on_ready, 2 * (2 * r2.n + half))
                                for a in range(HALF):
                                    pair = HALF * half + a
                                    mm = pe.matmul(p_q[:, a * 4 * E:(a + 1) * 4 * E],
                                                   qf[:, r2.ch.slot, pair, r2.t * PART:(r2.t + 1) * PART],
                                                   kv[:, r2.slot, pair, :, :, :].rearrange("p b h e -> p (b h e)"),
                                                   start=True, stop=True)
                                mm.then_inc(q_mm, 1)
                        if r3.live:
                            pe.wait_ge(on_ready, 4 * (r3.n + 1))
                            past(pe, ot_ready, r3.n)
                            past(pe, y_ready, r3.n - 1)
                            for k in range(KC):
                                mm = pe.transpose(p_y[:, k * PART:(k + 1) * PART],
                                                  on[:, r3.slot, k * PART:(k + 1) * PART], ident[:])
                            mm.then_inc(ot_mm, 1)
                        if r4.live:
                            pe.wait_ge(ot_ready, r4.n + 1)
                            past(pe, y_ready, r4.n)
                            if r3.live:
                                pe.wait_ge(ot_ready, r3.n + 1)
                            for k in range(KC):
                                mm = pe.matmul(p_y[:, DIM:2 * DIM], o_t[:, r4.slot, k * PART:(k + 1) * PART],
                                               w_out[:, k, :], start=(k == 0), stop=(k == KC - 1))
                            mm.then_inc(y_mm, 1)
                program(pe, chunk_step)


def _layout_linear_attention(a):
    f = np.float32
    wq, wk, wv, wo = (np.asarray(a[f"L1_xattn_W{n}"]) for n in "qkvo")
    bq, bk, bv, bo = (np.asarray(a[f"L1_xattn_b{n}"]) for n in "qkvo")
    block = lambda w: w.reshape(2, PART, -1).transpose(1, 0, 2).reshape(PART, -1)
    feats = []
    for n in ("L1_xattn_Wqf", "L1_xattn_Wkf"):
        m = np.zeros((PART, 512), f)
        for h in range(8):
            m[16 * h:16 * h + 16, 64 * h:64 * h + 64] = np.asarray(a[n]).T
        feats.append(m)
    cols = np.zeros((PART, 8), f)
    for n, b in enumerate((bq[:128], bq[128:], bk[:128], bk[128:])):
        cols[:, n] = b
    cols[:, 4] = np.asarray(a["g_xattn"])[1]
    mask = np.ascontiguousarray(np.asarray(a["mask_BxS2_ff1"]).reshape(TILES, PART).T)
    return {"la_w": np.ascontiguousarray(np.concatenate([block(wq.T), block(wk.T), block(wv.T)] + feats, 1)),
            "la_w_out": np.ascontiguousarray(wo.T.reshape(2, PART, DIM).transpose(1, 0, 2)),
            "la_cols": cols, "la_mask": mask, "la_bv": np.tile(bv, (PART, 1)), "la_bo": np.tile(bo, (PART, 1)),
            "ident": np.eye(PART, dtype=f)}


QHEADS, KVHEADS, HD, RQ = 32, 8, 64, 4


def stage_causal_attention(nc, x_in, z_out, c):
    KC, PAIRS, GROUPS, TPC = 2, 4, 8, CHUNK // PART
    PIECE = 1024
    WQ, WK, WV, WO, WEND = 0, 4096, 5120, 6144, 10240
    PIECES = WEND // PIECE
    st = ExitStack()
    sb = lambda n, s, d=fp32: st.enter_context(nc.sbuf_tensor(f"ca_{n}", s, d))
    sem = lambda n: nc.alloc_semaphore(f"ca_{n}")
    with st:
        w_hi, w_lo = (sb(n, [PART, WEND], fp32r) for n in ("w_hi", "w_lo"))
        ident, swap = sb("ident", [PART, PART]), sb("swap", [PART, PART])
        mask = sb("mask", [PART, PART])
        cos_q, sin_q, cos_k, sin_k = (sb(n, [PART, SEQ]) for n in ("cos_q", "sin_q", "cos_k", "sin_k"))
        norm_w, half_neg = sb("norm_w", [PART, DIM]), sb("half_neg", [PART, 1])
        z = sb("z", [PART, 2, TPC, DIM])
        stats, mv = sb("stats", [PART, 6]), sb("mv", [PART, 2])
        var_eps, rstd = sb("var_eps", [PART, 1]), sb("rstd", [PART, 1])
        hn = sb("hn", [PART, TPC, DIM])
        ht_hi, ht_lo = (sb(n, [PART, 2, KC, CHUNK], fp32r) for n in ("ht_hi", "ht_lo"))
        q_f, by_cos, by_sin = sb("q_f", [PART, 2, CHUNK]), sb("by_cos", [PART, 2, CHUNK]), sb("by_sin", [PART, 2, CHUNK])
        qk = sb("qk", [PART, 2, RQ + 1, CHUNK])
        raw = [qk[:, n, 0:2, :].rearrange("p m t -> p (m t)") for n in range(2)]
        v = sb("v", [PART, 2, TPC, KVHEADS * HD])
        sm, neg_top = sb("sm", [PART, 2, CHUNK]), sb("neg_top", [PART, 2, RQ])
        prob, sums, rsum = sb("prob", [PART, 2, CHUNK]), sb("sums", [PART, 2, RQ]), sb("rsum", [PART, 2, RQ])
        pn, pt = sb("pn", [PART, 2, CHUNK]), sb("pt", [PART, 2, CHUNK])
        ot_hi, ot_lo = (sb(n, [PART, 2, RQ, CHUNK], fp32r) for n in ("ot_hi", "ot_lo"))
        y_t = hn[:].rearrange("p (k t) d -> p k (t d)", k=KC)
        bank = lambda n: st.enter_context(nc.psum_tensor(f"ca_{n}", [PART, CHUNK], fp32))
        p_p, p_r, p_t, p_o = bank("pp"), bank("pr"), bank("p_t"), bank("po")
        p_s, p_y = [bank(f"ps{i}") for i in range(2)], [bank(f"py{i}") for i in range(2)]

        const_in, zeroed = sem("const_in"), sem("zeroed")
        raw_in = [sem(f"raw{i}") for i in range(2)]
        whi_ready, wlo_ready = sem("whi"), sem("wlo")
        x_loaded = [sem(f"x{i}") for i in range(2)]
        stat, var_ready, rstd_ready, z_ready, hn_ready = sem("stat"), sem("var"), sem("rstd"), sem("z"), sem("hn")
        t_ready, hthi_ready, htlo_ready = sem("t"), sem("hthi"), sem("htlo")
        pp_ready, qf_ready, cos_done, rot_ready, sin_done = sem("pp"), sem("qf"), sem("cos"), sem("rot"), sem("sin")
        qk_ready, v_mm, v_ready = sem("qk"), sem("v_mm"), sem("v")
        s_ready, sm_ready, top_ready, prob_ready = sem("s"), sem("sm"), sem("top"), sem("prob")
        rsum_ready, pn_ready, pt_mm, pt_even, pt_odd = sem("rsum"), sem("pn"), sem("pt_mm"), sem("pt_e"), sem("pt_o")
        pv_ready, othi_ready, otlo_ready = sem("pv"), sem("othi"), sem("otlo")
        y_ready, yt_ready, back_ready, zn_ready = sem("y"), sem("yt"), sem("back"), sem("zn")
        held = sem("held")
        stored = [sem(f"stored{i}") for i in range(2)]

        def live(ch):
            return not isinstance(ch.k, int) or 0 <= ch.n < CHUNKS

        def program(eng, chunk_step):
            chunk_step(Tile(0, -1))
            chunk_step(Tile(0, 0))
            with eng.Fori(0, (CHUNKS - 2) // 2) as k:
                chunk_step(Tile(k, 1))
                chunk_step(Tile(k, 2))
            chunk_step(Tile(0, CHUNKS - 1))
            chunk_step(Tile(0, CHUNKS))

        class Unit:
            def __init__(self, ch, kp):
                self.ch, self.kp = ch.plus(kp // PAIRS), kp % PAIRS
                self.live = live(self.ch)
                self.n = PAIRS * self.ch.n + self.kp
                self.slot = self.kp % 2

        def group(ch, kp, g):
            u = Unit(ch, kp + g // GROUPS)
            return u, g % GROUPS, GROUPS * u.n + g % GROUPS

        with nc.Block() as block:
            @block.sync
            def _(sp):
                for dst, name in ((ident, "ident"), (swap, "ca_swap"), (mask, "ca_mask"), (cos_q, "ca_cos_q"),
                                  (sin_q, "ca_sin_q"), (cos_k, "ca_cos_k"), (sin_k, "ca_sin_k"),
                                  (norm_w, "ca_norm_w")):
                    sp.dma_start(dst[:], c[name]).then_inc(const_in, 16)

                def load_x(ch):
                    sp.dma_start(z[:, ch.slot, :, :], x_in[bass.ds(ch.n * TPC, TPC)].rearrange("t p d -> p t d")
                                 ).then_inc(x_loaded[ch.slot], 16)
                load_x(Tile(0, 0))
                for n in range(PIECES):
                    hold(sp, whi_ready, n - 1, held)
                    hold(sp, wlo_ready, n - 1, held)
                    sp.dma_start(raw[n % 2], c["ca_w"][:, n * PIECE:(n + 1) * PIECE]).then_inc(raw_in[n % 2], 16)

                def chunk_step(ch):
                    old, new = ch.plus(-1), ch.plus(1)
                    if live(old):
                        for h in range(2):
                            hold(sp, zn_ready, 2 * old.n + h + 1, held)
                            sp.dma_start(z_out[bass.ds(old.n * TPC + 2 * h, 2)].rearrange("t p d -> p t d"),
                                         z[:, old.slot, 2 * h:2 * h + 2, :]).then_inc(stored[h], 16)
                    if live(new) and not (isinstance(ch.k, int) and ch.n < 0):
                        for h in range(2):
                            hold(sp, stored[h], 16 * ch.n, held)
                        load_x(new)
                program(sp, chunk_step)
                for h in range(2):
                    sp.wait_ge(stored[h], 16 * CHUNKS)

            @block.gpsimd
            def _(pool):
                pool.memset(half_neg[:], -0.5).then_inc(zeroed, 1)
                pool.wait_ge(zeroed, 1)

                def chunk_step(ch):
                    for kp in range(PAIRS):
                        nxt = Unit(ch, kp + 1)
                        for g in range(GROUPS):
                            if kp == 2 and g < TPC and live(ch.plus(1)):
                                n = 2 * (TPC * ch.plus(1).n + g)
                                for k in range(2):
                                    pool.wait_ge(var_ready, n + k + 1)
                                    pool.tensor_tensor(rstd[:], var_eps[:], half_neg[:], ALU.pow).then_inc(rstd_ready, 1)
                            if nxt.live and 1 <= g <= RQ + 1:
                                m = g - 1
                                n = (RQ + 1) * nxt.n + m
                                s = (nxt.kp + m) % 2
                                pool.wait_ge(cos_done, n + 1)
                                pool.wait_ge(sin_done, n + 1)
                                if m == 0:
                                    past(pool, s_ready, GROUPS * (nxt.n - 1))
                                pool.tensor_tensor(qk[:, nxt.slot, m, :], by_cos[:, s, :], by_sin[:, s, :], ALU.add
                                                   ).then_inc(qk_ready, 1)
                            u, gg, n = group(ch, kp, g - 1)
                            if u.live:
                                pool.wait_ge(rsum_ready, n + 1)
                                past(pool, pt_mm, n - 1)
                                pool.tensor_tensor(pn[:, gg % 2, :].rearrange("p (r k) -> p r k", r=RQ),
                                                   prob[:, gg % 2, :].rearrange("p (r k) -> p r k", r=RQ),
                                                   rsum[:, gg % 2, :].unsqueeze(2).to_broadcast([PART, RQ, PART]),
                                                   ALU.mult).then_inc(pn_ready, 1)
                program(pool, chunk_step)

            @block.scalar
            def _(act):
                for n in range(PIECES):
                    act.wait_ge(raw_in[n % 2], 16 * (n // 2 + 1))
                    act.activation(w_hi[:, n * PIECE:(n + 1) * PIECE], raw[n % 2], ACT.Copy).then_inc(whi_ready, 1)

                def chunk_step(ch):
                    for kp in range(PAIRS):
                        nxt = Unit(ch, kp + 1)
                        for g in range(GROUPS):
                            if nxt.live and g <= RQ:
                                n = (RQ + 1) * nxt.n + g
                                act.wait_ge(pp_ready, n + 1)
                                past(act, rot_ready, n - 1)
                                past(act, cos_done, n - 1)
                                act.activation(q_f[:, (nxt.kp + g) % 2, :], p_p[:], ACT.Copy).then_inc(qf_ready, 1)
                            if kp == 3 and g >= 4 and live(ch.plus(1)):
                                n = TPC * ch.plus(1).n + g - 4
                                act.wait_ge(v_mm, n + 1)
                                act.activation(v[:, ch.plus(1).slot, g - 4, :], p_p[:], ACT.Copy).then_inc(v_ready, 1)
                            if kp == 2 and g >= 6 and live(ch.plus(1)):
                                h = g - 6
                                act.wait_ge(t_ready, 2 * ch.plus(1).n + h + 1)
                                act.activation(ht_hi[:, ch.plus(1).slot, :, 2 * h * PART:(2 * h + 2) * PART],
                                               p_r[:].rearrange("p (k t) -> p k t", k=KC), ACT.Copy
                                               ).then_inc(hthi_ready, 1)
                            u, gg, n = group(ch, kp, g - 3)
                            if u.live and gg % 2 == 0:
                                act.wait_ge(pt_mm, n + 1)
                                past(act, pv_ready, n - 1)
                                act.activation(pt[:, 0, :], p_t[:], ACT.Copy).then_inc(pt_even, 1)
                            u, gg, n = group(ch, kp, g - 4)
                            if u.live and gg % 2 == 1:
                                t = gg // 2
                                act.wait_ge(pv_ready, n + 1)
                                if t == 0:
                                    past(act, y_ready, u.n - 1)
                                act.activation(ot_hi[:, u.slot, :, t * PART:(t + 1) * PART],
                                               p_o[:].rearrange("p (r t) -> p r t", r=RQ), ACT.Copy
                                               ).then_inc(othi_ready, 1)
                            if kp == 0 and g == 6 and live(ch.plus(-1)):
                                act.wait_ge(y_ready, PAIRS * ch.n)
                                past(act, back_ready, 2 * ch.plus(-1).n)
                                for k in range(KC):
                                    act.activation(y_t[:, k, :], p_y[k][:], ACT.Copy).then_inc(yt_ready, 1)
                            u, gg, n = group(ch, kp, g)
                            if u.live:
                                s = gg % 2
                                act.wait_ge(top_ready, n + 1)
                                past(act, pn_ready, n - 1)
                                past(act, rsum_ready, n - 1)
                                for r in range(RQ):
                                    act.activation(prob[:, s, r * PART:(r + 1) * PART], sm[:, s, r * PART:(r + 1) * PART],
                                                   ACT.Exp, bias=neg_top[:, s, r:r + 1],
                                                   accum_out=sums[:, s, r:r + 1]).then_inc(prob_ready, 1)
                program(act, chunk_step)

            @block.vector
            def _(dve):
                dve.wait_ge(const_in, 16 * 8)
                for n in range(PIECES):
                    dve.wait_ge(whi_ready, n + 1)
                    at = slice(n * PIECE, (n + 1) * PIECE)
                    dve.tensor_tensor(w_lo[:, at], raw[n % 2], w_hi[:, at].bitcast(fp32), ALU.subtract
                                      ).then_inc(wlo_ready, 1)

                def normalise(ch, t):
                    n = TPC * ch.n + t
                    if t == 0:
                        dve.wait_ge(x_loaded[ch.slot], 16 * (ch.turn + 1))
                    rows = z[:, ch.slot, t, :]
                    for k in range(2):
                        if k == 1:
                            dve.wait_ge(z_ready, n + 1)
                        dve.bn_stats(stats[:], rows).then_inc(stat, 1)
                        hold(dve, stat, 5 * n + 2 * k + 1, held)
                        dve.bn_aggr(mv[:], stats[:]).then_inc(stat, 1)
                        dve.wait_ge(stat, 5 * n + 2 * k + 2)
                        if k == 1:
                            dve.scalar_tensor_tensor(out=mv[:, 1:2], in0=mv[:, 0:1], scalar=mv[:, 0:1],
                                                     in1=mv[:, 1:2], op0=ALU.mult, op1=ALU.add).then_inc(stat, 1)
                            dve.wait_ge(stat, 5 * n + 5)
                        dve.tensor_scalar_add(var_eps[:], mv[:, 1:2], EPS).then_inc(var_ready, 1)
                        dve.wait_ge(rstd_ready, 2 * n + k + 1)
                        if k == 0:
                            dve.tensor_scalar(rows, rows, mv[:, 0:1], rstd[:], ALU.subtract, ALU.mult
                                              ).then_inc(z_ready, 1)
                        else:
                            if t == 0:
                                past(dve, t_ready, 2 * ch.n)
                            dve.scalar_tensor_tensor(out=hn[:, t, :], in0=rows, scalar=rstd[:], in1=norm_w[:],
                                                     op0=ALU.mult, op1=ALU.mult).then_inc(hn_ready, 1)

                def rope(u, m, which):
                    src, tab, out, done = ((q_f[:, (u.kp + m) % 2, :], (cos_q, cos_k), by_cos, cos_done),
                                           (p_r[:], (sin_q, sin_k), by_sin, sin_done))[which]
                    n = (RQ + 1) * u.n + m
                    past(dve, qk_ready, n - 1)
                    dve.tensor_tensor(out[:, (u.kp + m) % 2, :].rearrange("p (b s) -> p b s", s=SEQ),
                                      src.rearrange("p (b s) -> p b s", s=SEQ),
                                      tab[int(m == RQ)][:].unsqueeze(1).to_broadcast([PART, CHUNK // SEQ, SEQ]),
                                      ALU.mult).then_inc(done, 1)

                def chunk_step(ch):
                    for kp in range(PAIRS):
                        nxt = Unit(ch, kp + 1)
                        for g in range(GROUPS):
                            if nxt.live and g <= RQ:
                                n = (RQ + 1) * nxt.n + g
                                dve.wait_ge(qf_ready, n + 1)
                                rope(nxt, g, 0)
                            u, gg, n = group(ch, kp, g)
                            if u.live:
                                s = gg % 2
                                dve.wait_ge(s_ready, n + 1)
                                past(dve, prob_ready, RQ * (n - 1))
                                dve.tensor_tensor(sm[:, s, :].rearrange("p (r k) -> p r k", r=RQ),
                                                  p_s[s][:].rearrange("p (r k) -> p r k", r=RQ),
                                                  mask[:].unsqueeze(1).to_broadcast([PART, RQ, PART]), ALU.add
                                                  ).then_inc(sm_ready, 1)
                                dve.wait_ge(sm_ready, n + 1)
                                dve.tensor_reduce(neg_top[:, s, :], sm[:, s, :].rearrange("p (r k) -> p r k", r=RQ),
                                                  AX, ALU.max, negate=True).then_inc(top_ready, 1)
                            u, gg, n = group(ch, kp, g - 1)
                            if u.live:
                                s = gg % 2
                                dve.wait_ge(prob_ready, RQ * (n + 1))
                                past(dve, pn_ready, n - 1)
                                dve.reciprocal(rsum[:, s, :], sums[:, s, :]).then_inc(rsum_ready, 1)
                            if nxt.live and 1 <= g <= RQ + 1:
                                n = (RQ + 1) * nxt.n + g - 1
                                dve.wait_ge(rot_ready, n + 1)
                                rope(nxt, g - 1, 1)
                            if kp == 2 and g < TPC and live(ch.plus(1)):
                                normalise(ch.plus(1), g)
                            if kp == 2 and g >= 6 and live(ch.plus(1)):
                                h = g - 6
                                dve.wait_ge(hthi_ready, 2 * ch.plus(1).n + h + 1)
                                at = slice(2 * h * PART, (2 * h + 2) * PART)
                                dve.tensor_tensor(ht_lo[:, ch.plus(1).slot, :, at],
                                                  p_r[:].rearrange("p (k t) -> p k t", k=KC),
                                                  ht_hi[:, ch.plus(1).slot, :, at].bitcast(fp32), ALU.subtract
                                                  ).then_inc(htlo_ready, 1)
                            u, gg, n = group(ch, kp, g - 3)
                            if u.live and gg % 2 == 1:
                                dve.wait_ge(pt_mm, n + 1)
                                past(dve, pv_ready, n - 1)
                                dve.tensor_copy(pt[:, 1, :], p_t[:]).then_inc(pt_odd, 1)
                            u, gg, n = group(ch, kp, g - 4)
                            if u.live and gg % 2 == 1:
                                t = gg // 2
                                dve.wait_ge(othi_ready, TPC * u.n + t + 1)
                                at = slice(t * PART, (t + 1) * PART)
                                dve.tensor_tensor(ot_lo[:, u.slot, :, at], p_o[:].rearrange("p (r t) -> p r t", r=RQ),
                                                  ot_hi[:, u.slot, :, at].bitcast(fp32), ALU.subtract
                                                  ).then_inc(otlo_ready, 1)
                            if (kp, g) in ((0, 7), (1, 6)) and live(ch.plus(-1)):
                                h, old = kp, ch.plus(-1)
                                dve.wait_ge(back_ready, 2 * old.n + h + 1)
                                dve.tensor_tensor(z[:, old.slot, 2 * h:2 * h + 2, :], p_r[:].rearrange("p (t d) -> p t d", t=2),
                                                  z[:, old.slot, 2 * h:2 * h + 2, :], ALU.add).then_inc(zn_ready, 1)
                program(dve, chunk_step)

            @block.tensor
            def _(pe):
                pe.wait_ge(const_in, 16 * 8)

                def products(out, pairs, start=True, stop=True):
                    todo = [xy for lh, ll, rh, rl in pairs for xy in ((lh, rh), (lh, rl), (ll, rh))]
                    for n, (x, y) in enumerate(todo):
                        mm = pe.matmul(out, x, y, start=start and n == 0, stop=stop and n == len(todo) - 1)
                    return mm

                def project(u, m):
                    n = (RQ + 1) * u.n + m
                    if n == 0 if isinstance(n, int) else False:
                        pe.wait_ge(wlo_ready, PIECES)
                    if m == 0 and u.kp == 0:
                        pe.wait_ge(htlo_ready, 2 * (u.ch.n + 1))
                    past(pe, qf_ready, n)
                    if m == 0 and u.kp == 1:
                        pe.wait_ge(v_ready, TPC * (u.ch.n + 1))
                    width = QHEADS * HD if m < RQ else KVHEADS * HD
                    at = WQ + (RQ * u.kp + m) * PART if m < RQ else WK + u.kp * PART
                    products(p_p[:], [(w_hi[:, at + k * width:at + k * width + PART],
                                       w_lo[:, at + k * width:at + k * width + PART],
                                       ht_hi[:, u.ch.slot, k, :], ht_lo[:, u.ch.slot, k, :])
                                      for k in range(KC)]).then_inc(pp_ready, 1)

                def chunk_step(ch):
                    new, old = ch.plus(1), ch.plus(-1)
                    for kp in range(PAIRS):
                        nxt = Unit(ch, kp + 1)
                        for g in range(GROUPS):
                            if nxt.live and g <= RQ:
                                project(nxt, g)
                            if kp == 3 and g >= 4 and live(new):
                                t = g - 4
                                if t == 0:
                                    pe.wait_ge(qf_ready, (RQ + 1) * (nxt.n + 1))
                                else:
                                    pe.wait_ge(v_ready, TPC * new.n + t)
                                tok = slice(t * PART, (t + 1) * PART)
                                products(p_p[:], [(ht_hi[:, new.slot, k, tok], ht_lo[:, new.slot, k, tok],
                                                   w_hi[:, WV + k * CHUNK:WV + (k + 1) * CHUNK],
                                                   w_lo[:, WV + k * CHUNK:WV + (k + 1) * CHUNK])
                                                  for k in range(KC)]).then_inc(v_mm, 1)
                            u, gg, n = group(ch, kp, g)
                            if u.live:
                                t, s = gg // 2, gg % 2
                                if gg == 0:
                                    pe.wait_ge(qk_ready, (RQ + 1) * (u.n + 1))
                                past(pe, sm_ready, n - 1)
                                half, tok = slice(HD * s, HD * s + HD), slice(t * PART, (t + 1) * PART)
                                for r in range(RQ):
                                    mm = pe.matmul(p_s[s][:, r * PART:(r + 1) * PART], qk[half, u.slot, r, tok],
                                                   qk[half, u.slot, RQ, tok], start=True, stop=True)
                                mm.then_inc(s_ready, 1)
                            if nxt.live and 1 <= g <= RQ + 1:
                                n = (RQ + 1) * nxt.n + g - 1
                                pe.wait_ge(qf_ready, n + 1)
                                past(pe, sin_done, n)
                                if g == 1:
                                    if kp == 3:
                                        pe.wait_ge(htlo_ready, 2 * (new.n + 1))
                                    if kp == 1 and live(old):
                                        pe.wait_ge(zn_ready, 2 * old.n + 1)
                                    if kp == 2 and live(old):
                                        pe.wait_ge(zn_ready, 2 * old.n + 2)
                                pe.matmul(p_r[:], swap[:], q_f[:, (nxt.kp + g - 1) % 2, :], start=True, stop=True
                                          ).then_inc(rot_ready, 1)
                            if kp == 2 and g >= 6 and live(new):
                                h = g - 6
                                pe.wait_ge(hn_ready, TPC * (new.n + 1))
                                if nxt.live:
                                    pe.wait_ge(sin_done, (RQ + 1) * (nxt.n + 1))
                                if h == 1:
                                    pe.wait_ge(htlo_ready, 2 * new.n + 1)
                                for t in range(2):
                                    for k in range(KC):
                                        mm = pe.transpose(p_r[:, k * DIM + t * PART:k * DIM + (t + 1) * PART],
                                                          hn[:, 2 * h + t, k * PART:(k + 1) * PART], ident[:])
                                mm.then_inc(t_ready, 1)
                            u, gg, n = group(ch, kp, g - 3)
                            if u.live:
                                pe.wait_ge(pn_ready, n + 1)
                                if gg % 2 == 1:
                                    pe.wait_ge(pt_even, 4 * u.n + gg // 2 + 1)
                                else:
                                    past(pe, pt_odd, 4 * u.n + gg // 2)
                                for r in range(RQ):
                                    mm = pe.transpose(p_t[:, r * PART:(r + 1) * PART],
                                                      pn[:, gg % 2, r * PART:(r + 1) * PART], ident[:])
                                mm.then_inc(pt_mm, 1)
                            u, gg, n = group(ch, kp, g - 4)
                            if u.live:
                                t, s = gg // 2, gg % 2
                                pe.wait_ge(pt_odd if s else pt_even, 4 * u.n + t + 1)
                                if s == 0:
                                    past(pe, otlo_ready, TPC * u.n + t)
                                at = (2 * u.kp + s) * HD
                                pe.matmul(p_o[HD * s:HD * s + HD, :], v[:, u.ch.slot, t, at:at + HD], pt[:, s, :],
                                          start=True, stop=True, tile_position=(0, HD * s)).then_inc(pv_ready, 1)
                            u = Unit(ch, kp - 1)
                            if g == 5 and u.live:
                                pe.wait_ge(otlo_ready, TPC * (u.n + 1))
                                if u.kp == 0:
                                    past(pe, yt_ready, KC * u.ch.n)
                                for dh in range(KC):
                                    blocks = []
                                    for r in range(RQ):
                                        at = WO + (RQ * u.kp + r) * DIM + dh * PART
                                        blocks.append((w_hi[:, at:at + PART], w_lo[:, at:at + PART],
                                                       ot_hi[:, u.slot, r, :], ot_lo[:, u.slot, r, :]))
                                    mm = products(p_y[dh][:], blocks, start=(u.kp == 0), stop=(u.kp == PAIRS - 1))
                                mm.then_inc(y_ready, 1)
                            if (kp, g) in ((0, 7), (1, 6)) and live(old):
                                h = kp
                                pe.wait_ge(yt_ready, KC * (old.n + 1))
                                if nxt.live:
                                    pe.wait_ge(sin_done, (RQ + 1) * (nxt.n + 1))
                                if h == 1:
                                    pe.wait_ge(zn_ready, 2 * old.n + 1)
                                for t in range(2):
                                    for dh in range(KC):
                                        mm = pe.transpose(p_r[:, t * DIM + dh * PART:t * DIM + (dh + 1) * PART],
                                                          y_t[:, dh, (2 * h + t) * PART:(2 * h + t + 1) * PART], ident[:])
                                mm.then_inc(back_ready, 1)
                program(pe, chunk_step)


def _layout_causal_attention(a):
    f = np.float32
    half = HD // 2
    inv = f(1.0) / f(150000.0) ** (np.arange(half, dtype=f) / f(half))
    ang = (np.arange(SEQ, dtype=f)[:, None] * inv).T
    cos = np.tile(np.cos(ang).astype(f), (4, 1))
    sin = np.tile(np.concatenate([-np.sin(ang), np.sin(ang)]).astype(f), (2, 1))
    scale = f(1 / np.sqrt(HD))
    swap = np.zeros((PART, PART), f)
    for p in range(PART):
        swap[p, p ^ half] = 1
    mask = np.full((PART, PART), -1e30, f)
    for b in range(2):
        mask[64 * b:64 * b + 64, 64 * b:64 * b + 64] = np.where(np.tril(np.ones((64, 64), bool)), 0, -1e30)
    wq, wk, wv, wo = (np.asarray(a[f"L1_ffn_w{n}"]) for n in "qkvo")
    block = lambda w: w.reshape(2, PART, -1).transpose(1, 0, 2).reshape(PART, -1)
    wq = wq.reshape(DIM, 4, 2, RQ, HD).transpose(0, 1, 3, 2, 4).reshape(DIM, -1)
    wo = wo.reshape(4, 2, RQ, HD, DIM).transpose(0, 2, 1, 3, 4).reshape(16, PART, DIM).transpose(1, 0, 2)
    w = np.concatenate([block(wq), block(wk), block(wv), wo.reshape(PART, -1)], 1)
    return {"ca_w": np.ascontiguousarray(w), "ca_swap": swap, "ca_mask": mask, "ca_cos_q": cos * scale,
            "ca_sin_q": sin * scale, "ca_cos_k": cos, "ca_sin_k": sin,
            "ca_norm_w": np.tile(np.asarray(a["L1_ffn_ln_w"]), (PART, 1)), "ident": np.eye(PART, dtype=f)}


_WEIGHTS = ["L0_ffn_gate_proj", "L0_ffn_up_proj", "L0_ffn_down_proj", "L1_ffn_w1", "L1_ffn_w3", "L1_ffn_w2"]


def build(nc, a, out, scratch):
    with nc.cleanup_on_exit():
        stage_softmax_attention(nc, a["x"], scratch[0], a["ctx"], a)
    with nc.cleanup_on_exit():
        stage_experts(nc, "moe0", scratch[0], scratch[1], a["L0_ffn_gate_proj"], a["L0_ffn_up_proj"],
                      a["L0_ffn_down_proj"], a, 8, 128, 2, "layer")
    with nc.cleanup_on_exit():
        stage_linear_attention(nc, scratch[1], scratch[2], a["ctx"], a)
    with nc.cleanup_on_exit():
        stage_causal_attention(nc, scratch[2], scratch[3], a)
    with nc.cleanup_on_exit():
        stage_experts(nc, "moe1", scratch[3], out, a["L1_ffn_w1"], a["L1_ffn_w3"], a["L1_ffn_w2"],
                      a, 16, 256, 4, "rms", skip=scratch[2])


def kernel(**inputs):
    import concourse.bacc as _bacc
    from concourse.bass_utils import run_bass_kernel_spmd as _run

    nc = _bacc.Bacc("TRN2", target_bir_lowering=False, num_devices=1)
    tiles = (TILES, PART, DIM)
    host = {"x": np.asarray(inputs["x"]).reshape(tiles), "ctx": np.asarray(inputs["ctx_2048"]).reshape(tiles)}
    for n in _WEIGHTS:
        host[n] = np.asarray(inputs[n])
    host.update(_tables())
    for lay in (_layout_softmax_attention, _layout_experts, _layout_linear_attention, _layout_causal_attention):
        host.update(lay(inputs))
    arrays, a = {}, {}
    for n, v in host.items():
        arrays[f"in_{n}"] = np.ascontiguousarray(v)
        a[n] = nc.dram_tensor(f"in_{n}", v.shape, fp32, kind="ExternalInput").ap()
    out = nc.dram_tensor("out_0", tiles, fp32, kind="ExternalOutput").ap()
    scratch = [nc.dram_tensor(f"scratch_{i}", tiles, fp32, kind="Internal").ap() for i in range(4)]
    build(nc, a, out, scratch)
    r = _run(nc, [arrays], core_ids=[0])
    return r.results[0]["out_0"].reshape(BATCH, SEQ, DIM)
```

```python
from contextlib import ExitStack

import numpy as np
import concourse.bass as bass
from concourse import mybir

fp32 = mybir.dt.float32
fp32r = mybir.dt.float32r
ALU = mybir.AluOpType
ACT = mybir.ActivationFunctionType
AX = mybir.AxisListType.X

BATCH, SEQ, DIM = 64, 64, 256
ROWS = BATCH * SEQ
PART = 128
TILES = ROWS // PART
EPS = 1e-5


class Tile:

    def __init__(self, k, c):
        self.k, self.c = k, c
        self.n = 2 * k + c
        self.slot = c % 2
        self.turn = k + c // 2
        self.live = not isinstance(k, int) or 0 <= self.n < TILES

    def plus(self, d):
        return Tile(self.k, self.c + d)


def past(eng, sem, count):
    if not (isinstance(count, int) and count <= 0):
        eng.wait_ge(sem, count)


def hold(eng, sem, count, held):
    if not (isinstance(count, int) and count <= 0):
        eng.wait_ge(sem, count)
        if not isinstance(count, int):
            eng.sem_inc(held, 1)


def stage_softmax_attention(nc, x_in, x_out, ctx, c):
    HEADS, GROUPS, KC, T, HALF = 16, 4, 8, 256, 2
    SPLIT = 3 * KC
    st = ExitStack()
    sb = lambda n, s, d=fp32: st.enter_context(nc.sbuf_tensor("soft_" + n, s, d))
    sem = lambda n: nc.alloc_semaphore("soft_" + n)
    with st:
        w_in = sb("w_in", [PART, 5, PART])
        w_out = sb("w_out", [PART, GROUPS, PART])
        spread = sb("spread", [PART, PART])
        cos_t, sin_t = sb("cos", [PART, 2 * T]), sb("sin", [PART, 2 * T])
        cols = sb("cols", [PART, 8])
        bv = sb("bv", [PART, 2 * PART])
        sel_f = sb("sel_f", [PART, 17, PART])
        sel = sb("sel", [PART, 17, PART], fp32r)
        gate = sb("gate", [PART, 1])
        half_neg = sb("half_neg", [PART, 1])
        xt, ct = sb("xt", [PART, 2, T]), sb("ct", [PART, 2, T])
        xr = sb("xr", [PART, 2, T])
        xn = sb("xn", [PART, 2, T])
        stats, mv = sb("stats", [PART, 6]), sb("mv", [PART, 2])
        var_eps, rstd = sb("var_eps", [PART, 1]), sb("rstd", [PART, 1])
        by_cos, by_sin = sb("by_cos", [PART, 2 * T]), sb("by_sin", [PART, 2 * T])
        roped = sb("roped", [PART, 2 * T])
        hi, lo = sb("hi", [PART, 2, 2 * T], fp32r), sb("lo", [PART, 2, 2 * T], fp32r)
        rep = sb("rep", [PART, 2, GROUPS, 2 * T], fp32r)
        qm = sb("qm", [PART, GROUPS, T], fp32r)
        top = sb("top", [PART, 2, GROUPS, HALF, PART], fp32r)
        vaug = sb("vaug", [PART, 2, HALF, HEADS, 32])
        prob = sb("prob", [PART, 4, 2 * T])
        o_raw = sb("o_raw", [PART, 2, GROUPS, T])
        den = sb("den", [PART, 32])
        rden = sb("rden", [PART, 32])
        rrow = sb("rrow", [PART, GROUPS, T])
        on = sb("on", [PART, GROUPS, T])
        y, xo = sb("y", [PART, T]), sb("xo", [PART, 2, T])
        ps = lambda n: st.enter_context(nc.psum_tensor("soft_" + n, [PART, 2 * T], fp32))
        p_a, p_b, p_o, p_x = ([ps(f"{n}{i}") for i in range(2)] for n in ("pa", "pb", "po", "px"))

        const_in, zeroed = sem("const_in"), sem("zeroed")
        sel_ready, gate_ready = sem("sel_ready"), sem("gate_ready")
        x_in_s, c_in_s, xr_in_s = ([sem(f"{n}{i}") for i in range(2)] for n in ("x", "c", "xr"))
        stats_ready, var_ready, rstd_ready, xn_ready = sem("stats"), sem("var"), sem("rstd"), sem("xn")
        qk_ready, qkrot_ready, v_ready = sem("qk"), sem("qkrot"), sem("v")
        cos_done, sin_done, roped_ready = sem("cosd"), sem("sind"), sem("roped")
        hi_ready, lo_ready, vaug_ready = sem("hi"), sem("lo"), sem("vaug")
        rep_ready, rep_out = sem("rep"), sem("rep_out")
        a_ready, a_done = sem("a"), sem("a_done")
        m_ready, qm_ready = sem("m"), sem("qm")
        b_ready, prob_ready, pv_done, o_out = sem("b"), sem("prob"), sem("pv"), sem("o_out")
        den_in, rden_ready, rrow_in = sem("den_in"), sem("rden"), sem("rrow_in")
        spread_ready, on_ready, wo_ready = sem("spread"), sem("on"), sem("wo")
        y_ready, xo_ready = sem("y"), sem("xo")
        held = sem("held")
        stored = [sem(f"stored{i}") for i in range(2)]

        def program(eng, step):
            for s in range(-3, 3):
                step(Tile(0, s))
            with eng.Fori(0, (TILES - 6) // 2) as k:
                step(Tile(k, 3))
                step(Tile(k, 4))
            for s in range(TILES - 3, TILES + 1):
                step(Tile(0, s))

        with nc.Block() as block:
            @block.sync
            def _(sp):
                for dst, src in ((w_in, c["sa_w_in"]), (w_out, c["sa_w_out"]), (spread, c["spread"]),
                                 (cos_t, c["sa_cos"]), (sin_t, c["sa_sin"]), (cols, c["sa_cols"]),
                                 (bv, c["sa_bv"]), (sel_f, c["sa_sel"])):
                    sp.dma_start(dst[:], src).then_inc(const_in, 16)

                def step(i):
                    new, last = i.plus(3), i.plus(-1)
                    if new.live:
                        hold(sp, xn_ready, new.n - 1, held)
                        sp.dma_start(xt[:, new.slot, :], x_in[new.n]).then_inc(x_in_s[new.slot], 16)
                    if last.live:
                        hold(sp, o_out, 4 * (last.n + 1), held)
                        hold(sp, rden_ready, last.n, held)
                        for j in range(4):
                            sp.dma_start(den[32 * j:32 * j + 32, :],
                                         o_raw[32 * j + KC:32 * j + KC + 1, last.slot, :, :]
                                         ).then_inc(den_in, 16)
                        hold(sp, rden_ready, last.n + 1, held)
                        hold(sp, spread_ready, 2 * last.n, held)
                        for j in range(4):
                            sp.dma_start(rrow[32 * j:32 * j + 1, :, :],
                                         rden[32 * j:32 * j + 32, :]).then_inc(rrow_in, 16)
                        sp.dma_start(xr[:, last.slot, :], x_in[last.n]).then_inc(xr_in_s[last.slot], 16)
                    if new.live:
                        hold(sp, v_ready, new.n - 1, held)
                        hold(sp, qkrot_ready, new.n - 1, held)
                        sp.dma_start(ct[:, new.slot, :], ctx[new.n]).then_inc(c_in_s[new.slot], 16)
                    if last.live:
                        hold(sp, xo_ready, last.n + 1, held)
                        sp.dma_start(x_out[last.n], xo[:, last.slot, :]).then_inc(stored[last.slot], 16)
                program(sp, step)
                for s in range(2):
                    sp.wait_ge(stored[s], 16 * TILES // 2)

            @block.gpsimd
            def _(pool):
                pool.memset(half_neg[:], -0.5).then_inc(zeroed, 1)
                pool.memset(top[:].bitcast(fp32), 0.0).then_inc(zeroed, 1)
                pool.memset(vaug[:], 0.0).then_inc(zeroed, 1)
                pool.memset(rrow[:], 0.0).then_inc(zeroed, 1)
                pool.wait_ge(zeroed, 4)
                pool.memset(vaug[:, :, :, :, KC:KC + 1], 1.0).then_inc(zeroed, 1)
                pool.wait_ge(zeroed, 5)

                def step(i):
                    new, proj, last = i.plus(3), i.plus(2), i.plus(-1)
                    if proj.live:
                        pool.wait_ge(cos_done, 2 * (proj.n + 1))
                        pool.wait_ge(sin_done, 2 * (proj.n + 1))
                        past(pool, lo_ready, proj.n)
                        past(pool, hi_ready, proj.n)
                        pool.tensor_tensor(roped[:], by_cos[:], by_sin[:], ALU.add).then_inc(roped_ready, 1)
                        pool.wait_ge(hi_ready, proj.n + 1)
                        past(pool, rep_ready, 4 * (proj.n - 1))
                        pool.tensor_tensor(lo[:, proj.slot, :], roped[:], hi[:, proj.slot, :].bitcast(fp32),
                                           ALU.subtract).then_inc(lo_ready, 1)
                    if new.live:
                        pool.wait_ge(var_ready, new.n + 1)
                        pool.tensor_tensor(rstd[:], var_eps[:], half_neg[:], ALU.pow).then_inc(rstd_ready, 1)
                    if last.live:
                        pool.wait_ge(y_ready, last.n + 1)
                        pool.wait_ge(xr_in_s[last.slot], 16 * (last.turn + 1))
                        past(pool, stored[last.slot], 16 * last.turn)
                        pool.tensor_tensor(xo[:, last.slot, :], y[:], xr[:, last.slot, :],
                                           ALU.add).then_inc(xo_ready, 1)
                program(pool, step)

            @block.scalar
            def _(act):
                act.wait_ge(const_in, 16 * 8)
                act.activation(gate[:], cols[:, 6:7], ACT.Tanh).then_inc(gate_ready, 1)

                def step(i):
                    proj, nxt = i.plus(2), i.plus(1)
                    for s in range(20):
                        if nxt.live and s in (0, 3, 6, 9):
                            g = s // 3
                            act.wait_ge(rep_ready, 4 * nxt.n + g + 1)
                            act.activation(rep[:, nxt.slot, g, :], p_x[0][:], ACT.Identity,
                                           bias=cols[:, 5:6]).then_inc(rep_out, 1)
                        if i.live and s < HEADS:
                            act.wait_ge(b_ready, HEADS * i.n + s + 1)
                            past(act, pv_done, HEADS * i.n + s + 1 - 4)
                            act.activation(prob[:, s % 4, :], p_b[s % 2][:], ACT.Exp).then_inc(prob_ready, 1)
                        if i.live and s >= 6 and (s - 6) % 4 == 0:
                            g = (s - 6) // 4
                            act.wait_ge(pv_done, HEADS * i.n + 4 * g + 4)
                            if g == 0:
                                past(act, den_in, 64 * (i.n - 1))
                                past(act, on_ready, 2 * (i.n - 1))
                            act.activation(o_raw[:, i.slot, g, :], p_o[g % 2][:, 0:T], ACT.Copy
                                           ).then_inc(o_out, 1)
                        if proj.live and s == 12:
                            act.wait_ge(roped_ready, proj.n + 1)
                            past(act, rep_ready, 4 * (proj.n - 1))
                            act.activation(hi[:, proj.slot, :], roped[:], ACT.Copy).then_inc(hi_ready, 1)
                program(act, step)

            @block.vector
            def _(dve):
                dve.wait_ge(const_in, 16 * 8)
                dve.tensor_copy(sel[:], sel_f[:]).then_inc(sel_ready, 1)
                dve.wait_ge(gate_ready, 1)
                dve.wait_ge(zeroed, 5)

                def rope(i, rotated):
                    table, out, done = (sin_t, by_sin, sin_done) if rotated else (cos_t, by_cos, cos_done)
                    dve.wait_ge(qkrot_ready if rotated else qk_ready, i.n + 1)
                    past(dve, roped_ready, i.n)
                    for n in range(2):
                        b = 2 * n + int(rotated)
                        dve.scalar_tensor_tensor(out=out[:, n * T:(n + 1) * T], in0=p_x[1][:, n * T:(n + 1) * T],
                                                 scalar=cols[:, b:b + 1], in1=table[:, n * T:(n + 1) * T],
                                                 op0=ALU.add, op1=ALU.mult).then_inc(done, 1)

                def with_maxima(i, g):
                    dve.wait_ge(m_ready, GROUPS * i.n + g + 1)
                    dve.wait_ge(rep_out, GROUPS * i.n + g + 1)
                    past(dve, b_ready, HEADS * (i.n - 1) + 4 * g + 4)
                    dve.tensor_tensor(qm[:, g, :], p_o[g % 2][:, T:2 * T], rep[:, i.slot, g, 0:T].bitcast(fp32),
                                      ALU.add).then_inc(qm_ready, 1)

                def step(i):
                    new, proj, nxt, last = i.plus(3), i.plus(2), i.plus(1), i.plus(-1)
                    for s in range(20):
                        if i.live and s == 2:
                            with_maxima(i, 3)
                        if nxt.live and 2 <= s <= HEADS + 1:
                            h = s - 2
                            dve.wait_ge(a_ready, HEADS * nxt.n + h + 1)
                            if h == 0:
                                past(dve, m_ready, GROUPS * (nxt.n - 1))
                            dve.tensor_reduce(top[:, nxt.slot, h // 4, :, 32 * (h % 4) + SPLIT],
                                              p_a[h % 2][:].rearrange("p (c s) -> p c s", c=HALF), AX, ALU.max
                                              ).then_inc(a_done, 1)
                        if nxt.live and s in (8, 12, 16):
                            with_maxima(nxt, (s - 8) // 4)
                        if proj.live and s == 3:
                            rope(proj, False)
                        if proj.live and s == 9:
                            rope(proj, True)
                        if last.live and s == 7:
                            dve.wait_ge(den_in, 64 * (last.n + 1))
                            dve.reciprocal(rden[:], den[:]).then_inc(rden_ready, 1)
                        if nxt.live and s == 11:
                            dve.wait_ge(v_ready, nxt.n + 1)
                            past(dve, pv_done, HEADS * (nxt.n - 1))
                            dve.tensor_tensor(vaug[:, nxt.slot, :, :, 0:KC].rearrange("p c h k -> p (c h) k"),
                                              p_x[0][:, 0:2 * PART].rearrange("p (n k) -> p n k", k=KC),
                                              bv[:].rearrange("p (n k) -> p n k", k=KC), ALU.add
                                              ).then_inc(vaug_ready, 1)
                        if last.live and s in (14, 15):
                            g2 = s - 14
                            dve.wait_ge(spread_ready, 2 * last.n + g2 + 1)
                            past(dve, wo_ready, last.n)
                            dve.tensor_tensor(on[:, 2 * g2:2 * g2 + 2, :],
                                              p_x[1 - g2][:].rearrange("p (g t) -> p g t", g=2),
                                              o_raw[:, last.slot, 2 * g2:2 * g2 + 2, :], ALU.mult
                                              ).then_inc(on_ready, 1)
                        if last.live and s == 19:
                            dve.wait_ge(wo_ready, last.n + 1)
                            past(dve, xo_ready, last.n)
                            dve.tensor_scalar(y[:], p_x[1][:, 0:T], cols[:, 4:5], gate[:], ALU.add, ALU.mult
                                              ).then_inc(y_ready, 1)
                        if new.live and s == 13:
                            dve.wait_ge(x_in_s[new.slot], 16 * (new.turn + 1))
                            dve.bn_stats(stats[:], xt[:, new.slot, :]).then_inc(stats_ready, 1)
                            hold(dve, stats_ready, 2 * new.n + 1, held)
                            dve.bn_aggr(mv[:], stats[:]).then_inc(stats_ready, 1)
                            dve.wait_ge(stats_ready, 2 * new.n + 2)
                            past(dve, rstd_ready, new.n)
                            dve.tensor_scalar_add(var_eps[:], mv[:, 1:2], EPS).then_inc(var_ready, 1)
                        if new.live and s == 17:
                            dve.wait_ge(rstd_ready, new.n + 1)
                            past(dve, qkrot_ready, new.n - 1)
                            dve.tensor_scalar(xn[:, new.slot, :], xt[:, new.slot, :], mv[:, 0:1], rstd[:],
                                              ALU.subtract, ALU.mult).then_inc(xn_ready, 1)
                program(dve, step)

            @block.tensor
            def _(pe):
                pe.wait_ge(sel_ready, 1)
                pe.wait_ge(zeroed, 5)

                def project(i, rotated):
                    r = int(rotated)
                    if not rotated:
                        pe.wait_ge(xn_ready, i.n + 1)
                        pe.wait_ge(c_in_s[i.slot], 16 * (i.turn + 1))
                    pe.matmul(p_x[1][:, 0:T], w_in[:, r, :], xn[:, i.slot, :], start=True, stop=True)
                    pe.matmul(p_x[1][:, T:2 * T], w_in[:, 2 + r, :], ct[:, i.slot, :], start=True, stop=True
                              ).then_inc(qkrot_ready if rotated else qk_ready, 1)

                def move_maxima(i, g):
                    pe.wait_ge(a_done, HEADS * i.n + 4 * g + 4)
                    past(pe, o_out, GROUPS * (i.n - 1) + g + 1)
                    for tc in range(HALF):
                        mm = pe.matmul(p_o[g % 2][:, T + tc * PART:T + (tc + 1) * PART], top[:, i.slot, g, tc, :],
                                       sel[:, 16, :], start=True, stop=True)
                    mm.then_inc(m_ready, 1)

                def step(i):
                    proj, nxt, last = i.plus(2), i.plus(1), i.plus(-1)
                    for s in range(20):
                        if i.live and s == 2:
                            move_maxima(i, 3)
                        if nxt.live and s in (7, 11, 15):
                            move_maxima(nxt, (s - 7) // 4)
                        if nxt.live and s in (0, 3, 6, 9):
                            g = s // 3
                            if g == 0:
                                pe.wait_ge(lo_ready, nxt.n + 1)
                                past(pe, vaug_ready, nxt.n)
                                past(pe, on_ready, 2 * last.n)
                            else:
                                pe.wait_ge(rep_out, 4 * nxt.n + g)
                            for n in range(2):
                                for part, of in enumerate((hi, lo)):
                                    mm = pe.matmul(p_x[0][:, n * T:(n + 1) * T], sel[:, 4 * g + 2 * n + part, :],
                                                   of[:, nxt.slot, n * T:(n + 1) * T],
                                                   start=(part == 0), stop=(part == 1))
                            mm.then_inc(rep_ready, 1)
                        if proj.live and s == 2:
                            past(pe, y_ready, i.n - 1)
                            past(pe, sin_done, 2 * proj.n)
                            project(proj, False)
                        if proj.live and s == 8:
                            pe.wait_ge(cos_done, 2 * (proj.n + 1))
                            project(proj, True)
                        if nxt.live and s == 10:
                            pe.wait_ge(rep_out, 4 * nxt.n + 4)
                            for sc in range(HALF):
                                mm = pe.matmul(p_x[0][:, sc * PART:(sc + 1) * PART],
                                               ct[:, nxt.slot, sc * PART:(sc + 1) * PART], w_in[:, 4, :],
                                               start=True, stop=True)
                            mm.then_inc(v_ready, 1)
                        if last.live and s in (13, 14):
                            g2 = s - 13
                            if g2 == 0:
                                pe.wait_ge(rrow_in, 64 * (last.n + 1))
                                if proj.live:
                                    pe.wait_ge(sin_done, 2 * (proj.n + 1))
                                else:
                                    past(pe, y_ready, last.n)
                            elif nxt.live:
                                pe.wait_ge(vaug_ready, nxt.n + 1)
                            for g in range(2):
                                mm = pe.matmul(p_x[1 - g2][:, g * T:(g + 1) * T], spread[:],
                                               rrow[:, 2 * g2 + g, :], start=True, stop=True)
                            mm.then_inc(spread_ready, 1)
                        if last.live and s == 18:
                            pe.wait_ge(on_ready, 2 * last.n + 2)
                            for g in range(GROUPS):
                                mm = pe.matmul(p_x[1][:, 0:T], w_out[:, g, :], on[:, g, :],
                                               start=(g == 0), stop=(g == GROUPS - 1))
                            mm.then_inc(wo_ready, 1)
                        if i.live and s < HEADS:
                            h, g, r = s, s // 4, 32 * (s % 4)
                            if s % 4 == 0:
                                pe.wait_ge(qm_ready, GROUPS * i.n + g + 1)
                            past(pe, prob_ready, HEADS * i.n + h - 1)
                            for sc in range(HALF):
                                at = T + sc * PART
                                mm = pe.matmul(p_b[h % 2][:, sc * T:(sc + 1) * T],
                                               rep[r:r + SPLIT + 1, i.slot, g, at:at + PART],
                                               qm[r:r + SPLIT + 1, g, :], start=True, stop=True)
                            mm.then_inc(b_ready, 1)
                        if i.live and 2 <= s <= HEADS + 1:
                            h, g, r = s - 2, (s - 2) // 4, 32 * ((s - 2) % 4)
                            pe.wait_ge(prob_ready, HEADS * i.n + h + 1)
                            if h % 4 == 0:
                                past(pe, o_out, GROUPS * i.n + g - 1)
                                if g < 2 or nxt.live:
                                    pe.wait_ge(qm_ready, GROUPS * i.n + 3 + g)
                            for sc in range(HALF):
                                mm = pe.matmul(p_o[g % 2][r:r + 32, 0:T], vaug[:, i.slot, sc, h, :],
                                               prob[:, h % 4, sc * T:(sc + 1) * T],
                                               start=(sc == 0), stop=(sc == HALF - 1), tile_position=(0, r))
                            mm.then_inc(pv_done, 1)
                        if nxt.live and 2 <= s <= HEADS + 1:
                            h = s - 2
                            g, r = h // 4, 32 * (h % 4)
                            if h % 4 == 0:
                                pe.wait_ge(rep_out, 4 * nxt.n + g + 1)
                            past(pe, a_done, HEADS * nxt.n + h - 1)
                            for tc in range(HALF):
                                mm = pe.matmul(p_a[h % 2][:, tc * T:(tc + 1) * T],
                                               rep[r:r + SPLIT, nxt.slot, g, tc * PART:(tc + 1) * PART],
                                               rep[r:r + SPLIT, nxt.slot, g, T:2 * T], start=True, stop=True)
                            mm.then_inc(a_ready, 1)
                program(pe, step)


def _tables():
    f = np.float32
    inv = f(1.0) / f(10000.0) ** (np.arange(0, 8, 2, dtype=f) / f(8))
    ang = np.arange(256, dtype=f)[None, :] * np.tile(inv, 2)[:, None].astype(f)
    cos8, sin8 = np.cos(ang).astype(f), np.sin(ang).astype(f)
    sin8 = sin8 * np.array([-1] * 4 + [1] * 4, f)[:, None]
    s = f(1 / np.sqrt(8.0))
    out = {}
    out["sa_cos"] = np.concatenate([np.tile(cos8, (16, 1)) * s, np.tile(cos8, (16, 1))], 1).astype(f)
    out["sa_sin"] = np.concatenate([np.tile(sin8, (16, 1)) * s, np.tile(sin8, (16, 1))], 1).astype(f)
    sel = np.zeros((128, 17, 128), f)
    for g in range(4):
        for j in range(4):
            for c in range(8):
                row = (4 * g + j) * 8 + c
                at = 32 * j + c
                for kind, places in enumerate(((0, 8), (16,), (0, 16), (8,))):
                    for p in places:
                        sel[row, 4 * g + kind, at + p] = 1
    sel[:, 16, :] = np.eye(128, dtype=f)
    out["sa_sel"] = sel
    spread = np.zeros((128, 128), f)
    for j in range(4):
        spread[32 * j, 32 * j:32 * j + 32] = 1
    out["spread"] = spread
    return out


def _layout_softmax_attention(a):
    f = np.float32
    perm = np.arange(64).reshape(8, 2, 4)[:, ::-1].reshape(64)
    w_in = np.zeros((128, 5, 128), f)
    Wq, Wk, Wv, Wo = (np.asarray(a[f"L0_xattn_W{n}"]) for n in "qkvo")
    for n, w in enumerate((Wq, Wq[perm], Wk, Wk[perm], Wv)):
        for b in range(2):
            w_in[64 * b:64 * b + 64, n, 64 * b:64 * b + 64] = w.T
    w_out = np.zeros((128, 4, 128), f)
    for g in range(4):
        for j in range(4):
            h = 4 * (g % 2) + j
            w_out[32 * j:32 * j + 8, g, 64 * (g // 2):64 * (g // 2) + 64] = Wo[:, 8 * h:8 * h + 8].T
    cols = np.zeros((128, 8), f)
    bq, bk, bo, bv = (np.asarray(a[f"L0_xattn_b{n}"]) for n in ("q", "k", "o", "v"))
    for n, b in enumerate((bq, bq[perm], bk, bk[perm], bo)):
        cols[:, n] = np.tile(b, 2)
    cols[24::32, 5] = -1
    cols[:, 6] = np.asarray(a["g_xattn"])[0]
    return {"sa_w_in": w_in, "sa_w_out": w_out, "sa_cols": cols, "sa_bv": np.tile(bv, (128, 4))}

CHUNK = 512
CHUNKS = ROWS // CHUNK


def stage_experts(nc, name, x_in, x_out, w_gate, w_up, w_down, c, EXPERTS, HIDDEN, TOP, norm, skip=None):
    KC = DIM // PART
    MC = HIDDEN // PART
    WIDTH = 2 * KC * HIDDEN + MC * DIM
    UP, DOWN = KC * HIDDEN, 2 * KC * HIDDEN
    E8 = EXPERTS + 8
    LOWEST, MARK = -3.0e38, -3.2e38
    GRP = 8
    FREE = 2 * CHUNK // PART
    st = ExitStack()
    sb = lambda n, s, d=fp32: st.enter_context(nc.sbuf_tensor(f"{name}_{n}", s, d))
    sem = lambda n: nc.alloc_semaphore(f"{name}_{n}")
    with st:
        total = sb("total", [PART, TILES, DIM])
        ht_hi, ht_lo = (sb(n, [PART, KC, ROWS], fp32r) for n in ("ht_hi", "ht_lo"))
        ident, router = sb("ident", [PART, PART]), sb("router", [PART, KC, EXPERTS])
        g_col, gate = sb("g_col", [PART, 1]), sb("gate", [PART, 1])
        norm_w = sb("norm_w", [PART, DIM]) if norm == "rms" else None
        half_neg = sb("half_neg", [PART, GRP])
        stats, mv = sb("stats", [PART, TILES, 6]), sb("mv", [PART, TILES, 2])
        var_eps, rstd = sb("var_eps", [PART, TILES]), sb("rstd", [PART, TILES])
        hn, ht = sb("hn", [PART, 2, DIM]), sb("ht", [PART, 2, DIM])
        score, left = sb("score", [PART, TILES, E8]), sb("left", [PART, TILES, E8])
        top8, taken = sb("top8", [PART, TILES, 8]), sb("taken", [PART, TILES, 8])
        shifted, picked = sb("shifted", [PART, TILES, EXPERTS]), sb("picked", [PART, TILES, EXPERTS])
        weight = sb("weight", [PART, TILES, EXPERTS])
        wsum = sb("wsum", [PART, TILES])
        raw = sb("raw", [PART, 2, WIDTH])
        w_hi, w_lo = (sb(n, [PART, 2, WIDTH], fp32r) for n in ("w_hi", "w_lo"))
        silu, act_f = sb("silu", [PART, 2, CHUNK]), sb("act_f", [PART, 2, CHUNK])
        a_hi, a_lo = (sb(n, [PART, 2, MC, CHUNK], fp32r) for n in ("a_hi", "a_lo"))
        bank = lambda n: st.enter_context(nc.psum_tensor(f"{name}_{n}", [PART, CHUNK], fp32))
        p_gate, p_up = [bank(f"pg{i}") for i in range(2)], [bank(f"pu{i}") for i in range(2)]
        p_y = [bank(f"py{i}") for i in range(4)]
        p_t, p_s = p_gate, p_up

        const_in, zeroed, gate_ready = sem("const_in"), sem("zeroed"), sem("gate")
        x_loaded = [sem(f"x{i}") for i in range(TILES // GRP)]
        stat, var_ready, rstd_ready, hn_ready = sem("stat"), sem("var"), sem("rstd"), sem("hn")
        t_ready, ht_ready, hi_ready, lo_ready = sem("t"), sem("ht"), sem("hi"), sem("lo")
        s_ready, score_out, route = sem("s"), sem("score_out"), sem("route")
        shifted_ready, exp_ready = sem("shifted"), sem("exp")
        weight_ready, square = sem("weight"), sem("square")
        raw_in = [sem(f"raw{i}") for i in range(2)]
        whi_ready, wlo_ready = sem("whi"), sem("wlo")
        gate_mm, up_mm, silu_ready, act_ready = sem("gate_mm"), sem("up_mm"), sem("silu"), sem("act")
        ahi_ready, alo_ready, y_mm, y_added = sem("ahi"), sem("alo"), sem("y_mm"), sem("y_added")
        skip_in = [sem(f"skip{i}") for i in range(2)]
        final = sem("final")
        held = sem("held")
        stored = sem("stored")

        def per_tile(eng, step):
            for n in range(-1, 3):
                step(Tile(0, n))
            with eng.Fori(0, (TILES - 4) // 2) as k:
                step(Tile(k, 3))
                step(Tile(k, 4))
            step(Tile(0, TILES - 1))

        def per_unit(eng, begin, unit):
            def chunks(e):
                begin(e)
                unit(e, Tile(0, 0), (e.plus(-1), Tile(0, CHUNKS - 1)))
                unit(e, Tile(0, 1), (e, Tile(0, 0)))
                with eng.Fori(0, CHUNKS // 2 - 1) as j:
                    unit(e, Tile(j, 2), (e, Tile(j, 1)))
                    unit(e, Tile(j, 3), (e, Tile(j, 2)))
            for s in range(2):
                chunks(Tile(0, s))
            with eng.Fori(0, EXPERTS // 2 - 1) as k:
                for s in range(2, 4):
                    chunks(Tile(k, s))

        def first(e):
            return isinstance(e.k, int) and e.n < 0

        with nc.Block() as block:
            @block.sync
            def _(sp):
                consts = [(ident, c["ident"]), (router, c[name + "_router"]), (g_col, c[name + "_g"])]
                if norm == "rms":
                    consts.append((norm_w, c[name + "_norm_w"]))
                for dst, src in consts:
                    sp.dma_start(dst[:], src).then_inc(const_in, 16)
                for g in range(TILES // GRP):
                    sp.dma_start(total[:, g * GRP:(g + 1) * GRP, :],
                                 x_in[g * GRP:(g + 1) * GRP].rearrange("t p d -> p t d")).then_inc(x_loaded[g], 16)

                def load(e):
                    hold(sp, whi_ready, e.n - 1, held)
                    hold(sp, wlo_ready, e.n - 1, held)
                    r = raw[:, e.slot, :]
                    sp.dma_start(r[:, 0:UP].rearrange("p (k h) -> p k h", k=KC),
                                 w_gate[e.n].rearrange("(k p) h -> p k h", p=PART)).then_inc(raw_in[e.slot], 16)
                    sp.dma_start(r[:, UP:DOWN].rearrange("p (k h) -> p k h", k=KC),
                                 w_up[e.n].rearrange("(k p) h -> p k h", p=PART)).then_inc(raw_in[e.slot], 16)
                    sp.dma_start(r[:, DOWN:WIDTH].rearrange("p (k h) -> p k h", k=MC),
                                 w_down[e.n].rearrange("(k p) h -> p k h", p=PART)).then_inc(raw_in[e.slot], 16)
                for s in range(2):
                    load(Tile(0, s))
                with sp.Fori(0, EXPERTS // 2 - 1) as k:
                    for s in range(2, 4):
                        load(Tile(k, s))
                if norm == "layer":
                    for g in range(TILES // GRP):
                        sp.wait_ge(y_added, FREE + (EXPERTS - 1) * TILES + (g + 1) * GRP)
                        sp.dma_start(x_out[g * GRP:(g + 1) * GRP].rearrange("t p d -> p t d"),
                                     total[:, g * GRP:(g + 1) * GRP, :]).then_inc(stored, 16)
                    sp.wait_ge(stored, 16 * TILES // GRP)
                else:
                    sp.wait_ge(y_mm, 2 * CHUNKS * EXPERTS)
                    room = ht_hi[:].rearrange("p k r -> p (k r)").rearrange("p (t d) -> p t d", d=DIM)
                    for g in range(2):
                        sp.dma_start(room[:, g * 16:(g + 1) * 16, :].bitcast(fp32),
                                     skip[g * 16:(g + 1) * 16].rearrange("t p d -> p t d")
                                     ).then_inc(skip_in[g], 16)
                    for g in range(8):
                        sp.wait_ge(final, g + 1)
                        sp.dma_start(x_out[g * 4:(g + 1) * 4].rearrange("t p d -> p t d"),
                                     total[:, g * 4:(g + 1) * 4, :]).then_inc(stored, 16)
                    sp.wait_ge(stored, 16 * 8)

            @block.gpsimd
            def _(pool):
                pool.memset(half_neg[:], -0.5).then_inc(zeroed, 1)
                pool.memset(score[:], LOWEST).then_inc(zeroed, 1)
                pool.memset(taken[:], LOWEST).then_inc(zeroed, 1)
                pool.wait_ge(zeroed, 3)

                for g in range(TILES // GRP):
                    grp = slice(g * GRP, (g + 1) * GRP)
                    pool.wait_ge(var_ready, g + 1)
                    pool.tensor_tensor(rstd[:, grp], var_eps[:, grp], half_neg[:], ALU.pow).then_inc(rstd_ready, GRP)

                def step(i):
                    if i.live:
                        pool.wait_ge(hi_ready, i.n + 1)
                        pool.wait_ge(ht_ready, i.n + 1)
                        pool.tensor_tensor(ht_lo[:, :, bass.ds(i.n * PART, PART)],
                                           ht[:, i.slot, :].rearrange("p (k t) -> p k t", k=KC),
                                           ht_hi[:, :, bass.ds(i.n * PART, PART)].bitcast(fp32),
                                           ALU.subtract).then_inc(lo_ready, 1)
                per_tile(pool, step)

                def unit(e, ch, prev):
                    for m in range(MC):
                        n = (e.n * CHUNKS + ch.n) * MC + m
                        pool.wait_ge(ahi_ready, n + 1)
                        pool.tensor_tensor(a_lo[:, ch.slot, m, :], act_f[:, m if MC == 2 else ch.slot, :],
                                           a_hi[:, ch.slot, m, :].bitcast(fp32), ALU.subtract
                                           ).then_inc(alo_ready, 1)
                per_unit(pool, lambda e: None, unit)

            @block.scalar
            def _(act):
                act.wait_ge(const_in, 16 * (4 if norm == "rms" else 3))
                act.activation(gate[:], g_col[:], ACT.Tanh).then_inc(gate_ready, 1)
                act.wait_ge(zeroed, 3)

                def keep_score(i):
                    act.wait_ge(s_ready, i.n + 1)
                    act.activation(score[:, i.n, 0:EXPERTS], p_s[i.slot][:, 0:EXPERTS], ACT.Copy
                                   ).then_inc(score_out, 1)

                def step(i):
                    old = i.plus(-1)
                    if i.live:
                        act.wait_ge(t_ready, i.n + 1)
                        past(act, s_ready, i.n - 1)
                        past(act, lo_ready, i.n - 1)
                        act.activation(ht[:, i.slot, :], p_t[i.slot][:, 0:DIM], ACT.Copy).then_inc(ht_ready, 1)
                        act.activation(ht_hi[:, :, bass.ds(i.n * PART, PART)],
                                       p_t[i.slot][:, 0:DIM].rearrange("p (k t) -> p k t", k=KC),
                                       ACT.Copy).then_inc(hi_ready, 1)
                    if old.live:
                        keep_score(old)
                per_tile(act, step)
                keep_score(Tile(0, TILES - 1))

                def split(e):
                    act.wait_ge(raw_in[e.slot], 48 * (e.turn + 1))
                    past(act, y_mm, 2 * CHUNKS * (e.n - 1))
                    act.activation(w_hi[:, e.slot, :], raw[:, e.slot, :], ACT.Copy).then_inc(whi_ready, 1)
                split(Tile(0, 0))
                split(Tile(0, 1))
                act.wait_ge(shifted_ready, 1)
                act.activation(weight[:], shifted[:], ACT.Exp).then_inc(exp_ready, 1)

                def begin(e):
                    if not isinstance(e.k, int):
                        split(e)

                def unit(e, ch, prev):
                    for m in range(MC):
                        n = (e.n * CHUNKS + ch.n) * MC + m
                        slot = m if MC == 2 else ch.slot
                        act.wait_ge(gate_mm, n + 1)
                        past(act, act_ready, n - 1)
                        act.activation(silu[:, slot, :], p_gate[slot][:], ACT.Silu).then_inc(silu_ready, 1)
                    for m in range(MC):
                        n = (e.n * CHUNKS + ch.n) * MC + m
                        slot = m if MC == 2 else ch.slot
                        act.wait_ge(act_ready, n + 1)
                        past(act, y_mm, 2 * (e.n * CHUNKS + ch.n - 1))
                        act.activation(a_hi[:, ch.slot, m, :], act_f[:, slot, :], ACT.Copy).then_inc(ahi_ready, 1)
                per_unit(act, begin, unit)

            @block.vector
            def _(dve):
                dve.wait_ge(zeroed, 3)
                dve.wait_ge(const_in, 16 * (4 if norm == "rms" else 3))
                for g in range(TILES // GRP):
                    grp = slice(g * GRP, (g + 1) * GRP)
                    dve.wait_ge(x_loaded[g], 16)
                    for t in range(g * GRP, (g + 1) * GRP):
                        dve.bn_stats(stats[:, t, :], total[:, t, :]).then_inc(stat, 1)
                    dve.wait_ge(stat, (2 * g + 1) * GRP)
                    for t in range(g * GRP, (g + 1) * GRP):
                        dve.bn_aggr(mv[:, t, :], stats[:, t, :]).then_inc(stat, 1)
                    dve.wait_ge(stat, (2 * g + 2) * GRP)
                    mean, var = mv[:, grp, 0], mv[:, grp, 1]
                    if norm == "rms":
                        dve.tensor_tensor(var_eps[:, grp], mean, mean, ALU.mult).then_inc(square, 1)
                        dve.wait_ge(square, 2 * g + 1)
                        dve.tensor_tensor(var_eps[:, grp], var_eps[:, grp], var, ALU.add).then_inc(square, 1)
                        dve.wait_ge(square, 2 * g + 2)
                        var = var_eps[:, grp]
                    dve.tensor_scalar_add(var_eps[:, grp], var, EPS).then_inc(var_ready, 1)

                def step(i):
                    new = i.plus(1)
                    if new.live:
                        s = new.slot
                        dve.wait_ge(rstd_ready, new.n + 1)
                        past(dve, t_ready, new.n - 1)
                        if norm == "rms":
                            dve.scalar_tensor_tensor(out=hn[:, s, :], in0=total[:, new.n, :],
                                                     scalar=rstd[:, bass.ds(new.n, 1)], in1=norm_w[:],
                                                     op0=ALU.mult, op1=ALU.mult).then_inc(hn_ready, 1)
                        else:
                            dve.tensor_scalar(hn[:, s, :], total[:, new.n, :], mv[:, new.n, 0:1],
                                              rstd[:, bass.ds(new.n, 1)], ALU.subtract, ALU.mult
                                              ).then_inc(hn_ready, 1)
                per_tile(dve, step)

                def split(e):
                    dve.wait_ge(whi_ready, e.n + 1)
                    dve.tensor_tensor(w_lo[:, e.slot, :], raw[:, e.slot, :], w_hi[:, e.slot, :].bitcast(fp32),
                                      ALU.subtract).then_inc(wlo_ready, 1)
                split(Tile(0, 0))
                split(Tile(0, 1))

                dve.wait_ge(score_out, TILES)
                for t in range(TILES):
                    dve.max(top8[:, t, :], score[:, t, 0:EXPERTS]).then_inc(route, 1)
                dve.wait_ge(route, TILES)
                dve.tensor_tensor(shifted[:], score[:, :, 0:EXPERTS],
                                  top8[:, :, 0:1].to_broadcast([PART, TILES, EXPERTS]), ALU.subtract
                                  ).then_inc(shifted_ready, 1)
                dve.tensor_copy(taken[:, :, 0:TOP], top8[:, :, 0:TOP]).then_inc(route, 1)
                dve.wait_ge(route, TILES + 1)
                for t in range(TILES):
                    dve.match_replace(left[:, t, :], taken[:, t, :], score[:, t, :], MARK).then_inc(route, 1)
                dve.wait_ge(route, 2 * TILES + 1)
                dve.tensor_tensor(picked[:], left[:, :, 0:EXPERTS], score[:, :, 0:EXPERTS], ALU.not_equal
                                  ).then_inc(weight_ready, 1)
                dve.wait_ge(weight_ready, 1)
                dve.engine_nop().then_inc(y_added, FREE)
                dve.wait_ge(exp_ready, 1)
                dve.tensor_tensor(weight[:], weight[:], picked[:], ALU.mult).then_inc(weight_ready, 1)
                dve.wait_ge(weight_ready, 2)
                dve.tensor_reduce(wsum[:], weight[:], AX, ALU.add).then_inc(weight_ready, 1)
                dve.wait_ge(weight_ready, 3)
                dve.reciprocal(wsum[:], wsum[:]).then_inc(weight_ready, 1)
                dve.wait_ge(weight_ready, 4)
                if norm == "layer":
                    dve.wait_ge(gate_ready, 1)
                    dve.tensor_scalar(wsum[:], wsum[:], gate[:], None, ALU.mult).then_inc(weight_ready, 1)
                else:
                    dve.tensor_scalar(wsum[:], wsum[:], 1.0, None, ALU.mult).then_inc(weight_ready, 1)
                dve.wait_ge(weight_ready, 5)
                dve.tensor_tensor(weight[:], weight[:], wsum[:].unsqueeze(2).to_broadcast([PART, TILES, EXPERTS]),
                                  ALU.mult).then_inc(weight_ready, 1)
                dve.wait_ge(weight_ready, 6)

                def begin(e):
                    if not isinstance(e.k, int):
                        split(e)

                def add(e, ch):
                    for t in range(CHUNK // PART):
                        n = (e.n * CHUNKS + ch.n) * 4 + t
                        if t % 2 == 0:
                            dve.wait_ge(y_mm, (e.n * CHUNKS + ch.n) * 2 + t // 2 + 1)
                        tile = 4 * ch.n + t
                        if not (isinstance(e.k, int) and e.n == 0):
                            dve.wait_ge(y_added, FREE + n - 31)
                        dve.scalar_tensor_tensor(out=total[:, tile, :],
                                                 in0=p_y[2 * ch.slot + t // 2][:, (t % 2) * DIM:(t % 2 + 1) * DIM],
                                                 scalar=weight[:, tile, bass.ds(e.n, 1)], in1=total[:, tile, :],
                                                 op0=ALU.mult, op1=ALU.add).then_inc(y_added, 1)

                def unit(e, ch, prev):
                    for m in range(MC):
                        n = (e.n * CHUNKS + ch.n) * MC + m
                        slot = m if MC == 2 else ch.slot
                        dve.wait_ge(silu_ready, n + 1)
                        dve.wait_ge(up_mm, n + 1)
                        past(dve, alo_ready, n - 1)
                        dve.tensor_tensor(act_f[:, slot, :], silu[:, slot, :], p_up[slot][:], ALU.mult
                                          ).then_inc(act_ready, 1)
                    if not first(prev[0]):
                        add(*prev)
                per_unit(dve, begin, unit)
                add(Tile(0, EXPERTS - 1), Tile(0, CHUNKS - 1))
                if norm == "rms":
                    dve.wait_ge(gate_ready, 1)
                    dve.wait_ge(y_added, FREE + EXPERTS * TILES)
                    room = ht_hi[:].rearrange("p k r -> p (k r)").rearrange("p (t d) -> p t d", d=DIM)
                    for g in range(8):
                        if g % 4 == 0:
                            dve.wait_ge(skip_in[g // 4], 16)
                        rows = total[:, 4 * g:4 * g + 4, :]
                        dve.scalar_tensor_tensor(out=rows, in0=rows, scalar=gate[:],
                                                 in1=room[:, 4 * g:4 * g + 4, :].bitcast(fp32),
                                                 op0=ALU.mult, op1=ALU.add).then_inc(final, 1)

            @block.tensor
            def _(pe):
                pe.wait_ge(const_in, 16 * (4 if norm == "rms" else 3))

                def step(i):
                    new = i.plus(1)
                    if new.live:
                        pe.wait_ge(hn_ready, new.n + 1)
                        past(pe, ht_ready, new.n - 1)
                        past(pe, hi_ready, new.n - 1)
                        for k in range(KC):
                            mm = pe.transpose(p_t[new.slot][:, k * PART:(k + 1) * PART],
                                              hn[:, new.slot, k * PART:(k + 1) * PART], ident[:])
                        mm.then_inc(t_ready, 1)
                    if i.live:
                        pe.wait_ge(ht_ready, i.n + 1)
                        past(pe, score_out, i.n - 1)
                        for k in range(KC):
                            mm = pe.matmul(p_s[i.slot][:, 0:EXPERTS], ht[:, i.slot, k * PART:(k + 1) * PART],
                                           router[:, k, :], start=(k == 0), stop=(k == KC - 1))
                        mm.then_inc(s_ready, 1)
                per_tile(pe, step)
                pe.wait_ge(lo_ready, TILES)
                pe.wait_ge(score_out, TILES)

                def product(out, lhs, rhs, blocks):
                    n = 0
                    for b in range(blocks):
                        (lh, ll), (rh, rl) = lhs(b), rhs(b)
                        for x, y in ((lh, rh), (lh, rl), (ll, rh)):
                            mm = pe.matmul(out, x, y, start=(n == 0), stop=(n == 3 * blocks - 1))
                            n += 1
                    return mm

                def down(e, ch):
                    pe.wait_ge(alo_ready, (e.n * CHUNKS + ch.n + 1) * MC)
                    for t in range(4):
                        if t % 2 == 0:
                            pe.wait_ge(y_added, FREE + 4 * (e.n * CHUNKS + ch.n - 2) + 2 * (t // 2) + 2)
                        mm = product(p_y[2 * ch.slot + t // 2][:, (t % 2) * DIM:(t % 2 + 1) * DIM],
                                     lambda m: [a[:, ch.slot, m, t * PART:(t + 1) * PART] for a in (a_hi, a_lo)],
                                     lambda m: [w[:, e.slot, DOWN + m * DIM:DOWN + (m + 1) * DIM]
                                                for w in (w_hi, w_lo)], MC)
                        if t % 2 == 1:
                            mm.then_inc(y_mm, 1)

                def begin(e):
                    pe.wait_ge(wlo_ready, e.n + 1)

                def unit(e, ch, prev):
                    for m in range(MC):
                        n = (e.n * CHUNKS + ch.n) * MC + m
                        slot = m if MC == 2 else ch.slot
                        for bank_, at, done, free in ((p_gate, 0, gate_mm, silu_ready), (p_up, UP, up_mm, act_ready)):
                            past(pe, free, n - 1)
                            product(bank_[slot][:],
                                    lambda k: [w[:, e.slot, at + k * HIDDEN + m * PART:at + k * HIDDEN + (m + 1) * PART]
                                               for w in (w_hi, w_lo)],
                                    lambda k: [h[:, k, bass.ds(ch.n * CHUNK, CHUNK)] for h in (ht_hi, ht_lo)], KC
                                    ).then_inc(done, 1)
                    if not first(prev[0]):
                        down(*prev)
                per_unit(pe, begin, unit)
                down(Tile(0, EXPERTS - 1), Tile(0, CHUNKS - 1))



def _layout_experts(a):
    f = np.float32
    block = lambda w: np.ascontiguousarray(np.asarray(w).reshape(2, 128, -1).transpose(1, 0, 2))
    col = lambda v: np.full((128, 1), v, f)
    return {"ident": np.eye(128, dtype=f),
            "moe0_router": block(a["L0_ffn_router_w"]), "moe0_g": col(np.asarray(a["g_ffn"])[0]),
            "moe1_router": block(a["L1_ffn_wg"]), "moe1_g": col(np.asarray(a["g_ffn"])[1]),
            "moe1_norm_w": np.tile(np.asarray(a["L1_ffn_ff_ln_w"]), (128, 1))}


def stage_linear_attention(nc, x_in, x_out, ctx, c):
    KC, TPC, HEADS, HC, F = 2, CHUNK // PART, 16, 16, 64
    PAIRS, HALF = HEADS // 2, 4
    E = HC + 1
    WQ, WK, WV, WFQ, WFK, WEND = 0, 512, 1024, 1536, 2048, 2560
    st = ExitStack()
    sb = lambda n, s, d=fp32: st.enter_context(nc.sbuf_tensor(f"la_{n}", s, d))
    sem = lambda n: nc.alloc_semaphore(f"la_{n}")
    with st:
        raw = sb("raw", [PART, WEND])
        w_hi, w_lo = (sb(n, [PART, WEND], fp32r) for n in ("w_hi", "w_lo"))
        w_out = sb("w_out", [PART, KC, DIM])
        ident, cols, mask = sb("ident", [PART, PART]), sb("cols", [PART, 8]), sb("mask", [PART, TILES])
        bv, bo = sb("bv", [PART, DIM]), sb("bo", [PART, DIM])
        gate, half_neg = sb("gate", [PART, 1]), sb("half_neg", [PART, TPC])
        rows = sb("rows", [PART, 2, 2, TPC, DIM])
        stats, mv = sb("stats", [PART, TPC, 6]), sb("mv", [PART, TPC, 2])
        var_eps, rstd = sb("var_eps", [PART, TPC]), sb("rstd", [PART, TPC])
        hn = sb("hn", [PART, TPC, DIM])
        t_hi, t_lo = (sb(n, [PART, 2, 2, KC, CHUNK], fp32r) for n in ("t_hi", "t_lo"))
        qk_hi, qk_lo = (sb(n, [PART, 2, 4, CHUNK], fp32r) for n in ("qk_hi", "qk_lo"))
        qf = sb("qf", [PART, 2, PAIRS, CHUNK])
        kf = sb("kf", [PART, 2, HEADS * F])
        vb = sb("vb", [PART, 2, PAIRS, 2, 2, E])
        kv = sb("kv", [PART, 2, PAIRS, 2, 2, E])
        den, rden = sb("den", [PART, HALF, 2]), sb("rden", [PART, HALF, 2])
        on, o_t = sb("on", [PART, 2, DIM]), sb("o_t", [PART, 2, DIM])
        xr, y, xo = sb("xr", [PART, 2, DIM]), sb("y", [PART, DIM]), sb("xo", [PART, 2, DIM])
        bank = lambda n: st.enter_context(nc.psum_tensor(f"la_{n}", [PART, CHUNK], fp32))
        p_t, p_k, p_v, p_kv, p_q, p_y = (bank(n) for n in ("ptt", "pk", "pv", "pkv", "pq", "py"))
        p_p = [bank(f"pp{i}") for i in range(2)]

        const_in, zeroed, gate_ready = sem("const_in"), sem("zeroed"), sem("gate")
        whi_ready, wlo_ready = sem("whi"), sem("wlo")
        in_s = [sem(f"in{i}") for i in range(2)]
        xr_s = [sem(f"xr{i}") for i in range(2)]
        stat, var_ready, rstd_ready, hn_ready = sem("stat"), sem("var"), sem("rstd"), sem("hn")
        t_ready, thi_ready, tlo_ready = sem("t"), sem("thi"), sem("tlo")
        qk_mm, qkhi_ready, qklo_ready, qf_mm, qf_ready = sem("qk_mm"), sem("qkhi"), sem("qklo"), sem("qf_mm"), sem("qf")
        kf_mm, kf_ready, v_mm, v_ready = sem("kf_mm"), sem("kf"), sem("v_mm"), sem("v")
        kv_mm, kv_low, kv_high = sem("kv_mm"), sem("kv_low"), sem("kv_high")
        q_mm, den_ready, on_ready = sem("q_mm"), sem("den"), sem("on")
        ot_mm, ot_ready, y_mm, y_ready, xo_ready = sem("ot_mm"), sem("ot"), sem("y_mm"), sem("y"), sem("xo")
        held = sem("held")
        stored = [sem(f"stored{i}") for i in range(2)]

        def live(ch):
            return not isinstance(ch.k, int) or 0 <= ch.n < CHUNKS

        def program(eng, chunk_step):
            for n in range(-1, 2):
                chunk_step(Tile(0, n))
            with eng.Fori(0, (CHUNKS - 4) // 2) as k:
                chunk_step(Tile(k, 2))
                chunk_step(Tile(k, 3))
            for n in range(CHUNKS - 2, CHUNKS + 1):
                chunk_step(Tile(0, n))

        class Row:
            def __init__(self, ch, t):
                self.ch, self.t = ch.plus(t // TPC), t % TPC
                self.live = live(self.ch)
                self.n = TPC * self.ch.n + self.t
                self.slot = self.t % 2
                self.turn = 2 * self.ch.n + self.t // 2

        def due(t, half, first, count, each):
            at = (2 * t + half - first) * each
            return range(at, at + each) if 0 <= at < count else ()

        TRANSPOSE, QK, QF = (1, TPC, 1), (5, 4, 2), (0, PAIRS, 2)

        with nc.Block() as block:
            @block.sync
            def _(sp):
                for dst, name in ((raw, "la_w"), (w_out, "la_w_out"), (ident, "ident"), (cols, "la_cols"),
                                  (mask, "la_mask"), (bv, "la_bv"), (bo, "la_bo")):
                    sp.dma_start(dst[:], c[name]).then_inc(const_in, 16)

                def load(ch):
                    for k, src in enumerate((x_in, ctx)):
                        sp.dma_start(rows[:, ch.slot, k, :, :],
                                     src[bass.ds(ch.n * TPC, TPC)].rearrange("t p d -> p t d")).then_inc(in_s[ch.slot], 16)
                load(Tile(0, 0))
                load(Tile(0, 1))

                def chunk_step(ch):
                    after = ch.plus(2)
                    if live(after) and after.c >= 2:
                        hold(sp, t_ready, TPC * (ch.n + 1), held)
                        load(after)
                    for t in range(TPC):
                        r = Row(ch, t - 4)
                        if r.live:
                            sp.dma_start(xr[:, r.slot, :], x_in[r.n]).then_inc(xr_s[r.slot], 16)
                            hold(sp, xo_ready, r.n + 1, held)
                            sp.dma_start(x_out[r.n], xo[:, r.slot, :]).then_inc(stored[r.slot], 16)
                program(sp, chunk_step)
                for s in range(2):
                    sp.wait_ge(stored[s], 16 * TILES // 2)

            @block.gpsimd
            def _(pool):
                pool.memset(half_neg[:], -0.5).then_inc(zeroed, 1)
                pool.memset(vb[:], 0.0).then_inc(zeroed, 1)
                pool.memset(kv[:], 0.0).then_inc(zeroed, 1)
                pool.wait_ge(zeroed, 3)
                for b in range(2):
                    pool.memset(vb[64 * b:64 * b + 64, :, :, b, :, HC:E], 1.0).then_inc(zeroed, 1)

                def chunk_step(ch):
                    new = ch.plus(1)
                    if live(new):
                        pool.wait_ge(var_ready, new.n + 1)
                        pool.tensor_tensor(rstd[:], var_eps[:], half_neg[:], ALU.pow).then_inc(rstd_ready, 1)
                program(pool, chunk_step)

            @block.scalar
            def _(act):
                act.wait_ge(const_in, 16 * 7)
                act.activation(w_hi[:], raw[:], ACT.Copy).then_inc(whi_ready, 1)
                act.activation(gate[:], cols[:, 4:5], ACT.Tanh).then_inc(gate_ready, 1)

                def chunk_step(ch):
                    new = ch.plus(1)
                    for t in range(TPC):
                        r = Row(ch, t - 1)
                        for half in range(2):
                            if r.live:
                                n = 2 * r.n + half
                                act.wait_ge(kv_mm, n + 1)
                                past(act, q_mm, n - 3)
                                act.activation(kv[0:F, r.slot, HALF * half:HALF * half + HALF, :, 0, :],
                                               p_kv[0:F, 0:HALF * 4 * E].rearrange("p (a b h e) -> p a b h e", a=HALF, b=2, h=2)[:, :, :, 0, :],
                                               ACT.Copy).then_inc(kv_low, 1)
                            for m in due(t, half, *TRANSPOSE) if live(new) else ():
                                act.wait_ge(t_ready, TPC * new.n + m + 1)
                                act.activation(t_hi[:, new.slot, :, :, m * PART:(m + 1) * PART],
                                               p_t[:].rearrange("p (x k t) -> p x k t", x=2, k=KC), ACT.Copy
                                               ).then_inc(thi_ready, 1)
                            for m in due(t, half, *QK) if live(new) else ():
                                act.wait_ge(qk_mm, 4 * new.n + m + 1)
                                act.activation(qk_hi[:, new.slot, m, :], p_p[m % 2][:], ACT.Identity,
                                               bias=cols[:, m:m + 1]).then_inc(qkhi_ready, 1)
                            for m in due(t, half, *QF) if live(ch) else ():
                                act.wait_ge(qf_mm, PAIRS * ch.n + m + 1)
                                act.activation(qf[:, ch.slot, m, :], p_p[m % 2][:], ACT.Relu).then_inc(qf_ready, 1)
                        r = Row(ch, t - 3)
                        if r.live:
                            act.wait_ge(ot_mm, r.n + 1)
                            past(act, y_mm, r.n - 1)
                            act.activation(o_t[:, r.slot, :], p_y[:, 0:DIM], ACT.Copy).then_inc(ot_ready, 1)
                program(act, chunk_step)

            @block.vector
            def _(dve):
                dve.wait_ge(const_in, 16 * 7)
                dve.wait_ge(whi_ready, 1)
                dve.tensor_tensor(w_lo[:], raw[:], w_hi[:].bitcast(fp32), ALU.subtract).then_inc(wlo_ready, 1)
                dve.wait_ge(gate_ready, 1)
                dve.wait_ge(zeroed, 5)

                def statistics(ch):
                    dve.wait_ge(in_s[ch.slot], 32 * (ch.turn + 1))
                    for t in range(TPC):
                        dve.bn_stats(stats[:, t, :], rows[:, ch.slot, 0, t, :]).then_inc(stat, 1)
                    hold(dve, stat, 2 * TPC * ch.n + TPC, held)
                    for t in range(TPC):
                        dve.bn_aggr(mv[:, t, :], stats[:, t, :]).then_inc(stat, 1)
                    dve.wait_ge(stat, 2 * TPC * (ch.n + 1))
                    dve.tensor_scalar_add(var_eps[:], mv[:, :, 1], EPS).then_inc(var_ready, 1)

                def normalise(ch):
                    dve.wait_ge(rstd_ready, ch.n + 1)
                    past(dve, t_ready, TPC * ch.n)
                    for t in range(TPC):
                        dve.tensor_scalar(hn[:, t, :], rows[:, ch.slot, 0, t, :], mv[:, t, 0:1], rstd[:, t:t + 1],
                                          ALU.subtract, ALU.mult).then_inc(hn_ready, 1)

                def chunk_step(ch):
                    new = ch.plus(1)
                    for t in range(TPC):
                        now, r1, r2, r4 = Row(ch, t), Row(ch, t - 1), Row(ch, t - 2), Row(ch, t - 4)
                        for half in range(2):
                            if now.live:
                                dve.wait_ge(kf_mm, 2 * now.n + half + 1)
                                past(dve, kv_mm, 2 * (now.n - 1))
                                dve.tensor_scalar(kf[:, now.slot, half * CHUNK:(half + 1) * CHUNK], p_k[:], 0.0,
                                                  mask[:, bass.ds(now.n, 1)], ALU.max, ALU.mult).then_inc(kf_ready, 1)
                            if r1.live:
                                n = 2 * r1.n + half
                                dve.wait_ge(kv_mm, n + 1)
                                past(dve, q_mm, n - 3)
                                dve.tensor_copy(kv[F:PART, r1.slot, HALF * half:HALF * half + HALF, :, 1, :],
                                                p_kv[F:PART, 0:HALF * 4 * E].rearrange("p (a b h e) -> p a b h e", a=HALF, b=2, h=2)[:, :, :, 1, :]
                                                ).then_inc(kv_high, 1)
                            if now.live and half == 0:
                                dve.wait_ge(v_mm, now.n + 1)
                                for b in range(2):
                                    p = slice(64 * b, 64 * b + 64)
                                    dve.tensor_tensor(vb[p, now.slot, :, b, :, 0:HC],
                                                      p_v[p, 0:DIM].rearrange("p (a h e) -> p a h e", a=PAIRS, h=2),
                                                      bv[p].rearrange("p (a h e) -> p a h e", a=PAIRS, h=2), ALU.add
                                                      ).then_inc(v_ready, 1)
                            if t == 0 and live(new):
                                (statistics, normalise)[half](new)
                            for m in due(t, half, *TRANSPOSE) if live(new) else ():
                                dve.wait_ge(thi_ready, TPC * new.n + m + 1)
                                at = slice(m * PART, (m + 1) * PART)
                                dve.tensor_tensor(t_lo[:, new.slot, :, :, at],
                                                  p_t[:].rearrange("p (x k t) -> p x k t", x=2, k=KC),
                                                  t_hi[:, new.slot, :, :, at].bitcast(fp32), ALU.subtract
                                                  ).then_inc(tlo_ready, 1)
                            for m in due(t, half, *QK) if live(new) else ():
                                dve.wait_ge(qkhi_ready, 4 * new.n + m + 1)
                                dve.scalar_tensor_tensor(out=qk_lo[:, new.slot, m, :], in0=p_p[m % 2][:],
                                                         scalar=cols[:, m:m + 1],
                                                         in1=qk_hi[:, new.slot, m, :].bitcast(fp32),
                                                         op0=ALU.add, op1=ALU.subtract).then_inc(qklo_ready, 1)
                            if r4.live and half == 1:
                                dve.wait_ge(y_mm, r4.n + 1)
                                past(dve, stored[r4.slot], 16 * r4.turn)
                                past(dve, xo_ready, r4.n)
                                dve.tensor_tensor(y[:], p_y[:, DIM:2 * DIM], bo[:], ALU.add).then_inc(y_ready, 1)
                                dve.wait_ge(y_ready, r4.n + 1)
                                dve.wait_ge(xr_s[r4.slot], 16 * (r4.turn + 1))
                                dve.scalar_tensor_tensor(out=xo[:, r4.slot, :], in0=y[:], scalar=gate[:],
                                                         in1=xr[:, r4.slot, :], op0=ALU.mult, op1=ALU.add).then_inc(xo_ready, 1)
                            if r2.live:
                                n = 2 * r2.n + half
                                dve.wait_ge(q_mm, n + 1)
                                if half == 0:
                                    past(dve, ot_mm, r2.n - 1)
                                batches = [(slice(64 * b, 64 * b + 64), p_q[64 * b:64 * b + 64, 0:HALF * 4 * E].rearrange(
                                    "p (a b h e) -> p a b h e", a=HALF, b=2, h=2)[:, :, b, :, :]) for b in range(2)]
                                for p, src in batches:
                                    dve.tensor_scalar_add(den[p, :, :], src[:, :, :, HC], 1e-8).then_inc(den_ready, 1)
                                dve.wait_ge(den_ready, 3 * n + 2)
                                dve.reciprocal(rden[:], den[:]).then_inc(den_ready, 1)
                                dve.wait_ge(den_ready, 3 * n + 3)
                                for p, src in batches:
                                    dve.tensor_tensor(on[p, r2.slot, half * PART:(half + 1) * PART].rearrange("p (a h e) -> p a h e", a=HALF, h=2),
                                                      src[:, :, :, 0:HC],
                                                      rden[p, :, :].unsqueeze(3).to_broadcast([64, HALF, 2, HC]),
                                                      ALU.mult).then_inc(on_ready, 1)
                program(dve, chunk_step)

            @block.tensor
            def _(pe):
                pe.wait_ge(const_in, 16 * 7)
                pe.wait_ge(wlo_ready, 1)
                pe.wait_ge(zeroed, 5)

                def products(out, pairs):
                    todo = [xy for lh, ll, rh, rl in pairs for xy in ((lh, rh), (lh, rl), (ll, rh))]
                    for n, (x, y) in enumerate(todo):
                        mm = pe.matmul(out, x, y, start=(n == 0), stop=(n == len(todo) - 1))
                    return mm

                def output(r):
                    pe.wait_ge(ot_ready, r.n + 1)
                    past(pe, y_ready, r.n)
                    for k in range(KC):
                        mm = pe.matmul(p_y[:, DIM:2 * DIM], o_t[:, r.slot, k * PART:(k + 1) * PART],
                                       w_out[:, k, :], start=(k == 0), stop=(k == KC - 1))
                    mm.then_inc(y_mm, 1)

                def chunk_step(ch):
                    new = ch.plus(1)
                    for t in range(TPC):
                        now, r1, r2, r3, r4 = (Row(ch, t - d) for d in range(5))
                        for half in range(2):
                            if now.live:
                                past(pe, kf_ready, 2 * now.n + half)
                                if t == 0 and half == 0:
                                    pe.wait_ge(qklo_ready, 4 * (ch.n + 1))
                                tok = slice(t * PART, (t + 1) * PART)
                                products(p_k[:], [(qk_hi[:, ch.slot, 2 + half, tok], qk_lo[:, ch.slot, 2 + half, tok],
                                                   w_hi[:, WFK:WFK + CHUNK], w_lo[:, WFK:WFK + CHUNK])]
                                         ).then_inc(kf_mm, 1)
                            if r1.live:
                                if half == 0:
                                    pe.wait_ge(v_ready, 2 * (r1.n + 1))
                                pe.wait_ge(kf_ready, 2 * r1.n + half + 1)
                                past(pe, kv_low, 2 * r1.n + half)
                                past(pe, kv_high, 2 * r1.n + half)
                                for a in range(HALF):
                                    pair = HALF * half + a
                                    mm = pe.matmul(p_kv[:, a * 4 * E:(a + 1) * 4 * E],
                                                   kf[:, r1.slot, pair * PART:(pair + 1) * PART],
                                                   vb[:, r1.slot, pair, :, :, :].rearrange("p b h e -> p (b h e)"),
                                                   start=True, stop=True)
                                mm.then_inc(kv_mm, 1)
                            if now.live and half == 0:
                                past(pe, v_ready, 2 * now.n)
                                tok = slice(t * PART, (t + 1) * PART)
                                products(p_v[:, 0:DIM], [(t_hi[:, ch.slot, 1, k, tok], t_lo[:, ch.slot, 1, k, tok],
                                                          w_hi[:, WV + k * DIM:WV + (k + 1) * DIM],
                                                          w_lo[:, WV + k * DIM:WV + (k + 1) * DIM])
                                                         for k in range(KC)]).then_inc(v_mm, 1)
                            for m in due(t, half, *TRANSPOSE) if live(new) else ():
                                pe.wait_ge(hn_ready, TPC * new.n + m + 1)
                                if m == 0:
                                    pe.wait_ge(in_s[new.slot], 32 * (new.turn + 1))
                                past(pe, tlo_ready, TPC * new.n + m)
                                for k in range(KC):
                                    at = slice(k * PART, (k + 1) * PART)
                                    pe.transpose(p_t[:, k * PART:(k + 1) * PART], hn[:, m, at], ident[:])
                                    mm = pe.transpose(p_t[:, DIM + k * PART:DIM + (k + 1) * PART],
                                                      rows[:, new.slot, 1, m, at], ident[:])
                                mm.then_inc(t_ready, 1)
                            for m in due(t, half, *QF) if live(ch) else ():
                                if m >= 2:
                                    pe.wait_ge(qf_ready, PAIRS * ch.n + m - 1)
                                at = WFQ + (m % HALF) * PART
                                products(p_p[m % 2][:], [(w_hi[:, at:at + PART], w_lo[:, at:at + PART],
                                                          qk_hi[:, ch.slot, m // HALF, :],
                                                          qk_lo[:, ch.slot, m // HALF, :])]).then_inc(qf_mm, 1)
                            for m in due(t, half, *QK) if live(new) else ():
                                if m == 0:
                                    pe.wait_ge(tlo_ready, TPC * (new.n + 1))
                                if m < 2:
                                    past(pe, qf_ready, PAIRS * new.n)
                                else:
                                    pe.wait_ge(qklo_ready, 4 * new.n + m - 1)
                                at = (WQ, WK)[m // 2] + (m % 2) * PART
                                products(p_p[m % 2][:], [(w_hi[:, at + k * DIM:at + k * DIM + PART],
                                                          w_lo[:, at + k * DIM:at + k * DIM + PART],
                                                          t_hi[:, new.slot, m // 2, k, :],
                                                          t_lo[:, new.slot, m // 2, k, :]) for k in range(KC)]
                                         ).then_inc(qk_mm, 1)
                            if half == 0 and r4.live:
                                output(r4)
                            if r2.live:
                                if half == 0 and r2.t == 0:
                                    pe.wait_ge(qf_ready, PAIRS * (r2.ch.n + 1))
                                pe.wait_ge(kv_low, 2 * r2.n + half + 1)
                                pe.wait_ge(kv_high, 2 * r2.n + half + 1)
                                past(pe, on_ready, 2 * (2 * r2.n + half))
                                for a in range(HALF):
                                    pair = HALF * half + a
                                    mm = pe.matmul(p_q[:, a * 4 * E:(a + 1) * 4 * E],
                                                   qf[:, r2.ch.slot, pair, r2.t * PART:(r2.t + 1) * PART],
                                                   kv[:, r2.slot, pair, :, :, :].rearrange("p b h e -> p (b h e)"),
                                                   start=True, stop=True)
                                mm.then_inc(q_mm, 1)
                        if r3.live:
                            pe.wait_ge(on_ready, 4 * (r3.n + 1))
                            past(pe, ot_ready, r3.n)
                            past(pe, y_ready, r3.n)
                            for k in range(KC):
                                mm = pe.transpose(p_y[:, k * PART:(k + 1) * PART],
                                                  on[:, r3.slot, k * PART:(k + 1) * PART], ident[:])
                            mm.then_inc(ot_mm, 1)
                program(pe, chunk_step)


def _layout_linear_attention(a):
    f = np.float32
    wq, wk, wv, wo = (np.asarray(a[f"L1_xattn_W{n}"]) for n in "qkvo")
    bq, bk, bv, bo = (np.asarray(a[f"L1_xattn_b{n}"]) for n in "qkvo")
    block = lambda w: w.reshape(2, PART, -1).transpose(1, 0, 2).reshape(PART, -1)
    feats = []
    for n in ("L1_xattn_Wqf", "L1_xattn_Wkf"):
        m = np.zeros((PART, 512), f)
        for h in range(8):
            m[16 * h:16 * h + 16, 64 * h:64 * h + 64] = np.asarray(a[n]).T
        feats.append(m)
    cols = np.zeros((PART, 8), f)
    for n, b in enumerate((bq[:128], bq[128:], bk[:128], bk[128:])):
        cols[:, n] = b
    cols[:, 4] = np.asarray(a["g_xattn"])[1]
    mask = np.ascontiguousarray(np.asarray(a["mask_BxS2_ff1"]).reshape(TILES, PART).T)
    return {"la_w": np.ascontiguousarray(np.concatenate([block(wq.T), block(wk.T), block(wv.T)] + feats, 1)),
            "la_w_out": np.ascontiguousarray(wo.T.reshape(2, PART, DIM).transpose(1, 0, 2)),
            "la_cols": cols, "la_mask": mask, "la_bv": np.tile(bv, (PART, 1)), "la_bo": np.tile(bo, (PART, 1)),
            "ident": np.eye(PART, dtype=f)}


QHEADS, KVHEADS, HD, RQ = 32, 8, 64, 4


def stage_causal_attention(nc, x_in, z_out, c):
    KC, PAIRS, GROUPS, TPC = 2, 4, 8, CHUNK // PART
    PIECE = 1024
    WQ, WK, WV, WO, WEND = 0, 4096, 5120, 6144, 10240
    PIECES = WEND // PIECE
    st = ExitStack()
    sb = lambda n, s, d=fp32: st.enter_context(nc.sbuf_tensor(f"ca_{n}", s, d))
    sem = lambda n: nc.alloc_semaphore(f"ca_{n}")
    with st:
        w_hi, w_lo = (sb(n, [PART, WEND], fp32r) for n in ("w_hi", "w_lo"))
        ident = sb("ident", [PART, PART])
        mask = sb("mask", [PART, PART])
        cos_q, sin_q, cos_k, sin_k = (sb(n, [PART, SEQ]) for n in ("cos_q", "sin_q", "cos_k", "sin_k"))
        norm_w, half_neg = sb("norm_w", [PART, DIM]), sb("half_neg", [PART, TPC])
        xt, z = sb("xt", [PART, TPC, DIM]), sb("z", [PART, 2, TPC, DIM])
        stats, mv = sb("stats", [PART, TPC, 6]), sb("mv", [PART, TPC, 2])
        var_eps, rstd = sb("var_eps", [PART, TPC]), sb("rstd", [PART, TPC])
        hn = sb("hn", [PART, TPC, DIM])
        ht_hi, ht_lo = (sb(n, [PART, 2, KC, CHUNK], fp32r) for n in ("ht_hi", "ht_lo"))
        q_f, q_swap = sb("q_f", [PART, 2, CHUNK]), sb("q_swap", [PART, 2, CHUNK])
        qk = sb("qk", [PART, 2, RQ + 1, CHUNK])
        qk_flat = qk[:].rearrange("p s m t -> p (s m t)")
        RAWS = 2 * (RQ + 1) * CHUNK // PIECE
        raw = [qk_flat[:, n * PIECE:(n + 1) * PIECE] for n in range(RAWS)]
        v = sb("v", [PART, 2, TPC, KVHEADS * HD])
        sm, neg_top = sb("sm", [PART, 2, CHUNK]), sb("neg_top", [PART, 2, RQ])
        prob, sums, rsum = sb("prob", [PART, 2, CHUNK]), sb("sums", [PART, 2, RQ]), sb("rsum", [PART, 2, RQ])
        pn, pt = sb("pn", [PART, 2, CHUNK]), sb("pt", [PART, 2, CHUNK])
        ot_hi, ot_lo = (sb(n, [PART, 2, RQ, CHUNK], fp32r) for n in ("ot_hi", "ot_lo"))
        y_t = hn[:].rearrange("p (k t) d -> p k (t d)", k=KC)
        bank = lambda n: st.enter_context(nc.psum_tensor(f"ca_{n}", [PART, CHUNK], fp32))
        p_p, p_r, p_t, p_o = bank("pp"), bank("pr"), bank("p_t"), bank("po")
        p_s, p_y = [bank(f"ps{i}") for i in range(2)], [bank(f"py{i}") for i in range(2)]

        const_in, zeroed = sem("const_in"), sem("zeroed")
        raw_in = [sem(f"raw{i}") for i in range(RAWS)]
        whi_ready, wlo_ready = sem("whi"), sem("wlo")
        x_loaded, square = sem("x"), sem("square")
        stat, var_ready, rstd_ready, z_ready, hn_ready = sem("stat"), sem("var"), sem("rstd"), sem("z"), sem("hn")
        t_ready, hthi_ready, htlo_ready = sem("t"), sem("hthi"), sem("htlo")
        pp_ready, qf_ready, cos_done, sin_done = sem("pp"), sem("qf"), sem("cos"), sem("sin")
        swapped = [sem(f"swap{i}") for i in range(2)]
        qk_ready, v_mm, v_ready = sem("qk"), sem("v_mm"), sem("v")
        s_ready, sm_ready, top_ready, prob_ready = sem("s"), sem("sm"), sem("top"), sem("prob")
        rsum_ready, pn_ready, pt_mm, pt_even, pt_odd = sem("rsum"), sem("pn"), sem("pt_mm"), sem("pt_e"), sem("pt_o")
        pv_ready, othi_ready, otlo_ready = sem("pv"), sem("othi"), sem("otlo")
        y_ready, yt_ready, back_ready, zn_ready = sem("y"), sem("yt"), sem("back"), sem("zn")
        held = sem("held")
        stored = [sem(f"stored{i}") for i in range(2)]

        def live(ch):
            return not isinstance(ch.k, int) or 0 <= ch.n < CHUNKS

        def program(eng, chunk_step):
            chunk_step(Tile(0, -1))
            chunk_step(Tile(0, 0))
            with eng.Fori(0, (CHUNKS - 2) // 2) as k:
                chunk_step(Tile(k, 1))
                chunk_step(Tile(k, 2))
            chunk_step(Tile(0, CHUNKS - 1))
            chunk_step(Tile(0, CHUNKS))

        class Unit:
            def __init__(self, ch, kp):
                self.ch, self.kp = ch.plus(kp // PAIRS), kp % PAIRS
                self.live = live(self.ch)
                self.n = PAIRS * self.ch.n + self.kp
                self.slot = self.kp % 2

        def swap_turn(u, m):
            return PAIRS * (RQ + 1) // 2 * u.ch.n + ((RQ + 1) * u.kp + m) // 2

        def group(ch, kp, g):
            u = Unit(ch, kp + g // GROUPS)
            return u, g % GROUPS, GROUPS * u.n + g % GROUPS

        with nc.Block() as block:
            @block.sync
            def _(sp):
                for dst, name in ((ident, "ident"), (mask, "ca_mask"), (cos_q, "ca_cos_q"),
                                  (sin_q, "ca_sin_q"), (cos_k, "ca_cos_k"), (sin_k, "ca_sin_k"),
                                  (norm_w, "ca_norm_w")):
                    sp.dma_start(dst[:], c[name]).then_inc(const_in, 16)

                def load_x(ch):
                    sp.dma_start(xt[:], x_in[bass.ds(ch.n * TPC, TPC)].rearrange("t p d -> p t d")
                                 ).then_inc(x_loaded, 16)
                for n in range(PIECES):
                    if n >= RAWS:
                        sp.wait_ge(whi_ready, n - RAWS + 1)
                        sp.wait_ge(wlo_ready, n - RAWS + 1)
                    sp.dma_start(raw[n % RAWS], c["ca_w"][:, n * PIECE:(n + 1) * PIECE]).then_inc(raw_in[n % RAWS], 16)
                load_x(Tile(0, 0))

                def chunk_step(ch):
                    old, new = ch.plus(-1), ch.plus(1)
                    if live(ch) and live(new):
                        hold(sp, z_ready, TPC * (ch.n + 1), held)
                        load_x(new)
                    for kp in range(PAIRS):
                        nxt = Unit(ch, kp + 1)
                        for g in range(GROUPS):
                            if nxt.live and g <= RQ:
                                n = (RQ + 1) * nxt.n + g
                                s = (nxt.kp + g) % 2
                                hold(sp, qf_ready, n + 1, held)
                                hold(sp, qk_ready, n - 1, held)
                                for p in range(0, PART, 32):
                                    sp.dma_start(q_swap[p:p + 32, s, :], q_f[p ^ 32:(p ^ 32) + 32, s, :]
                                                 ).then_inc(swapped[s], 16)
                            if (kp, g) in ((0, 7), (1, 6)) and live(old):
                                h = kp
                                hold(sp, zn_ready, 2 * old.n + h + 1, held)
                                sp.dma_start(z_out[bass.ds(old.n * TPC + 2 * h, 2)].rearrange("t p d -> p t d"),
                                             z[:, old.slot, 2 * h:2 * h + 2, :]).then_inc(stored[h], 16)
                program(sp, chunk_step)
                for h in range(2):
                    sp.wait_ge(stored[h], 16 * CHUNKS)

            @block.gpsimd
            def _(pool):
                pool.memset(half_neg[:], -0.5).then_inc(zeroed, 1)
                pool.wait_ge(zeroed, 1)

                def chunk_step(ch):
                    for kp in range(PAIRS):
                        nxt = Unit(ch, kp + 1)
                        for g in range(GROUPS):
                            if kp == 2 and g in (0, 2) and live(ch.plus(1)):
                                pool.wait_ge(var_ready, 2 * ch.plus(1).n + g // 2 + 1)
                                pool.tensor_tensor(rstd[:], var_eps[:], half_neg[:], ALU.pow).then_inc(rstd_ready, 1)
                            if nxt.live and 2 <= g <= RQ + 2:
                                m = g - 2
                                n = (RQ + 1) * nxt.n + m
                                s = (nxt.kp + m) % 2
                                pool.wait_ge(cos_done, n + 1)
                                pool.wait_ge(sin_done, n + 1)
                                pool.tensor_tensor(qk[:, nxt.slot, m, :], qk[:, nxt.slot, m, :], q_swap[:, s, :], ALU.add
                                                   ).then_inc(qk_ready, 1)
                            u, gg, n = group(ch, kp, g - 1)
                            if u.live:
                                pool.wait_ge(rsum_ready, n + 1)
                                past(pool, pt_mm, n - 1)
                                pool.tensor_tensor(pn[:, gg % 2, :].rearrange("p (r k) -> p r k", r=RQ),
                                                   prob[:, gg % 2, :].rearrange("p (r k) -> p r k", r=RQ),
                                                   rsum[:, gg % 2, :].unsqueeze(2).to_broadcast([PART, RQ, PART]),
                                                   ALU.mult).then_inc(pn_ready, 1)
                program(pool, chunk_step)

            @block.scalar
            def _(act):
                for n in range(PIECES):
                    act.wait_ge(raw_in[n % RAWS], 16 * (n // RAWS + 1))
                    act.activation(w_hi[:, n * PIECE:(n + 1) * PIECE], raw[n % RAWS], ACT.Copy).then_inc(whi_ready, 1)

                def chunk_step(ch):
                    for kp in range(PAIRS):
                        nxt = Unit(ch, kp + 1)
                        for g in range(GROUPS):
                            if nxt.live and g <= RQ:
                                n = (RQ + 1) * nxt.n + g
                                act.wait_ge(pp_ready, n + 1)
                                past(act, swapped[(nxt.kp + g) % 2], 64 * swap_turn(nxt, g))
                                past(act, cos_done, n - 1)
                                act.activation(q_f[:, (nxt.kp + g) % 2, :], p_p[:], ACT.Copy).then_inc(qf_ready, 1)
                            if kp == 3 and g >= 4 and live(ch.plus(1)):
                                n = TPC * ch.plus(1).n + g - 4
                                act.wait_ge(v_mm, n + 1)
                                act.activation(v[:, ch.plus(1).slot, g - 4, :], p_p[:], ACT.Copy).then_inc(v_ready, 1)
                            if kp == 2 and g >= 6 and live(ch.plus(1)):
                                h = g - 6
                                act.wait_ge(t_ready, 2 * ch.plus(1).n + h + 1)
                                act.activation(ht_hi[:, ch.plus(1).slot, :, 2 * h * PART:(2 * h + 2) * PART],
                                               p_r[:].rearrange("p (k t) -> p k t", k=KC), ACT.Copy
                                               ).then_inc(hthi_ready, 1)
                            u, gg, n = group(ch, kp, g - 3)
                            if u.live and gg % 2 == 0:
                                act.wait_ge(pt_mm, n + 1)
                                past(act, pv_ready, n - 1)
                                act.activation(pt[:, 0, :], p_t[:], ACT.Copy).then_inc(pt_even, 1)
                            u, gg, n = group(ch, kp, g - 4)
                            if u.live and gg % 2 == 1:
                                t = gg // 2
                                act.wait_ge(pv_ready, n + 1)
                                if t == 0:
                                    past(act, y_ready, u.n - 1)
                                act.activation(ot_hi[:, u.slot, :, t * PART:(t + 1) * PART],
                                               p_o[:].rearrange("p (r t) -> p r t", r=RQ), ACT.Copy
                                               ).then_inc(othi_ready, 1)
                            if kp == 0 and g == 6 and live(ch.plus(-1)):
                                act.wait_ge(y_ready, PAIRS * ch.n)
                                for k in range(KC):
                                    act.activation(y_t[:, k, :], p_y[k][:], ACT.Copy).then_inc(yt_ready, 1)
                            u, gg, n = group(ch, kp, g)
                            if u.live:
                                s = gg % 2
                                act.wait_ge(top_ready, n + 1)
                                past(act, pn_ready, n - 1)
                                past(act, rsum_ready, n - 1)
                                for r in range(RQ):
                                    act.activation(prob[:, s, r * PART:(r + 1) * PART], sm[:, s, r * PART:(r + 1) * PART],
                                                   ACT.Exp, bias=neg_top[:, s, r:r + 1],
                                                   accum_out=sums[:, s, r:r + 1]).then_inc(prob_ready, 1)
                program(act, chunk_step)

            @block.vector
            def _(dve):
                dve.wait_ge(const_in, 16 * 7)
                for n in range(PIECES):
                    dve.wait_ge(whi_ready, n + 1)
                    at = slice(n * PIECE, (n + 1) * PIECE)
                    dve.tensor_tensor(w_lo[:, at], raw[n % RAWS], w_hi[:, at].bitcast(fp32), ALU.subtract
                                      ).then_inc(wlo_ready, 1)

                def statistics(ch, norm):
                    at = 4 * TPC * ch.n + 2 * TPC * (norm - 1)
                    if norm == 1:
                        dve.wait_ge(x_loaded, 16 * (ch.n + 1))
                    else:
                        dve.wait_ge(z_ready, TPC * (ch.n + 1))
                    for t in range(TPC):
                        src = xt[:, t, :] if norm == 1 else z[:, ch.slot, t, :]
                        dve.bn_stats(stats[:, t, :], src).then_inc(stat, 1)
                    hold(dve, stat, at + TPC, held)
                    for t in range(TPC):
                        dve.bn_aggr(mv[:, t, :], stats[:, t, :]).then_inc(stat, 1)
                    dve.wait_ge(stat, at + 2 * TPC)
                    var = mv[:, :, 1]
                    if norm == 2:
                        dve.tensor_tensor(var_eps[:], mv[:, :, 0], mv[:, :, 0], ALU.mult).then_inc(square, 1)
                        dve.wait_ge(square, 2 * ch.n + 1)
                        dve.tensor_tensor(var_eps[:], var_eps[:], var, ALU.add).then_inc(square, 1)
                        dve.wait_ge(square, 2 * ch.n + 2)
                        var = var_eps[:]
                    dve.tensor_scalar_add(var_eps[:], var, EPS).then_inc(var_ready, 1)

                def normalise(ch, norm):
                    dve.wait_ge(rstd_ready, 2 * ch.n + norm)
                    for t in range(TPC):
                        rows = z[:, ch.slot, t, :]
                        if norm == 1:
                            if t % 2 == 0:
                                past(dve, stored[t // 2], 16 * (ch.n - 1))
                            dve.tensor_scalar(rows, xt[:, t, :], mv[:, t, 0:1], rstd[:, t:t + 1],
                                              ALU.subtract, ALU.mult).then_inc(z_ready, 1)
                        else:
                            dve.scalar_tensor_tensor(out=hn[:, t, :], in0=rows, scalar=rstd[:, t:t + 1],
                                                     in1=norm_w[:], op0=ALU.mult, op1=ALU.mult
                                                     ).then_inc(hn_ready, 1)

                def rope(u, m, swapped_halves):
                    s = (u.kp + m) % 2
                    src, tab, out, done = ((q_swap[:, s, :], (sin_q, sin_k), q_swap[:, s, :], sin_done)
                                           if swapped_halves else
                                           (q_f[:, s, :], (cos_q, cos_k), qk[:, u.slot, m, :], cos_done))
                    if m == 0 and not swapped_halves:
                        past(dve, s_ready, GROUPS * (u.n - 1))
                    dve.tensor_tensor(out.rearrange("p (b s) -> p b s", s=SEQ), src.rearrange("p (b s) -> p b s", s=SEQ),
                                      tab[int(m == RQ)][:].unsqueeze(1).to_broadcast([PART, CHUNK // SEQ, SEQ]),
                                      ALU.mult).then_inc(done, 1)

                def chunk_step(ch):
                    for kp in range(PAIRS):
                        nxt = Unit(ch, kp + 1)
                        for g in range(GROUPS):
                            if nxt.live and 2 <= g <= RQ + 2:
                                m = g - 2
                                dve.wait_ge(swapped[(nxt.kp + m) % 2], 64 * (swap_turn(nxt, m) + 1))
                                rope(nxt, m, True)
                            u, gg, n = group(ch, kp, g)
                            if u.live:
                                s = gg % 2
                                dve.wait_ge(s_ready, n + 1)
                                past(dve, prob_ready, RQ * (n - 1))
                                dve.tensor_tensor(sm[:, s, :].rearrange("p (r k) -> p r k", r=RQ),
                                                  p_s[s][:].rearrange("p (r k) -> p r k", r=RQ),
                                                  mask[:].unsqueeze(1).to_broadcast([PART, RQ, PART]), ALU.add
                                                  ).then_inc(sm_ready, 1)
                                dve.wait_ge(sm_ready, n + 1)
                                dve.tensor_reduce(neg_top[:, s, :], sm[:, s, :].rearrange("p (r k) -> p r k", r=RQ),
                                                  AX, ALU.max, negate=True).then_inc(top_ready, 1)
                            u, gg, n = group(ch, kp, g - 1)
                            if u.live:
                                s = gg % 2
                                dve.wait_ge(prob_ready, RQ * (n + 1))
                                past(dve, pn_ready, n - 1)
                                dve.reciprocal(rsum[:, s, :], sums[:, s, :]).then_inc(rsum_ready, 1)
                            if nxt.live and g <= RQ:
                                dve.wait_ge(qf_ready, (RQ + 1) * nxt.n + g + 1)
                                rope(nxt, g, False)
                            if kp == 2 and g < 4 and live(ch.plus(1)):
                                (statistics, normalise)[g % 2](ch.plus(1), g // 2 + 1)
                            if kp == 2 and g >= 6 and live(ch.plus(1)):
                                h = g - 6
                                dve.wait_ge(hthi_ready, 2 * ch.plus(1).n + h + 1)
                                at = slice(2 * h * PART, (2 * h + 2) * PART)
                                dve.tensor_tensor(ht_lo[:, ch.plus(1).slot, :, at],
                                                  p_r[:].rearrange("p (k t) -> p k t", k=KC),
                                                  ht_hi[:, ch.plus(1).slot, :, at].bitcast(fp32), ALU.subtract
                                                  ).then_inc(htlo_ready, 1)
                            u, gg, n = group(ch, kp, g - 3)
                            if u.live and gg % 2 == 1:
                                dve.wait_ge(pt_mm, n + 1)
                                past(dve, pv_ready, n - 1)
                                dve.tensor_copy(pt[:, 1, :], p_t[:]).then_inc(pt_odd, 1)
                            u, gg, n = group(ch, kp, g - 4)
                            if u.live and gg % 2 == 1:
                                t = gg // 2
                                dve.wait_ge(othi_ready, TPC * u.n + t + 1)
                                at = slice(t * PART, (t + 1) * PART)
                                dve.tensor_tensor(ot_lo[:, u.slot, :, at], p_o[:].rearrange("p (r t) -> p r t", r=RQ),
                                                  ot_hi[:, u.slot, :, at].bitcast(fp32), ALU.subtract
                                                  ).then_inc(otlo_ready, 1)
                            if (kp, g) in ((0, 7), (1, 6)) and live(ch.plus(-1)):
                                h, old = kp, ch.plus(-1)
                                dve.wait_ge(back_ready, 2 * old.n + h + 1)
                                dve.tensor_tensor(z[:, old.slot, 2 * h:2 * h + 2, :], p_r[:].rearrange("p (t d) -> p t d", t=2),
                                                  z[:, old.slot, 2 * h:2 * h + 2, :], ALU.add).then_inc(zn_ready, 1)
                program(dve, chunk_step)

            @block.tensor
            def _(pe):
                pe.wait_ge(const_in, 16 * 7)

                def products(out, pairs, start=True, stop=True):
                    todo = [xy for lh, ll, rh, rl in pairs for xy in ((lh, rh), (lh, rl), (ll, rh))]
                    for n, (x, y) in enumerate(todo):
                        mm = pe.matmul(out, x, y, start=start and n == 0, stop=stop and n == len(todo) - 1)
                    return mm

                def project(u, m):
                    n = (RQ + 1) * u.n + m
                    if n == 0 if isinstance(n, int) else False:
                        pe.wait_ge(wlo_ready, PIECES)
                    if m == 0 and u.kp == 0:
                        pe.wait_ge(htlo_ready, 2 * (u.ch.n + 1))
                    past(pe, qf_ready, n)
                    if m == 0 and u.kp == 1:
                        pe.wait_ge(v_ready, TPC * (u.ch.n + 1))
                    width = QHEADS * HD if m < RQ else KVHEADS * HD
                    at = WQ + (RQ * u.kp + m) * PART if m < RQ else WK + u.kp * PART
                    products(p_p[:], [(w_hi[:, at + k * width:at + k * width + PART],
                                       w_lo[:, at + k * width:at + k * width + PART],
                                       ht_hi[:, u.ch.slot, k, :], ht_lo[:, u.ch.slot, k, :])
                                      for k in range(KC)]).then_inc(pp_ready, 1)

                def chunk_step(ch):
                    new, old = ch.plus(1), ch.plus(-1)
                    for kp in range(PAIRS):
                        nxt = Unit(ch, kp + 1)
                        for g in range(GROUPS):
                            if nxt.live and g <= RQ:
                                project(nxt, g)
                            if kp == 3 and g >= 4 and live(new):
                                t = g - 4
                                if t == 0:
                                    pe.wait_ge(qf_ready, (RQ + 1) * (nxt.n + 1))
                                else:
                                    pe.wait_ge(v_ready, TPC * new.n + t)
                                tok = slice(t * PART, (t + 1) * PART)
                                products(p_p[:], [(ht_hi[:, new.slot, k, tok], ht_lo[:, new.slot, k, tok],
                                                   w_hi[:, WV + k * CHUNK:WV + (k + 1) * CHUNK],
                                                   w_lo[:, WV + k * CHUNK:WV + (k + 1) * CHUNK])
                                                  for k in range(KC)]).then_inc(v_mm, 1)
                            u, gg, n = group(ch, kp, g)
                            if u.live:
                                t, s = gg // 2, gg % 2
                                if gg == 0:
                                    pe.wait_ge(qk_ready, (RQ + 1) * (u.n + 1))
                                past(pe, sm_ready, n - 1)
                                half, tok = slice(HD * s, HD * s + HD), slice(t * PART, (t + 1) * PART)
                                for r in range(RQ):
                                    mm = pe.matmul(p_s[s][:, r * PART:(r + 1) * PART], qk[half, u.slot, r, tok],
                                                   qk[half, u.slot, RQ, tok], start=True, stop=True)
                                mm.then_inc(s_ready, 1)
                            if kp == 2 and g >= 6 and live(new):
                                h = g - 6
                                pe.wait_ge(hn_ready, TPC * (new.n + 1))
                                if live(old):
                                    pe.wait_ge(zn_ready, 2 * (old.n + 1))
                                if h == 1:
                                    pe.wait_ge(htlo_ready, 2 * new.n + 1)
                                for t in range(2):
                                    for k in range(KC):
                                        mm = pe.transpose(p_r[:, k * DIM + t * PART:k * DIM + (t + 1) * PART],
                                                          hn[:, 2 * h + t, k * PART:(k + 1) * PART], ident[:])
                                mm.then_inc(t_ready, 1)
                            u, gg, n = group(ch, kp, g - 3)
                            if u.live:
                                pe.wait_ge(pn_ready, n + 1)
                                if gg % 2 == 1:
                                    pe.wait_ge(pt_even, 4 * u.n + gg // 2 + 1)
                                else:
                                    past(pe, pt_odd, 4 * u.n + gg // 2)
                                for r in range(RQ):
                                    mm = pe.transpose(p_t[:, r * PART:(r + 1) * PART],
                                                      pn[:, gg % 2, r * PART:(r + 1) * PART], ident[:])
                                mm.then_inc(pt_mm, 1)
                            u, gg, n = group(ch, kp, g - 4)
                            if u.live:
                                t, s = gg // 2, gg % 2
                                pe.wait_ge(pt_odd if s else pt_even, 4 * u.n + t + 1)
                                if s == 0:
                                    past(pe, otlo_ready, TPC * u.n + t)
                                at = (2 * u.kp + s) * HD
                                pe.matmul(p_o[HD * s:HD * s + HD, :], v[:, u.ch.slot, t, at:at + HD], pt[:, s, :],
                                          start=True, stop=True, tile_position=(0, HD * s)).then_inc(pv_ready, 1)
                            u = Unit(ch, kp - 1)
                            if g == 5 and u.live:
                                pe.wait_ge(otlo_ready, TPC * (u.n + 1))
                                if u.kp == 0:
                                    past(pe, yt_ready, KC * u.ch.n)
                                for dh in range(KC):
                                    blocks = []
                                    for r in range(RQ):
                                        at = WO + (RQ * u.kp + r) * DIM + dh * PART
                                        blocks.append((w_hi[:, at:at + PART], w_lo[:, at:at + PART],
                                                       ot_hi[:, u.slot, r, :], ot_lo[:, u.slot, r, :]))
                                    mm = products(p_y[dh][:], blocks, start=(u.kp == 0), stop=(u.kp == PAIRS - 1))
                                mm.then_inc(y_ready, 1)
                            if (kp, g) in ((0, 7), (1, 6)) and live(old):
                                h = kp
                                pe.wait_ge(yt_ready, KC * (old.n + 1))
                                if live(ch):
                                    pe.wait_ge(htlo_ready, 2 * (ch.n + 1))
                                if h == 1:
                                    pe.wait_ge(zn_ready, 2 * old.n + 1)
                                for t in range(2):
                                    for dh in range(KC):
                                        mm = pe.transpose(p_r[:, t * DIM + dh * PART:t * DIM + (dh + 1) * PART],
                                                          y_t[:, dh, (2 * h + t) * PART:(2 * h + t + 1) * PART], ident[:])
                                mm.then_inc(back_ready, 1)
                program(pe, chunk_step)


def _layout_causal_attention(a):
    f = np.float32
    half = HD // 2
    inv = f(1.0) / f(150000.0) ** (np.arange(half, dtype=f) / f(half))
    ang = (np.arange(SEQ, dtype=f)[:, None] * inv).T
    cos = np.tile(np.cos(ang).astype(f), (4, 1))
    sin = np.tile(np.concatenate([-np.sin(ang), np.sin(ang)]).astype(f), (2, 1))
    scale = f(1 / np.sqrt(HD))
    mask = np.full((PART, PART), -1e30, f)
    for b in range(2):
        mask[64 * b:64 * b + 64, 64 * b:64 * b + 64] = np.where(np.tril(np.ones((64, 64), bool)), 0, -1e30)
    wq, wk, wv, wo = (np.asarray(a[f"L1_ffn_w{n}"]) for n in "qkvo")
    block = lambda w: w.reshape(2, PART, -1).transpose(1, 0, 2).reshape(PART, -1)
    wq = wq.reshape(DIM, 4, 2, RQ, HD).transpose(0, 1, 3, 2, 4).reshape(DIM, -1)
    wo = wo.reshape(4, 2, RQ, HD, DIM).transpose(0, 2, 1, 3, 4).reshape(16, PART, DIM).transpose(1, 0, 2)
    w = np.concatenate([block(wq), block(wk), block(wv), wo.reshape(PART, -1)], 1)
    return {"ca_w": np.ascontiguousarray(w), "ca_mask": mask, "ca_cos_q": cos * scale,
            "ca_sin_q": sin * scale, "ca_cos_k": cos, "ca_sin_k": sin,
            "ca_norm_w": np.tile(np.asarray(a["L1_ffn_ln_w"]), (PART, 1)), "ident": np.eye(PART, dtype=f)}


_WEIGHTS = ["L0_ffn_gate_proj", "L0_ffn_up_proj", "L0_ffn_down_proj", "L1_ffn_w1", "L1_ffn_w3", "L1_ffn_w2"]


def build(nc, a, out, scratch):
    with nc.cleanup_on_exit():
        stage_softmax_attention(nc, a["x"], scratch[0], a["ctx"], a)
    with nc.cleanup_on_exit():
        stage_experts(nc, "moe0", scratch[0], scratch[1], a["L0_ffn_gate_proj"], a["L0_ffn_up_proj"],
                      a["L0_ffn_down_proj"], a, 8, 128, 2, "layer")
    with nc.cleanup_on_exit():
        stage_linear_attention(nc, scratch[1], scratch[2], a["ctx"], a)
    with nc.cleanup_on_exit():
        stage_causal_attention(nc, scratch[2], scratch[3], a)
    with nc.cleanup_on_exit():
        stage_experts(nc, "moe1", scratch[3], out, a["L1_ffn_w1"], a["L1_ffn_w3"], a["L1_ffn_w2"],
                      a, 16, 256, 4, "rms", skip=scratch[2])


def kernel(**inputs):
    import concourse.bacc as _bacc
    from concourse.bass_utils import run_bass_kernel_spmd as _run

    nc = _bacc.Bacc("TRN2", target_bir_lowering=False, num_devices=1)
    tiles = (TILES, PART, DIM)
    host = {"x": np.asarray(inputs["x"]).reshape(tiles), "ctx": np.asarray(inputs["ctx_2048"]).reshape(tiles)}
    for n in _WEIGHTS:
        host[n] = np.asarray(inputs[n])
    host.update(_tables())
    for lay in (_layout_softmax_attention, _layout_experts, _layout_linear_attention, _layout_causal_attention):
        host.update(lay(inputs))
    arrays, a = {}, {}
    for n, v in host.items():
        arrays[f"in_{n}"] = np.ascontiguousarray(v)
        a[n] = nc.dram_tensor(f"in_{n}", v.shape, fp32, kind="ExternalInput").ap()
    out = nc.dram_tensor("out_0", tiles, fp32, kind="ExternalOutput").ap()
    scratch = [nc.dram_tensor(f"scratch_{i}", tiles, fp32, kind="Internal").ap() for i in range(4)]
    build(nc, a, out, scratch)
    r = _run(nc, [arrays], core_ids=[0])
    return r.results[0]["out_0"].reshape(BATCH, SEQ, DIM)
```
